# Optimizing a Trainium2 kernel written in Bass

```python
import numpy as np
import jax
import jax.numpy as jnp

def _softmax(x, axis=-1):
    return jax.nn.softmax(x, axis=axis)

def _gelu(x):
    return jax.nn.gelu(x, approximate=True)

def _silu(x):
    return jax.nn.silu(x)

def _sigmoid(x):
    return jax.nn.sigmoid(x)

def _layernorm(x, axis=-1, eps=1e-05):
    m = jnp.mean(x, axis=axis, keepdims=True)
    v = jnp.var(x, axis=axis, keepdims=True)
    return (x - m) / jnp.sqrt(v + eps)

def _scatter_add(tgt, idx, src, axis=0):
    return tgt.at[idx].add(src)

def _segment_sum(src, seg, n):
    return jax.ops.segment_sum(src, seg, n)
kernel_name = 'mk_recurrent_d2_jaxref_r8_a2907b'

def setup_inputs(seed: int=0):
    np.random.seed(seed)
    _w = jnp.asarray

    def _L0_attn_setup():
        import jax, jax.numpy as jnp
        import numpy as np
        HIDDEN = 128
        B, S = (8, 256)
        key = jax.random.key(seed)
        k_in, k_w, k_b = jax.random.split(key, 3)
        inputs = jax.random.normal(k_in, (B, S, HIDDEN), dtype=jnp.float32)
        Wq = jax.random.normal(k_w, (HIDDEN, HIDDEN), dtype=jnp.float32) / np.sqrt(HIDDEN)
        bq = jax.random.normal(k_b, (HIDDEN,), dtype=jnp.float32) * 0.01
        return {'inputs': inputs, 'Wq': Wq, 'bq': bq}
    _L0_attn_in = _L0_attn_setup()

    def _L0_ffn_setup():
        import jax, jax.numpy as jnp
        import numpy as np
        T, Z, D_DIM = (8, 256, 128)
        N_EXP, P_SLOT, H = (64, 32, 128)
        LN_EPS = 1e-05
        key = jax.random.key(seed)
        k = jax.random.split(key, 5)
        s = 0.02
        return {'x': jax.random.normal(k[0], (T, Z, D_DIM), dtype=jnp.float32), 'phi_w': jax.random.normal(k[1], (N_EXP * P_SLOT, D_DIM), dtype=jnp.float32) * s, 'phi_b': jax.random.normal(k[2], (N_EXP * P_SLOT,), dtype=jnp.float32) * s, 'expert_w': jax.random.normal(k[3], (N_EXP, D_DIM, H), dtype=jnp.float32) * s, 'expert_b': jax.random.normal(k[4], (N_EXP, H), dtype=jnp.float32) * s}
    _L0_ffn_in = _L0_ffn_setup()

    def _L1_attn_setup():
        import jax, jax.numpy as jnp
        import numpy as np
        B, S, D = (4, 512, 128)
        H = D
        C = 8.0

        def _rmsnorm(x, w, eps=1e-06):
            xf = x.astype(jnp.float32)
            norm = xf * jax.lax.rsqrt(jnp.mean(xf * xf, axis=-1, keepdims=True) + eps)
            return (norm * w).astype(x.dtype)
        key = jax.random.key(seed)
        ks = jax.random.split(key, 8)
        s = 1.0 / np.sqrt(D)
        x = jax.random.normal(ks[0], (B, S, D), dtype=jnp.float32)
        W_in = jax.random.normal(ks[1], (H, D), dtype=jnp.float32) * s
        W_ig = jax.random.normal(ks[2], (H, D), dtype=jnp.float32) * s
        b_ig = jnp.zeros((H,), dtype=jnp.float32)
        W_rg = jax.random.normal(ks[3], (H, D), dtype=jnp.float32) * s
        b_rg = jnp.zeros((H,), dtype=jnp.float32)
        lam = jax.random.uniform(ks[4], (H,), dtype=jnp.float32, minval=4.0, maxval=9.0)
        W_out = jax.random.normal(ks[5], (D, H), dtype=jnp.float32) * (1.0 / np.sqrt(H))
        h0 = jnp.zeros((1, 1, H), dtype=jnp.float32)
        norm_w = jnp.ones((H,), dtype=jnp.float32)
        return {'x': x, 'W_in': W_in, 'W_ig': W_ig, 'b_ig': b_ig, 'W_rg': W_rg, 'b_rg': b_rg, 'lam': lam, 'W_out': W_out, 'h0': h0, 'norm_w': norm_w}
    _L1_attn_in = _L1_attn_setup()

    def _L1_ffn_setup():
        import jax, jax.numpy as jnp
        import numpy as np
        DIM = 128

        def _reference_tuple_inner(x, W_r, W_k, W_v, mu_r, mu_k):
            B, T, C = x.shape
            x_prev = jnp.concatenate([jnp.zeros((B, 1, C), x.dtype), x[:, :-1, :]], axis=1)
            xr = mu_r * x + (1.0 - mu_r) * x_prev
            xk = mu_k * x + (1.0 - mu_k) * x_prev
            r = jax.nn.sigmoid(jnp.einsum('btc,dc->btd', xr, W_r))
            k = jnp.einsum('btc,dc->btd', xk, W_k)
            k_act = jnp.square(jax.nn.relu(k))
            out = r * jnp.einsum('btc,dc->btd', k_act, W_v)
            new_state = x[:, -1, :]
            return (out, new_state)
        key = jax.random.key(seed)
        ks = jax.random.split(key, 6)
        B, T, C = (8, 256, DIM)
        x = jax.random.normal(ks[0], (B, T, C), dtype=jnp.float32)
        s = 1.0 / np.sqrt(C)
        W_r = jax.random.uniform(ks[1], (C, C), jnp.float32, -s, s)
        W_k = jax.random.uniform(ks[2], (C, C), jnp.float32, -s, s)
        W_v = jax.random.uniform(ks[3], (C, C), jnp.float32, -s, s)
        mu_r = jax.random.uniform(ks[4], (C,), jnp.float32)
        mu_k = jax.random.uniform(ks[5], (C,), jnp.float32)
        return {'x': x, 'W_r': W_r, 'W_k': W_k, 'W_v': W_v, 'mu_r': mu_r, 'mu_k': mu_k}
    _L1_ffn_in = _L1_ffn_setup()
    _d = {'L0_attn_inputs': _L0_attn_in['inputs'], 'L0_attn_Wq': _L0_attn_in['Wq'], 'L0_attn_bq': _L0_attn_in['bq'], 'L0_ffn_phi_w': _L0_ffn_in['phi_w'], 'L0_ffn_phi_b': _L0_ffn_in['phi_b'], 'L0_ffn_expert_w': _L0_ffn_in['expert_w'], 'L0_ffn_expert_b': _L0_ffn_in['expert_b'], 'L1_attn_W_in': _L1_attn_in['W_in'], 'L1_attn_W_ig': _L1_attn_in['W_ig'], 'L1_attn_b_ig': _L1_attn_in['b_ig'], 'L1_attn_W_rg': _L1_attn_in['W_rg'], 'L1_attn_b_rg': _L1_attn_in['b_rg'], 'L1_attn_lam': _L1_attn_in['lam'], 'L1_attn_W_out': _L1_attn_in['W_out'], 'L1_attn_h0': _L1_attn_in['h0'], 'L1_attn_norm_w': _L1_attn_in['norm_w'], 'L1_ffn_W_r': _L1_ffn_in['W_r'], 'L1_ffn_W_k': _L1_ffn_in['W_k'], 'L1_ffn_W_v': _L1_ffn_in['W_v'], 'L1_ffn_mu_r': _L1_ffn_in['mu_r'], 'L1_ffn_mu_k': _L1_ffn_in['mu_k']}
    _x0 = _d['L0_attn_inputs']
    _d['L0_attn_inputs'] = jax.random.normal(jax.random.fold_in(jax.random.key(seed), 1), (16, 512, 128), dtype=_x0.dtype)
    del _x0
    return _d

def reference(L0_attn_inputs, L0_attn_Wq, L0_attn_bq, L0_ffn_phi_w, L0_ffn_phi_b, L0_ffn_expert_w, L0_ffn_expert_b, L1_attn_W_in, L1_attn_W_ig, L1_attn_b_ig, L1_attn_W_rg, L1_attn_b_rg, L1_attn_lam, L1_attn_W_out, L1_attn_h0, L1_attn_norm_w, L1_ffn_W_r, L1_ffn_W_k, L1_ffn_W_v, L1_ffn_mu_r, L1_ffn_mu_k):

    def _L0_attn_ref(inputs, Wq, bq):
        import jax, jax.numpy as jnp
        import numpy as np
        HIDDEN = 128
        B, S = (8, 256)
        Q = jnp.einsum('bsh,hd->bsd', inputs, Wq) + bq
        K = Q
        V = Q
        scale = 1.0 / jnp.sqrt(jnp.float32(HIDDEN))
        scores = jnp.einsum('bqh,bkh->bqk', Q, K) * scale
        probs = jax.nn.softmax(scores, axis=-1)
        out = jnp.einsum('bqk,bkh->bqh', probs, V)
        return out

    def _L0_ffn_ref(x, phi_w, phi_b, expert_w, expert_b):
        import jax, jax.numpy as jnp
        import numpy as np
        T, Z, D_DIM = (8, 256, 128)
        N_EXP, P_SLOT, H = (64, 32, 128)
        LN_EPS = 1e-05
        t, z, d = x.shape
        n = expert_w.shape[0]
        p = phi_w.shape[0] // n
        logits = (jnp.einsum('tzd,ed->tze', x, phi_w) + phi_b).reshape(t, z, n, p)
        D = jax.nn.softmax(logits, axis=3)
        C = jax.nn.softmax(logits, axis=2)
        X_tilde = jnp.einsum('tznp,tzd->npd', D, x)
        X_tilde = jnp.clip(X_tilde, -33000.0, 65000.0)
        mu = jnp.mean(X_tilde, axis=-1, keepdims=True)
        var = jnp.mean(jnp.square(X_tilde - mu), axis=-1, keepdims=True)
        X_tilde = (X_tilde - mu) * jax.lax.rsqrt(var + LN_EPS)
        X_tilde = jnp.tanh(X_tilde)
        Y_tilde = jnp.einsum('npd,ndH->npH', X_tilde, expert_w) + expert_b[:, None, :]
        Y = jnp.einsum('tznp,npH->tzH', C, Y_tilde)
        return Y

    def _L1_attn_ref(x, W_in, W_ig, b_ig, W_rg, b_rg, lam, W_out, h0, norm_w):
        import jax, jax.numpy as jnp
        import numpy as np
        B, S, D = (4, 512, 128)
        H = D
        C = 8.0

        def _rmsnorm(x, w, eps=1e-06):
            xf = x.astype(jnp.float32)
            norm = xf * jax.lax.rsqrt(jnp.mean(xf * xf, axis=-1, keepdims=True) + eps)
            return (norm * w).astype(x.dtype)
        x_proj = jnp.einsum('bsd,hd->bsh', x, W_in)
        i_t = jax.nn.sigmoid(jnp.einsum('bsd,hd->bsh', x, W_ig) + b_ig)
        r_t = jax.nn.sigmoid(jnp.einsum('bsd,hd->bsh', x, W_rg) + b_rg)
        log_a = jnp.log(jax.nn.sigmoid(lam) + 1e-08)
        a_t = jnp.exp(C * r_t * log_a)
        gated = jnp.sqrt(1.0 - a_t * a_t + 1e-06) * (i_t * x_proj)
        h_init = jnp.broadcast_to(h0[0, 0], (x.shape[0], h0.shape[-1]))

        def step(h, inp):
            a, g = inp
            h = a * h + g
            return (h, h)
        xs = (jnp.swapaxes(a_t, 0, 1), jnp.swapaxes(gated, 0, 1))
        _, hs = jax.lax.scan(step, h_init, xs)
        out = jnp.swapaxes(hs, 0, 1)
        out = _rmsnorm(out, norm_w)
        return jnp.einsum('bsh,dh->bsd', out, W_out)

    def _L1_ffn_ref(x, W_r, W_k, W_v, mu_r, mu_k):
        import jax, jax.numpy as jnp
        import numpy as np
        DIM = 128

        def _reference_tuple_inner(x, W_r, W_k, W_v, mu_r, mu_k):
            B, T, C = x.shape
            x_prev = jnp.concatenate([jnp.zeros((B, 1, C), x.dtype), x[:, :-1, :]], axis=1)
            xr = mu_r * x + (1.0 - mu_r) * x_prev
            xk = mu_k * x + (1.0 - mu_k) * x_prev
            r = jax.nn.sigmoid(jnp.einsum('btc,dc->btd', xr, W_r))
            k = jnp.einsum('btc,dc->btd', xk, W_k)
            k_act = jnp.square(jax.nn.relu(k))
            out = r * jnp.einsum('btc,dc->btd', k_act, W_v)
            new_state = x[:, -1, :]
            return (out, new_state)
        return _reference_tuple_inner(x, W_r, W_k, W_v, mu_r, mu_k)[0]
    x = L0_attn_inputs
    xn = _layernorm(x, axis=-1)
    s = _L0_attn_ref(xn, L0_attn_Wq, L0_attn_bq)
    g = _silu(_L0_ffn_ref(xn, L0_ffn_phi_w, L0_ffn_phi_b, L0_ffn_expert_w, L0_ffn_expert_b))
    x = x + s * g
    xn = _layernorm(x, axis=-1)
    s = _L1_attn_ref(xn, L1_attn_W_in, L1_attn_W_ig, L1_attn_b_ig, L1_attn_W_rg, L1_attn_b_rg, L1_attn_lam, L1_attn_W_out, L1_attn_h0, L1_attn_norm_w)
    g = _silu(_L1_ffn_ref(xn, L1_ffn_W_r, L1_ffn_W_k, L1_ffn_W_v, L1_ffn_mu_r, L1_ffn_mu_k))
    x = x + s * g
    return x

_drawn_inputs = setup_inputs


def setup_inputs(seed=0):
    import zlib

    import numpy as np

    out = dict(_drawn_inputs(seed))
    spreads = {'L1_attn_b_ig': (0.0, 2.0),
     'L1_attn_b_rg': (0.0, 2.0),
     'L1_attn_h0': (0.0, 0.8),
     'L1_attn_norm_w': (1.0, 0.6)}
    factors = {'L0_attn_bq': 56.11,
     'L0_ffn_phi_w': 2.95,
     'L0_ffn_phi_b': 64.0,
     'L1_attn_W_rg': 35.968,
     'L1_attn_lam': 24.264,
     'L1_ffn_W_r': 5.904,
     'L1_ffn_mu_r': 8.0,
     'L1_attn_W_in': 35.739,
     'L1_attn_W_ig': 41.523}
    for name, (base, spread) in spreads.items():
        noise = np.random.default_rng([zlib.crc32(name.encode()), seed]).standard_normal(out[name].shape)
        drawn = base * np.exp(spread * noise) if base else spread * noise
        out[name] = jnp.asarray(drawn.astype(out[name].dtype))
    for name, factor in factors.items():
        out[name] = (out[name] * factor).astype(out[name].dtype)
    return out
```

```python
from contextlib import ExitStack

import concourse.bass as bass
import concourse.mybir as mybir
import numpy as np

F32 = mybir.dt.float32
F32R = mybir.dt.float32r
BF16 = mybir.dt.bfloat16
ALU = mybir.AluOpType
ACT = mybir.ActivationFunctionType
AX_X = mybir.AxisListType.X

P = 128
TILE = 128
BANK = 512
PE, ACTE, DVE, POOL, SP = "tensor", "scalar", "vector", "gpsimd", "sync"

V_BQ, V_BIG, V_BRG, V_LAM, V_H0, V_NORM, V_MUR, V_MUK = range(8)
W_Q, W_IN, W_IG, W_RG, W_OUT, W_R, W_K, W_V = range(8)


class Stage:

    def __init__(self, sem, producer, inc=1, credit=0):
        self.sem, self.producer, self.inc, self.credit = sem, producer, inc, credit

    def after(self, unit):
        return (unit + 1) * self.inc + self.credit


class Steps:

    def __init__(self, engine, name):
        self.engine, self.name = engine, name

    def __call__(self, who, make, waits=(), done=None):
        if who != self.name:
            return
        for stage, unit in waits:
            value = stage.after(unit)
            if isinstance(value, int) and value <= stage.credit:
                continue
            self.engine.wait_ge(stage.sem, value)
        instruction = make(self.engine)
        if done is not None:
            instruction.then_inc(done.sem, done.inc)


def build(nc, t):
    TOK = t["x"].shape[0]
    NT = TOK // TILE
    SLOTS = t["phiT"].shape[1]
    NEXP = t["expert_b"].shape[0]
    NP = SLOTS // NEXP
    HALVES = 2
    HS = SLOTS // HALVES
    HN = NEXP // HALVES
    SEQ = 512
    NB = TOK // SEQ
    TPB = SEQ // TILE
    CH = SLOTS // P
    EPC = P // NP
    G = 2 * NP
    assert HN == NP == 32 and HS == 2 * BANK and SEQ == BANK

    root = ExitStack()

    def sb(stack, name, shape, dt=F32):
        return stack.enter_context(nc.sbuf_tensor(name, shape, dt))

    def psum(stack, name, shape, dt=F32):
        return stack.enter_context(nc.psum_tensor(name, shape, dt))

    def stage(name, producer, inc=1, credit=0):
        return Stage(root.enter_context(nc.semaphore(name)), producer, inc, credit)

    def phase(program, stages=()):
        with nc.Block() as block:
            for name, part in ((SP, block.sync), (PE, block.tensor), (ACTE, block.scalar), (DVE, block.vector),
                               (POOL, block.gpsimd)):
                def engine_part(engine, name=name):
                    for s in stages:
                        if s.credit and s.producer == name:
                            engine.sem_inc(s.sem, s.credit)
                    program(Steps(engine, name), engine)
                part(engine_part)

    with root:
        XT = sb(root, "xn_transposed", [P, NT, 2, TILE], F32R)
        PHI = sb(root, "phi_transposed", [P, 2, SLOTS], F32R)
        LSE = sb(root, "lse_over_experts", [3 * NP, TOK], BF16)
        YHI = sb(root, "expert_out_high", [P, CH, P], F32R)
        YLO = sb(root, "expert_out_low", [P, CH, P], F32R)
        WRAW = sb(root, "weights", [P, 8, P])
        WHI = sb(root, "weights_high", [P, 4, P], F32R)
        WLO = sb(root, "weights_low", [P, 4, P], F32R)
        VEC = sb(root, "vectors", [P, 8])
        VX = sb(root, "derived_vectors", [P, 8])
        PHIB = sb(root, "phi_bias_by_slot", [P, CH])
        IDENT = sb(root, "identity", [P, P])
        IDENTB = sb(root, "identity_bf16", [P, P], BF16)
        MEAN = sb(root, "ones_over_width", [P, P])
        MINUS_P = sb(root, "minus_slot_pick", [3 * NP, P], BF16)
        EPS = sb(root, "epsilons", [P, 4])

        def hi_f32(ap):
            return ap.bitcast(F32)

        XND = nc.dram_tensor("xn_rows", (TOK, P), F32).ap()
        xnd = XND.rearrange("(n p) d -> p n d", p=P)
        both = ExitStack()
        SM = sb(both, "slot_max", [P, HALVES, NT, NP])
        SS = sb(both, "slot_sum", [P, HALVES, NT, NP])
        XTT = sb(both, "x_tilde", [P, SLOTS])
        front = ExitStack()
        BIAS3 = sb(front, "phi_bias_parts", [3, SLOTS], BF16)
        ONES3 = sb(front, "ones3", [3, TILE], BF16)
        S1M = sb(front, "shift_experts", [G, HS], F32R)
        S2M = sb(front, "shift_experts_to_slots", [G, HS], F32R)
        with ExitStack() as ph:
            XN = [SM[:, :, :, :].rearrange("q h t p -> q (h t p)").rearrange("q (n d) -> q n d", d=P),
                  SS[:, :, :, :].rearrange("q h t p -> q (h t p)").rearrange("q (n d) -> q n d", d=P)]
            xn = lambda k: XN[k // (NT // 2)][:, k % (NT // 2), :]
            phi_raw = XTT
            brow = sb(ph, "bias_row", [1, SLOTS])
            bpart = sb(ph, "bias_part", [1, 3, SLOTS], BF16)
            shifts = [sb(ph, f"shift_raw{k}", [G, HS]) for k in range(2)]
            stats = sb(ph, "stats", [P, NT, 6])
            mv = sb(ph, "mean_var", [P, NT, 2])
            std = sb(ph, "std", [P, NT])
            rstd = sb(ph, "rstd", [P, NT])
            lam2 = sb(ph, "lam_work", [P, 8])
            tp = [psum(ph, f"tp{k}", [P, BANK]) for k in range(2)]

            s_x = [stage(f"p0_x{k}", SP, 16) for k in range(4)]
            s_w = stage("p0_weights", SP, 16)
            s_b = stage("p0_bias", SP, 16)
            s_b3 = stage("p0_bias_parts", SP, 16)
            s_phi = stage("p0_phi", SP, 16)
            s_xnd = stage("p0_xn_stored", SP, 16)
            s_id = stage("p0_identity", POOL)
            s_dve = stage("p0_vector", DVE)
            s_std = stage("p0_std", ACTE)
            s_bn = stage("p0_stats", DVE)
            s_nrm = stage("p0_normalised", DVE)
            s_tp = stage("p0_transposed", PE)
            s_hi = stage("p0_high", ACTE)
            s_lo = stage("p0_low", DVE)
            s_lam = stage("p0_lam", ACTE)
            QX = NT // 4

            def phase0(op, eng):
                for k in range(4):
                    op(SP, lambda e, k=k: e.dma_start(
                        XN[k // 2][:, k % 2 * QX:(k % 2 + 1) * QX, :],
                        t["x"].rearrange("(n p) d -> p n d", p=P)[:, k * QX:(k + 1) * QX, :]), done=s_x[k])
                op(ACTE, lambda e: e.dma_start(phi_raw[:, :], t["phiT"]), done=s_phi)
                op(ACTE, lambda e: e.dma_start(brow[:, :], t["phi_b"]), done=s_b)
                op(ACTE, lambda e: e.dma_start(WRAW[:, :, :], t["weights"]), done=s_w)
                op(ACTE, lambda e: e.dma_start(VEC[:, :], t["vectors"]), done=s_w)
                op(ACTE, lambda e: e.dma_start(PHIB[:, :], t["phi_b_cols"]), done=s_w)

                made = [0]

                def pattern(dst, fill, step):
                    op(POOL, lambda e: e.affine_select(out=dst, in_=dst, compare_op=ALU.not_equal, fill=fill,
                                                       base=0, pattern=step, channel_multiplier=1),
                       [(s_id, made[0] - 1)], s_id)
                    made[0] += 1
                for dst in (IDENT, IDENTB, *shifts, MINUS_P):
                    op(POOL, lambda e, dst=dst: e.memset(dst[:, :], 0.0), done=s_id)
                    made[0] += 1
                pattern(IDENT[:, :], 1.0, [[-1, P]])
                pattern(IDENTB[:, :], 1.0, [[-1, P]])
                for m, rows, fill, step in ((shifts[0], 0, -1.0, [[-1, HN], [0, NP]]),
                                            (shifts[1], 0, 1.0, [[-1, HN], [0, NP]]),
                                            (shifts[1], HN, -1.0, [[0, HN], [-1, NP]])):
                    pattern(m[rows:rows + 32, :].rearrange("r (n p) -> r n p", p=NP), fill, step)
                for part in range(3):
                    pattern(MINUS_P[part * NP:(part + 1) * NP, :].rearrange("r (j p) -> r j p", p=NP),
                            -1.0, [[0, EPC], [-1, NP]])

                n = [0]

                def vec(make, waits=(), chain=True):
                    op(DVE, make, list(waits) + ([(s_dve, n[0] - 1)] if chain and n[0] else []), s_dve)
                    n[0] += 1
                vec(lambda e: e.memset(MEAN[:, :], 1.0 / P), chain=False)
                vec(lambda e: e.memset(ONES3[:, :], 1.0), chain=False)
                vec(lambda e: e.memset(EPS[:, 0:1], 1e-5), chain=False)
                vec(lambda e: e.memset(EPS[:, 1:2], 1e-6), chain=False)
                vec(lambda e: e.memset(EPS[:, 2:3], 1e-8), chain=False)
                vec(lambda e: e.memset(EPS[:, 3:4], 0.0), chain=False)
                eps_ready = n[0] - 1
                for k in range(NT):
                    op(DVE, lambda e, k=k: e.bn_stats(stats[:, k, :], xn(k)), [(s_x[k // QX], 0)], s_bn)
                for k in range(NT):
                    op(DVE, lambda e, k=k: e.bn_aggr(mv[:, k, :], stats[:, k, :]), [(s_bn, k)], s_bn)
                op(ACTE, lambda e: e.activation(std[:, :], mv[:, :, 1], ACT.Sqrt, bias=EPS[:, 0:1]),
                   [(s_bn, 2 * NT - 1), (s_dve, eps_ready)], s_std)
                vec(lambda e: e.reciprocal(rstd[:, :], std[:, :]), [(s_std, 0)], chain=False)
                rstd_ready = n[0] - 1

                def group(g):
                    for j in range(TPB):
                        k = g * TPB + j
                        op(DVE, lambda e, k=k: e.tensor_scalar(
                            xn(k), xn(k), mv[:, k, 0:1], rstd[:, k:k + 1],
                            ALU.subtract, ALU.mult), [(s_dve, rstd_ready)], s_nrm)
                    for j in range(TPB):
                        k = g * TPB + j
                        op(PE, lambda e, k=k, j=j: e.transpose(
                            tp[g % 2][:, j * TILE:(j + 1) * TILE], xn(k), IDENT[:, :]),
                           [(s_nrm, k), (s_id, 5), (s_lo, g - 2)], s_tp)
                    view = tp[g % 2][:, :].rearrange("p (n k) -> p n k", k=TILE)
                    tiles = slice(g * TPB, (g + 1) * TPB)
                    op(ACTE, lambda e: e.activation(XT[:, tiles, 0, :], view, ACT.Copy),
                       [(s_tp, (g + 1) * TPB - 1)], s_hi)
                    op(DVE, lambda e: e.tensor_tensor(XT[:, tiles, 1, :], view, hi_f32(XT[:, tiles, 0, :]),
                                                      ALU.subtract), [(s_hi, g)], s_lo)
                for g in range(NB):
                    group(g)
                for k in range(4):
                    op(SP, lambda e, k=k: e.dma_start(
                        xnd[:, k * QX:(k + 1) * QX, :], XN[k // 2][:, k % 2 * QX:(k % 2 + 1) * QX, :]),
                       [(s_nrm, (k + 1) * QX - 1)], s_xnd)

                for raw, dst in zip(shifts, (S1M, S2M)):
                    vec(lambda e, raw=raw, dst=dst: e.tensor_copy(dst[:, :], raw[:, :]), [(s_id, made[0] - 1)])
                vec(lambda e: e.tensor_copy(PHI[:, 0, :], phi_raw[:, :]), [(s_phi, 0)])
                vec(lambda e: e.tensor_tensor(PHI[:, 1, :], phi_raw[:, :], hi_f32(PHI[:, 0, :]), ALU.subtract))
                vec(lambda e: e.tensor_copy(WHI[:, :, :], WRAW[:, 0:4, :]), [(s_w, 2)])
                vec(lambda e: e.tensor_tensor(WLO[:, :, :], WRAW[:, 0:4, :], hi_f32(WHI[:, :, :]), ALU.subtract))
                vec(lambda e: e.tensor_copy(bpart[:, 0, :], brow[:, :]), [(s_b, 0)])
                vec(lambda e: e.tensor_tensor(brow[:, :], brow[:, :], bpart[:, 0, :], ALU.subtract))
                vec(lambda e: e.tensor_copy(bpart[:, 1, :], brow[:, :]))
                vec(lambda e: e.tensor_tensor(bpart[:, 2, :], brow[:, :], bpart[:, 1, :], ALU.subtract))
                bias_ready = n[0] - 1
                for part in range(3):
                    op(SP, lambda e, part=part: e.dma_start(BIAS3[part:part + 1, :], bpart[:, part, :]),
                       [(s_dve, bias_ready)], s_b3)
                vec(lambda e: e.tensor_scalar(WRAW[:, W_OUT, :], WRAW[:, W_OUT, :], VEC[:, V_NORM:V_NORM + 1], None,
                                              ALU.mult))
                vec(lambda e: e.tensor_scalar(VX[:, 0:1], VEC[:, V_BIG:V_BIG + 1], 0.5, None, ALU.mult))
                vec(lambda e: e.tensor_scalar(VX[:, 1:2], VEC[:, V_BRG:V_BRG + 1], 0.5, None, ALU.mult))
                vec(lambda e: e.tensor_scalar(VX[:, 3:5], VEC[:, V_MUR:V_MUK + 1], -1.0, 1.0, ALU.mult, ALU.add))
                op(ACTE, lambda e: e.activation(lam2[:, 0:1], VEC[:, V_LAM:V_LAM + 1], ACT.Exp, scale=-1.0),
                   [(s_w, 2)], s_lam)
                vec(lambda e: e.tensor_scalar(lam2[:, 1:2], lam2[:, 0:1], 1.0, None, ALU.add), [(s_lam, 0)])
                vec(lambda e: e.reciprocal(lam2[:, 2:3], lam2[:, 1:2]))
                vec(lambda e: e.tensor_scalar(lam2[:, 4:5], lam2[:, 2:3], 1e-8, None, ALU.add))
                lam_ready = n[0] - 1
                op(ACTE, lambda e: e.activation(lam2[:, 3:4], lam2[:, 4:5], ACT.Ln), [(s_dve, lam_ready)], s_lam)
                vec(lambda e: e.tensor_scalar(VX[:, 2:3], lam2[:, 3:4], 4.0, None, ALU.mult), [(s_lam, 1)])
                op(SP, lambda e: e.nop(), [(s_b3, 2), (s_xnd, 3)])
            phase(phase0)

        with ExitStack() as ph:
            xs = [sb(ph, f"xs{b}", [P, 2, TILE], F32R) for b in range(2)]
            xns = [sb(ph, f"xns{b}", [P, P]) for b in range(2)]
            mx = [sb(ph, f"mx{b}", [P, G]) for b in range(2)]
            mr = [sb(ph, f"mr{b}", [P, G], F32R) for b in range(2)]
            mt = [sb(ph, f"mt{b}", [G, TILE], F32R) for b in range(2)]
            ed = [sb(ph, f"ed{b}", [P, HS]) for b in range(2)]
            ec = [sb(ph, f"ec{b}", [P, HS]) for b in range(2)]
            dd = [sb(ph, f"dd{b}", [P, HS]) for b in range(2)]
            cs = [sb(ph, f"cs{b}", [P, HS // 2]) for b in range(2)]
            zd = [sb(ph, f"zd{b}", [P, HN]) for b in range(2)]
            rz = [sb(ph, f"rz{b}", [P, HN]) for b in range(2)]
            lg = [psum(ph, f"lg{b}", [P, HS]) for b in range(2)]
            acc = [psum(ph, f"acc{k}", [P, BANK]) for k in range(2)]
            tr = [psum(ph, f"tr{b}", [G, TILE]) for b in range(2)]

            s_xs = [stage(f"p1_xs{b}", SP, 16) for b in range(2)]
            s_xns = [stage(f"p1_xns{b}", SP, 16) for b in range(2)]
            s_l = [stage(f"p1_logits{k}", PE) for k in range(2)]
            s_mx = stage("p1_max", DVE)
            s_mm = stage("p1_max_rounded", ACTE)
            s_tr = stage("p1_max_transposed", PE)
            s_mt = stage("p1_max_transposed_copied", ACTE)
            s_s1 = [stage(f"p1_shift1{k}", PE) for k in range(2)]
            s_ed = [stage(f"p1_exp_experts{k}", ACTE) for k in range(2)]
            s_s2 = [stage(f"p1_shift2{k}", PE) for k in range(2)]
            s_ec = [stage(f"p1_exp_slots{k}", ACTE) for k in range(2)]
            s_zd = stage("p1_expert_sum", DVE)
            s_rz = stage("p1_expert_sum_inverse", DVE)
            s_cs = stage("p1_slot_half_sum", POOL)
            s_sm = stage("p1_slot_shift_kept", ACTE)
            s_dd = [stage(f"p1_dispatch{k}", POOL) for k in range(2)]
            s_ss = stage("p1_slot_sum", DVE)
            s_xa = [stage(f"p1_x_tilde{k}", PE) for k in range(2)]
            s_ev = stage("p1_x_tilde_copied", ACTE)

            def by_parity(s, u, b):
                class Halved:
                    sem, credit = s[b].sem, 0
                    after = staticmethod(lambda _: (u - b) // 2 * 16 + 16 if isinstance(u, int)
                                         else (u - b) * 8 + 16)
                return (Halved, 0)

            def slot(op, h, u, v, first, last, u_ok=True, v_ok=True, w_ok=True, xs_ok=True):
                a = h * NT + u
                b, c = v, 1 - v
                half = h * HS

                if xs_ok:
                    op(SP, lambda e: e.dma_start(hi_f32(xs[c][:, :, :]), hi_f32(
                        XT[:, bass.ds(u + 1, 1), :, :].rearrange("q o a k -> q (o a) k"))),
                       [(s_l[1], a - 1)], s_xs[c])
                if v_ok:
                    op(SP, lambda e: e.dma_start(xns[c][:, :], XND[bass.ds((u - 1) * TILE, TILE), :]),
                       [(s_xa[1], a - 3)], s_xns[c])

                def logits(k):
                    cols = slice(half + k * BANK, half + (k + 1) * BANK)
                    out = lg[b][:, k * BANK:(k + 1) * BANK]
                    op(PE, lambda e: e.matmul(out, ONES3[:, :], BIAS3[:, cols], start=True, stop=False),
                       [(s_ec[k], a - 2)])
                    op(PE, lambda e: e.matmul(out, xs[b][:, 0, :], PHI[:, 0, cols], start=False, stop=False),
                       [by_parity(s_xs, a, b)])
                    op(PE, lambda e: e.matmul(out, xs[b][:, 0, :], PHI[:, 1, cols], start=False, stop=False))
                    op(PE, lambda e: e.matmul(out, xs[b][:, 1, :], PHI[:, 0, cols], start=False, stop=True),
                       done=s_l[k])

                def shift(k, matrix, waits, done):
                    cols = slice(k * BANK, (k + 1) * BANK)
                    op(PE, lambda e: e.matmul(lg[c][:, cols], mt[c][:, :], matrix[:, cols], start=False, stop=True,
                                              skip_group_check=True), waits, done)

                def x_tilde(k):
                    cols = slice(k * BANK, (k + 1) * BANK)
                    op(PE, lambda e: e.matmul(acc[k][:, :], xns[b][:, :], dd[b][:, cols], start=first, stop=last,
                                              skip_group_check=True),
                       [by_parity(s_xns, a - 2, b), (s_dd[k], a - 2)] + ([(s_ev, 2 * h - 1)] if first else []),
                       s_xa[k])

                if u_ok:
                    logits(0)
                if v_ok:
                    op(PE, lambda e: e.matmul(tr[c][:, :], hi_f32(mr[c][:, :]), IDENT[:, :], start=True, stop=True),
                       [(s_mm, a - 1), (s_mt, a - 3)], s_tr)
                if u_ok:
                    logits(1)
                if v_ok:
                    shift(0, S1M, [(s_mt, a - 1)], s_s1[0])
                    shift(1, S1M, [], s_s1[1])
                if w_ok:
                    x_tilde(0)
                if v_ok:
                    shift(0, S2M, [(s_ed[0], a - 1)], s_s2[0])
                    shift(1, S2M, [(s_ed[1], a - 1)], s_s2[1])
                if w_ok:
                    x_tilde(1)

                if v_ok:
                    op(ACTE, lambda e: e.activation(mt[c][:, :], tr[c][:, :], ACT.Copy),
                       [(s_tr, a - 1), (s_s2[1], a - 3)], s_mt)
                    for k in range(2):
                        cols = slice(k * BANK, (k + 1) * BANK)
                        op(ACTE, lambda e, k=k, cols=cols: e.activation(ed[c][:, cols], lg[c][:, cols], ACT.Exp),
                           [(s_s1[k], a - 1), (s_dd[k], a - 3), (s_zd, a - 3)], s_ed[k])
                    for k in range(2):
                        cols = slice(k * BANK, (k + 1) * BANK)
                        op(ACTE, lambda e, k=k, cols=cols: e.activation(ec[c][:, cols], lg[c][:, cols], ACT.Exp),
                           [(s_s2[k], a - 1), (s_cs, a - 3)], s_ec[k])

                if u_ok:
                    op(ACTE, lambda e: e.activation(mr[b][:, :], mx[b][:, :], ACT.Copy),
                       [(s_mx2, a), (s_mx, 2 * a + 1), (s_tr, a - 2), (s_sm, a - 2)], s_mm)
                    op(ACTE, lambda e: e.activation(
                        SM[:, h, bass.ds(u, 1), :].rearrange("q o p -> q (o p)"), hi_f32(mr[b][:, HN:G]), ACT.Copy),
                       [(s_mm, a)], s_sm)

                def bank_max(k):
                    op(DVE, lambda e: e.tensor_reduce(
                        mx[b][:, k * HN // 2:(k + 1) * HN // 2],
                        lg[b][:, k * BANK:(k + 1) * BANK].rearrange("q (n p) -> q n p", p=NP), AX_X, ALU.max),
                       [(s_l[k], a), (s_mm, a - 2)], s_mx)
                if u_ok:
                    bank_max(0)
                if u_ok:
                    bank_max(1)
                    op(DVE, lambda e: e.tensor_reduce(
                        mx[b][:, HN:G], lg[b][:, :].rearrange("q (n p) -> q p n", p=NP), AX_X, ALU.max), [], s_mx2)
                if v_ok:
                    op(DVE, lambda e: e.tensor_reduce(
                        zd[c][:, :], ed[c][:, :].rearrange("q (n p) -> q n p", p=NP), AX_X, ALU.add),
                       [(s_ed[0], a - 1), (s_ed[1], a - 1)], s_zd)
                if w_ok:
                    op(DVE, lambda e: e.tensor_reduce(
                        SS[:, h, bass.ds(u - 2, 1), :].rearrange("q o p -> q (o p)"),
                        cs[b][:, :].rearrange("q (n p) -> q p n", p=NP), AX_X, ALU.add), [(s_cs, a - 2)], s_ss)
                if v_ok:
                    op(DVE, lambda e: e.reciprocal(rz[c][:, :], zd[c][:, :]),
                       [(s_zd, a - 1), (s_dd[1], a - 3)], s_rz)

                if v_ok:
                    op(POOL, lambda e: e.tensor_tensor(cs[c][:, :], ec[c][:, 0:BANK], ec[c][:, BANK:HS], ALU.add),
                       [(s_ec[0], a - 1), (s_ec[1], a - 1), (s_ss, a - 3)], s_cs)
                    for k in range(2):
                        cols = slice(k * BANK, (k + 1) * BANK)
                        op(POOL, lambda e, k=k, cols=cols: e.tensor_tensor(
                            dd[c][:, cols].rearrange("q (n p) -> q n p", p=NP),
                            ed[c][:, cols].rearrange("q (n p) -> q n p", p=NP),
                            rz[c][:, k * HN // 2:(k + 1) * HN // 2].unsqueeze(2).broadcast_to([P, HN // 2, NP]),
                            ALU.mult), [(s_rz, a - 1), (s_xa[k], a - 3)], s_dd[k])

            s_mx2 = stage("p1_slot_max", DVE)

            def phase1(op, eng):
                for h in range(HALVES):
                    op(SP, lambda e: e.dma_start(hi_f32(xs[0][:, :, :]), hi_f32(XT[:, 0, :, :])),
                       [(s_l[1], h * NT - 2)], s_xs[0])
                    for u in range(4):
                        slot(op, h, u, u % 2, u == 2, False, v_ok=u >= 1, w_ok=u >= 2)
                    with eng.Fori(4, NT - 3, 2) as u:
                        for v in range(2):
                            slot(op, h, u + v, v, False, False)
                    for u in range(NT - 2, NT + 2):
                        slot(op, h, u, u % 2, False, u == NT + 1, u_ok=u < NT, v_ok=u <= NT, xs_ok=u < NT - 1)
                    for k in range(2):
                        op(ACTE, lambda e, k=k, h=h: e.activation(
                            XTT[:, h * HS + k * BANK:h * HS + (k + 1) * BANK], acc[k][:, :], ACT.Copy),
                           [(s_xa[k], (h + 1) * NT - 1)], s_ev)
            phase(phase1)
        front.close()

        with ExitStack() as ph:
            W2 = NT * NP
            m0, m1 = (SM[:, h, :, :].rearrange("q t p -> q (t p)") for h in range(2))
            z0, z1 = (SS[:, h, :, :].rearrange("q t p -> q (t p)") for h in range(2))
            mj = sb(ph, "m_joined", [P, W2])
            l3 = SM[:, :, :, :].rearrange("q h t p -> q (h t p)").bitcast(BF16)[:, 0:NT * 3 * NP]\
                .rearrange("q (t a p) -> q t a p", a=3, p=NP)
            EG = 8
            ew = [sb(ph, f"expert_w{k}", [P, EG, P]) for k in range(2)]
            eb = sb(ph, "expert_b", [P, CH, P])
            xc = sb(ph, "xc", [P, SLOTS])
            sq = sb(ph, "sq", [P, SLOTS])
            yf = sq[:, :].rearrange("q (c h) -> q c h", h=P)
            pm = [psum(ph, f"pm{k}", [P, BANK]) for k in range(4)]
            py = [psum(ph, f"py{k}", [P, BANK]) for k in range(2)]
            pt = [psum(ph, f"pt{k}", [3 * NP, 8, TILE], BF16) for k in range(2)]
            s_ew = stage("pb_expert_b", SP, 16)
            s_ewg = [stage(f"pb_expert_w{k}", SP, 16) for k in range(2)]
            s_v = stage("pb_vector", DVE)
            s_a = stage("pb_scalar", ACTE)
            s_p = stage("pb_tensor", PE)
            s_lt = stage("pb_lse_transposed", PE)
            s_lc = stage("pb_lse_copied", ACTE)

            def phase1b(op, eng):
                nv, na, npe = [0], [0], [0]

                def vec(make, waits=()):
                    op(DVE, make, waits, s_v)
                    nv[0] += 1
                    return (s_v, nv[0] - 1)

                def act(make, waits=()):
                    op(ACTE, make, waits, s_a)
                    na[0] += 1
                    return (s_a, na[0] - 1)

                def pe(make, waits=()):
                    op(PE, make, waits, s_p)
                    npe[0] += 1
                    return (s_p, npe[0] - 1)

                def load_experts(g):
                    op(SP, lambda e: e.dma_start(ew[g % 2][:, :, :], t["expert_w"][:, g * EG:(g + 1) * EG, :]),
                       [ys[(g - 1) * EG // EPC - 1]] if g >= 2 else (), s_ewg[g % 2])
                for g in range(2):
                    load_experts(g)
                for j in range(EPC):
                    op(SP, lambda e, j=j: e.dma_start(
                        eb[j * NP:(j + 1) * NP, :, :],
                        t["expert_b"].rearrange("(c j) h -> j c h", j=EPC)[j:j + 1, :, :].broadcast_to([NP, CH, P])),
                       done=s_ew)
                quarter = [slice(q * BANK, (q + 1) * BANK) for q in range(4)]
                ys = {}
                clip, mean, cen, squ, var, ln, rs, hat, th = ({} for _ in range(9))
                for q, cols in enumerate(quarter):
                    clip[q] = vec(lambda e, cols=cols: e.tensor_scalar(XTT[:, cols], XTT[:, cols], -33000.0, 65000.0,
                                                                       ALU.max, ALU.min))
                for q, cols in enumerate(quarter):
                    mean[q] = pe(lambda e, cols=cols, q=q: e.matmul(pm[q][:, :], MEAN[:, :], XTT[:, cols],
                                                                    start=True, stop=True), [clip[q]])
                for q, cols in enumerate(quarter):
                    cen[q] = vec(lambda e, cols=cols, q=q: e.tensor_tensor(xc[:, cols], XTT[:, cols], pm[q][:, :],
                                                                           ALU.subtract), [mean[q]])
                    squ[q] = act(lambda e, cols=cols: e.activation(sq[:, cols], xc[:, cols], ACT.Square), [cen[q]])
                for q, cols in enumerate(quarter):
                    var[q] = pe(lambda e, cols=cols, q=q: e.matmul(pm[q][:, :], MEAN[:, :], sq[:, cols],
                                                                   start=True, stop=True), [squ[q]])
                jm = vec(lambda e: e.tensor_tensor(mj[:, :], m0, m1, ALU.max))
                d0 = vec(lambda e: e.tensor_tensor(m0, m0, mj[:, :], ALU.subtract), [jm])
                d1 = vec(lambda e: e.tensor_tensor(m1, m1, mj[:, :], ALU.subtract), [jm])
                e0 = act(lambda e: e.activation(m0, m0, ACT.Exp), [d0])
                e1 = act(lambda e: e.activation(m1, m1, ACT.Exp), [d1])
                for q, cols in enumerate(quarter):
                    ln[q] = act(lambda e, cols=cols, q=q: e.activation(sq[:, cols], pm[q][:, :], ACT.Ln,
                                                                       bias=EPS[:, 0:1]), [var[q]])
                for q, cols in enumerate(quarter):
                    rs[q] = act(lambda e, cols=cols: e.activation(sq[:, cols], sq[:, cols], ACT.Exp, scale=-0.5),
                                [ln[q]])
                p0 = vec(lambda e: e.tensor_tensor(z0, z0, m0, ALU.mult), [e0])
                p1 = vec(lambda e: e.tensor_tensor(z1, z1, m1, ALU.mult), [e1])
                js = vec(lambda e: e.tensor_tensor(z0, z0, z1, ALU.add), [p0, p1])
                jl = act(lambda e: e.activation(z1, z0, ACT.Ln), [js])
                for q, cols in enumerate(quarter):
                    hat[q] = vec(lambda e, cols=cols: e.tensor_tensor(xc[:, cols], xc[:, cols], sq[:, cols], ALU.mult),
                                 [rs[q]])
                for q, cols in enumerate(quarter):
                    th[q] = act(lambda e, cols=cols: e.activation(XTT[:, cols], xc[:, cols], ACT.Tanh), [hat[q]])
                lse = vec(lambda e: e.tensor_tensor(mj[:, :], mj[:, :], z1, ALU.add), [jl])
                tp3 = mj[:, :].rearrange("q (t p) -> q t p", p=NP)
                r3 = z0.rearrange("q (t p) -> q t p", p=NP)
                l_hi = vec(lambda e: e.tensor_copy(l3[:, :, 0, :], tp3), [lse])
                l_r = vec(lambda e: e.tensor_tensor(r3, tp3, l3[:, :, 0, :], ALU.subtract), [l_hi])
                l_mid = vec(lambda e: e.tensor_copy(l3[:, :, 1, :], r3), [l_r])
                l_lo = vec(lambda e: e.tensor_tensor(l3[:, :, 2, :], r3, l3[:, :, 1, :], ALU.subtract), [l_mid])
                for c in range(CH):
                    for j in range(EPC):
                        n = c * EPC + j
                        op(PE, lambda e, c=c, j=j, n=n: e.matmul(
                            py[c % 2][j * NP:(j + 1) * NP, 0:P], XTT[:, n * NP:(n + 1) * NP], ew[n // EG % 2][:, n % EG, :],
                            start=True, stop=True),
                           [(s_ewg[n // EG % 2], n // EG // 2), th[c * P // BANK]] + ([ys[c - 2]] if c >= 2 else [])
                           if j == 0 else (), s_p if j == EPC - 1 else None)
                    npe[0] += 1
                    yp = (s_p, npe[0] - 1)
                    ys[c] = vec(lambda e, c=c: e.tensor_tensor(yf[:, c, :], py[c % 2][:, 0:P], eb[:, c, :], ALU.add),
                                [yp, (s_ew, EPC - 1)])
                    if (c + 1) % (EG // EPC) == 0 and (c + 1) // (EG // EPC) + 1 < NEXP // EG:
                        load_experts((c + 1) // (EG // EPC) + 1)
                quads = [slice(c, c + 4) for c in range(0, CH, 4)]
                for n, cc in enumerate(quads):
                    yh = act(lambda e, cc=cc: e.activation(YHI[:, cc, :], yf[:, cc, :], ACT.Copy), [ys[cc.stop - 1]])
                    vec(lambda e, cc=cc: e.tensor_tensor(YLO[:, cc, :], yf[:, cc, :], hi_f32(YHI[:, cc, :]),
                                                         ALU.subtract), [yh])
                for g in range(NT // 8):
                    for k in range(8):
                        op(PE, lambda e, g=g, k=k: e.transpose(
                            pt[g % 2][:, k, :], l3[:, 8 * g + k, :, :].rearrange("q a p -> q (a p)"), IDENTB[:, :]),
                           [l_lo, (s_lc, g - 2)] if k == 0 else (), s_lt if k == 7 else None)
                    op(ACTE, lambda e, g=g: e.activation(
                        LSE[:, g * 8 * TILE:(g + 1) * 8 * TILE].rearrange("r (k n) -> r k n", n=TILE),
                        pt[g % 2][:, :, :], ACT.Copy), [(s_lt, g)], s_lc)
            phase(phase1b)
        both.close()

        with ExitStack() as ph:
            RC = 2
            cf = [sb(ph, f"cf{k}", [P, SEQ]) for k in range(2)]
            chi = [sb(ph, f"chi{k}", [P, SEQ], F32R) for k in range(RC)]
            clo = [sb(ph, f"clo{k}", [P, SEQ], F32R) for k in range(RC)]
            yt = sb(ph, "yt", [P, SEQ])
            names = ("qf", "e0", "e1", "e2", "e3", "st", "xraw", "ty", "x1", "xc", "sq", "rs",
                     "ti", "tg", "aa", "a2", "hh", "xr", "xk", "kr", "f1")
            B = {n: sb(ph, "b_" + n, [P, SEQ]) for n in names}
            XP = sb(ph, "xn1", [P, SEQ + 1])
            R = {n: sb(ph, "r_" + n, [P, SEQ], F32R) for n in ("qh", "ql", "vh", "vl", "xh", "xl")}
            pth = [sb(ph, f"pth{k}", [P, SEQ], F32R) for k in range(2)]
            ptl = [sb(ph, f"ptl{k}", [P, SEQ], F32R) for k in range(2)]
            nmx = sb(ph, "nmx", [P, 4 * TPB])

            lgp = [psum(ph, f"lgp{k}", [P, SEQ]) for k in range(2)]
            yac = psum(ph, "yac", [P, SEQ])
            at = [psum(ph, f"at{k}", [P, SEQ]) for k in range(2)]
            lp = [psum(ph, f"lp{k}", [P, SEQ]) for k in range(3)]

            c_l = stage("c_logits", PE)
            c_e = stage("c_exp", ACTE)
            c_h = stage("c_high", DVE)
            c_s = stage("c_low", DVE)
            c_y = stage("c_y", PE)
            side = []

            def once(name, producer, inc=1, credit=1):
                s = stage(name, producer, inc, credit)
                side.append(s)
                return s
            y_c = once("y_copied", ACTE)
            ALL = dict(
                q_p=PE, q_f=ACTE, q_h=DVE, q_l=DVE, v_p=PE, v_h=ACTE, v_l=DVE,
                o_c=ACTE,
                xr_dma=SP, out_dma=SP,
                t_y=ACTE, u_y=DVE, us=POOL, res=DVE, mn=PE, xc=DVE, sq=ACTE, vr=PE, ln=ACTE, rs=ACTE, xn=DVE,
                xh=DVE, xl=DVE, p_r=PE, p_i=PE, p_x=PE, t_r=ACTE, t_i=ACTE, a=ACTE, ix=DVE, a2=ACTE, om=DVE,
                sl=ACTE, sr=ACTE, gt=DVE, hh=DVE, hq=ACTE, hm=PE, hl=ACTE, hr=ACTE, po=PE, o1=DVE,
                wr=POOL, wk=POOL, xr=DVE, xk=DVE, pr=PE, pk=PE, tr2=ACTE, kr=ACTE, ka=ACTE, pv=PE, f1=DVE,
                tf=ACTE, f2=DVE, f3=DVE, f4=DVE)
            FOUR = dict(s=PE, m=DVE, n=DVE, x=ACTE, z=DVE, p=DVE, w=PE, k=PE, kh=ACTE, kl=DVE)
            S4 = {n: stage("a_" + n, who) for n, who in FOUR.items()}
            S = {n: once("b_" + n, who, credit=16 if who == SP else 1, inc=16 if who == SP else 1)
                 for n, who in ALL.items()}

            def tiles_of(i, part):
                return XT[:, bass.ds(i * TPB, TPB), part, :]

            def chunk_logits(op, i, c):
                g = i * CH + c
                cols = slice(c * P, (c + 1) * P)
                out = lgp[c % 2][:, :]
                op(PE, lambda e: e.matmul(out, MINUS_P[:, :], LSE[:, bass.ds(i * SEQ, SEQ)], start=True, stop=False),
                   [(c_e, g - 2)])
                op(PE, lambda e: e.matmul(out, PHI[:, 0, cols], tiles_of(i, 0), start=False, stop=False))
                op(PE, lambda e: e.matmul(out, PHI[:, 0, cols], tiles_of(i, 1), start=False, stop=False))
                op(PE, lambda e: e.matmul(out, PHI[:, 1, cols], tiles_of(i, 0), start=False, stop=True), done=c_l)
                op(ACTE, lambda e: e.activation(cf[c % 2][:, :], out, ACT.Exp, bias=PHIB[:, c:c + 1]),
                   [(c_l, g), (c_s, g - 2)], c_e)
                op(DVE, lambda e: e.tensor_copy(chi[c % RC][:, :], cf[c % 2][:, :]),
                   [(c_e, g), (c_y, g - RC)], c_h)
                op(DVE, lambda e: e.tensor_tensor(clo[c % RC][:, :], cf[c % 2][:, :], hi_f32(chi[c % RC][:, :]),
                                                  ALU.subtract), [(c_h, g)], c_s)

            def chunk_y(op, i, c):
                g = i * CH + c
                op(PE, lambda e: e.matmul(yac[:, :], YHI[:, c, :], chi[c % RC][:, :], start=c == 0, stop=False),
                   [(c_h, g)] + ([(y_c, i - 1)] if c == 0 else []))
                op(PE, lambda e: e.matmul(yac[:, :], YLO[:, c, :], chi[c % RC][:, :], start=False, stop=False))
                op(PE, lambda e: e.matmul(yac[:, :], YHI[:, c, :], clo[c % RC][:, :], start=False, stop=c == CH - 1),
                   [(c_s, g)], c_y)

            def three(op, out, w, hi, lo, waits, done):
                op(PE, lambda e: e.matmul(out, WHI[:, w, :], hi(), start=True, stop=False), waits)
                op(PE, lambda e: e.matmul(out, WHI[:, w, :], lo(), start=False, stop=False))
                op(PE, lambda e: e.matmul(out, WLO[:, w, :], hi(), start=False, stop=True), done=done)

            def attention(op, i):
                j = lambda n, back=0: (S[n], i - back)
                q = lambda n, k, back=0: (S4[n], (i - back) * TPB + k)
                scale = float(P) ** -0.5

                def project():
                    three(op, at[0][:, :], W_Q, lambda: tiles_of(i, 0), lambda: tiles_of(i, 1), [j("o_c", 1)], S["q_p"])
                    op(ACTE, lambda e: e.activation(B["qf"][:, :], at[0][:, :], ACT.Identity,
                                                    bias=VEC[:, V_BQ:V_BQ + 1]), [j("q_p"), j("v_p", 1)], S["q_f"])
                    op(DVE, lambda e: e.tensor_copy(R["qh"][:, :], B["qf"][:, :]), [j("q_f"), q("s", TPB-1, 1)], S["q_h"])
                    op(DVE, lambda e: e.tensor_tensor(R["ql"][:, :], B["qf"][:, :], hi_f32(R["qh"][:, :]),
                                                      ALU.subtract), [j("q_h")], S["q_l"])

                def values():
                    for k in range(TPB):
                        cols = slice(k * TILE, (k + 1) * TILE)
                        op(PE, lambda e, cols=cols: e.transpose(at[1][:, cols], B["qf"][:, cols], IDENT[:, :]),
                           [j("q_f"), q("kl", TPB-1, 1)] if k == 0 else (), S["v_p"] if k == TPB - 1 else None)
                    op(ACTE, lambda e: e.activation(R["vh"][:, :], at[1][:, :], ACT.Copy), [j("v_p"), q("w", TPB-1, 1)], S["v_h"])
                    op(DVE, lambda e: e.tensor_tensor(R["vl"][:, :], at[1][:, :], hi_f32(R["vh"][:, :]), ALU.subtract),
                       [j("v_h")], S["v_l"])

                def scores(r):
                    rows = slice(r * TILE, (r + 1) * TILE)
                    bank = at[r % 2][:, :]
                    free = [j("q_f"), j("v_l"), q("x", 0), q("x", 1)]
                    op(PE, lambda e: e.matmul(bank, R["qh"][:, rows], R["qh"][:, :], start=True, stop=False),
                       [j("q_h"), free[r]])
                    op(PE, lambda e: e.matmul(bank, R["qh"][:, rows], R["ql"][:, :], start=False, stop=False), [j("q_l")])
                    op(PE, lambda e: e.matmul(bank, R["ql"][:, rows], R["qh"][:, :], start=False, stop=True),
                       done=S4["s"])
                    m, nm, z, rz_ = (nmx[:, 4 * r + k:4 * r + k + 1] for k in range(4))
                    E = B[f"e{r}"][:, :]
                    op(DVE, lambda e: e.tensor_reduce(m, bank, AX_X, ALU.max), [q("s", r)], S4["m"])
                    op(DVE, lambda e: e.tensor_scalar(nm, m, -scale, None, ALU.mult), [q("m", r), q("x", r, 1)],
                       S4["n"])
                    op(ACTE, lambda e: e.activation(E, bank, ACT.Exp, bias=nm, scale=scale, accum_out=z),
                       [q("n", r), q("k", TPB-1, 1), q("z", r, 1)], S4["x"])
                    op(DVE, lambda e: e.reciprocal(rz_, z), [q("x", r), q("p", r, 1)], S4["z"])
                    op(DVE, lambda e: e.tensor_scalar(E, E, rz_, None, ALU.mult), [q("z", r)], S4["p"])

                def turn(k):
                    keys = slice(k * TILE, (k + 1) * TILE)
                    for r in range(TPB):
                        op(PE, lambda e, r=r: e.transpose(at[1][:, r * TILE:(r + 1) * TILE], B[f"e{r}"][:, keys],
                                                          IDENT[:, :]),
                           [q("p", r)] + ([q("x", 3) if k == 0 else q("kl", k - 1)] if r == 0 else []),
                           S4["k"] if r == TPB - 1 else None)
                    op(ACTE, lambda e: e.activation(pth[k % 2][:, :], at[1][:, :], ACT.Copy),
                       [q("k", k), q("w", k-2) if k >= 2 else q("w", k+2, 1)], S4["kh"])
                    op(DVE, lambda e: e.tensor_tensor(ptl[k % 2][:, :], at[1][:, :], hi_f32(pth[k % 2][:, :]),
                                                      ALU.subtract), [q("kh", k)], S4["kl"])

                def weigh(k):
                    keys = slice(k * TILE, (k + 1) * TILE)
                    for n, (v, pt_, after) in enumerate(((R["vh"], pth, "kh"), (R["vl"], pth, "kh"),
                                                         (R["vh"], ptl, "kl"))):
                        op(PE, lambda e, v=v, pt_=pt_, n=n: e.matmul(
                            at[0][:, :], v[:, keys], pt_[k % 2][:, :], start=k == 0 and n == 0,
                            stop=k == TPB - 1 and n == 2),
                           [q(after, k)] + ([j("v_l"), q("x", 2)] if k == 0 and n == 0 else []),
                           S4["w"] if n == 2 else None)

                def finish():
                    op(ACTE, lambda e: e.activation(B["st"][:, :], at[0][:, :], ACT.Copy),
                       [q("w", TPB-1), (S["us"], i - 1)], S["o_c"])

                def group(*pieces):
                    return lambda: [piece() for piece in pieces]
                return [project, values, lambda: scores(0), lambda: scores(1), lambda: scores(2), lambda: scores(3),
                        lambda: turn(0), lambda: turn(1), group(lambda: weigh(0), lambda: turn(2)),
                        group(lambda: weigh(1), lambda: turn(3)), lambda: weigh(2),
                        group(lambda: weigh(3), finish)]

            def layer1(op, i):
                j = lambda n, back=0: (S[n], i - back)
                one = lambda v, k: v[:, k:k + 1]
                x_in = XP[:, 1:SEQ + 1]
                x_prev = XP[:, 0:SEQ]

                def tt(who, out, a, b, f, waits, done):
                    op(who, lambda e: e.tensor_tensor(out[:, :], a[:, :], b[:, :], f), waits, S[done])

                def af(out, in_, func, waits, done, **kw):
                    op(ACTE, lambda e: e.activation(out[:, :], in_[:, :], func, **kw), waits, S[done])

                def residual():
                    op(SP, lambda e: e.dma_start(B["xraw"][:, :], t["xT"][:, bass.ds(i * SEQ, SEQ)]),
                       [j("res", 1)], S["xr_dma"])
                    op(DVE, lambda e: e.scalar_tensor_tensor(B["x1"][:, :], B["ty"][:, :], 0.5, B["xraw"][:, :],
                                                             ALU.mult, ALU.add),
                       [j("us"), j("xr_dma"), j("f4", 1)], S["res"])

                def norm_mean():
                    op(PE, lambda e: e.matmul(lp[0][:, :], MEAN[:, :], B["x1"][:, :], start=True, stop=True),
                       [j("res"), j("f1", 1), j("o1", 1)], S["mn"])
                    tt(DVE, B["xc"], B["x1"], lp[0], ALU.subtract, [j("mn")], "xc")
                    af(B["sq"], B["xc"], ACT.Square, [j("xc")], "sq")

                def norm_var():
                    op(PE, lambda e: e.matmul(lp[1][:, :], MEAN[:, :], B["sq"][:, :], start=True, stop=True),
                       [j("sq"), j("o1", 1), j("hl", 1)], S["vr"])
                    af(B["rs"], lp[1], ACT.Ln, [j("vr")], "ln", bias=one(EPS, 0))
                    af(B["rs"], B["rs"], ACT.Exp, [j("ln")], "rs", scale=-0.5)
                    op(DVE, lambda e: e.tensor_tensor(x_in, B["xc"][:, :], B["rs"][:, :], ALU.mult),
                       [j("rs"), j("wk", 1)], S["xn"])
                    op(DVE, lambda e: e.tensor_copy(R["xh"][:, :], x_in), [j("xn"), j("p_x", 1)], S["xh"])
                    op(DVE, lambda e: e.tensor_tensor(R["xl"][:, :], x_in, hi_f32(R["xh"][:, :]), ALU.subtract),
                       [j("xh")], S["xl"])

                def gates():
                    hi, lo = (lambda: R["xh"][:, :]), (lambda: R["xl"][:, :])
                    three(op, lp[2][:, :], W_RG, hi, lo, [j("xl"), j("o1", 1)], S["p_r"])
                    three(op, lp[0][:, :], W_IG, hi, lo, [j("xc")], S["p_i"])
                    af(B["tg"], lp[2], ACT.Tanh, [j("p_r")], "t_r", scale=0.5, bias=one(VX, 1))
                    af(B["ti"], lp[0], ACT.Tanh, [j("p_i"), j("out_dma", 1)], "t_i", scale=0.5, bias=one(VX, 0))
                    af(B["aa"], B["tg"], ACT.Exp, [j("t_r")], "a", scale=one(VX, 2), bias=one(VX, 2))
                    af(B["a2"], B["aa"], ACT.Square, [j("a")], "a2")
                    three(op, lp[1][:, :], W_IN, hi, lo, [j("rs")], S["p_x"])
                    op(DVE, lambda e: e.scalar_tensor_tensor(B["ti"][:, :], B["ti"][:, :], 1.0, lp[1][:, :],
                                                             ALU.add, ALU.mult), [j("t_i"), j("p_x")], S["ix"])
                    op(DVE, lambda e: e.tensor_scalar(B["a2"][:, :], B["a2"][:, :], -1.0, 1.0, ALU.mult, ALU.add),
                       [j("a2")], S["om"])

                def mix():
                    for n, k, dst in ((0, V_MUR, "wr"), (1, V_MUK, "wk")):
                        op(POOL, lambda e, n=n: e.tensor_tensor(
                            B["xr" if n == 0 else "xk"][:, :], x_prev, one(VX, 3 + n).broadcast_to([P, SEQ]),
                            ALU.mult),
                           [j("xn"), (S["xr" if n == 0 else "xk"], i - 1)], S[dst])
                    for n, k, src, dst, fin in ((0, V_MUR, "xr", "xr", "pr"), (1, V_MUK, "xk", "xk", "pk")):
                        op(DVE, lambda e, k=k, src=src, dst=dst: e.scalar_tensor_tensor(
                            B[dst][:, :], x_in, one(VEC, k), B[src][:, :], ALU.mult, ALU.add),
                           [j("wr" if n == 0 else "wk"), (S[fin], i - 1)], S[dst])

                def ffn_in():
                    op(PE, lambda e: e.matmul(lp[0][:, :], WRAW[:, W_R, :], B["xr"][:, :], start=True, stop=True),
                       [j("xr"), j("t_i")], S["pr"])
                    af(B["f1"], lp[0], ACT.Tanh, [j("pr"), j("f4", 1)], "tr2", scale=0.5)
                    op(PE, lambda e: e.matmul(lp[2][:, :], WRAW[:, W_K, :], B["xk"][:, :], start=True, stop=True),
                       [j("xk"), j("t_r")], S["pk"])
                    af(B["kr"], lp[2], ACT.Relu, [j("pk")], "kr")
                    af(B["kr"], B["kr"], ACT.Square, [j("kr"), j("pv", 1)], "ka")

                def ffn_out():
                    op(PE, lambda e: e.matmul(lp[0][:, :], WRAW[:, W_V, :], B["kr"][:, :], start=True, stop=True),
                       [j("ka"), j("tr2")], S["pv"])
                    op(DVE, lambda e: e.scalar_tensor_tensor(B["kr"][:, :], B["f1"][:, :], 1.0, lp[0][:, :],
                                                             ALU.add, ALU.mult), [j("pv"), j("ka")], S["f1"])
                    af(B["xr"], B["kr"], ACT.Tanh, [j("f1"), j("pr")], "tf", scale=0.25)
                    op(DVE, lambda e: e.scalar_tensor_tensor(B["f1"][:, :], B["xr"][:, :], 1.0, B["kr"][:, :],
                                                             ALU.add, ALU.mult), [j("tf")], S["f2"])

                def silu_y():
                    af(B["ty"], yt, ACT.Tanh, [(y_c, i), j("res", 1)], "t_y", scale=0.5)
                    op(DVE, lambda e: e.scalar_tensor_tensor(B["ty"][:, :], B["ty"][:, :], 1.0, yt[:, :],
                                                             ALU.add, ALU.mult), [j("t_y")], S["u_y"])
                    tt(POOL, B["ty"], B["ty"], B["st"], ALU.mult, [j("u_y"), (S["o_c"], i)], "us")

                def recur():
                    af(B["a2"], B["a2"], ACT.Ln, [j("om")], "sl", bias=one(EPS, 1))
                    af(B["a2"], B["a2"], ACT.Exp, [j("sl")], "sr", scale=0.5)
                    op(DVE, lambda e: e.scalar_tensor_tensor(B["ti"][:, :], B["ti"][:, :], 0.5, B["a2"][:, :],
                                                             ALU.mult, ALU.mult), [j("sr"), j("ix")], S["gt"])
                    op(DVE, lambda e: e.tensor_tensor_scan(B["hh"][:, :], B["aa"][:, :], B["ti"][:, :],
                                                           one(VEC, V_H0), ALU.mult, ALU.add),
                       [j("gt"), j("a"), j("po", 1)], S["hh"])
                    af(B["sq"], B["hh"], ACT.Square, [j("hh"), j("vr")], "hq")

                def output():
                    op(PE, lambda e: e.matmul(lp[2][:, :], WRAW[:, W_OUT, :], B["hh"][:, :], start=True, stop=True),
                       [j("hh"), j("kr")], S["po"])
                    op(PE, lambda e: e.matmul(lp[1][:, :], MEAN[:, :], B["sq"][:, :], start=True, stop=True),
                       [j("hq"), j("ix")], S["hm"])
                    af(B["rs"], lp[1], ACT.Ln, [j("hm"), j("xn")], "hl", bias=one(EPS, 1))
                    af(B["rs"], B["rs"], ACT.Exp, [j("hl")], "hr", scale=-0.5)
                    op(DVE, lambda e: e.tensor_tensor(B["xc"][:, :], lp[2][:, :], B["rs"][:, :], ALU.mult),
                       [j("po"), j("hr")], S["o1"])
                    op(DVE, lambda e: e.scalar_tensor_tensor(B["xc"][:, :], B["f1"][:, :], 0.25, B["xc"][:, :],
                                                             ALU.mult, ALU.mult), [j("o1"), j("f2")], S["f3"])
                    op(DVE, lambda e: e.tensor_tensor(B["ti"][:, :], B["xc"][:, :], B["x1"][:, :], ALU.add),
                       [j("f3")], S["f4"])
                    op(SP, lambda e: e.dma_start(t["out"][:, bass.ds(i * SEQ, SEQ)], B["ti"][:, :]),
                       [j("f4")], S["out_dma"])

                return dict(silu_y=silu_y, residual=residual, norm_mean=norm_mean, norm_var=norm_var, gates=gates,
                            mix=mix, ffn_in=ffn_in, ffn_out=ffn_out, recur=recur, output=output)

            def table(op, name):
                op(ACTE, lambda e: e.preload_act_table_set(name))

            def y_copy(op, i):
                op(ACTE, lambda e: e.activation(yt[:, :], yac[:, :], ACT.Copy),
                   [(c_y, i * CH + CH - 1), (S["u_y"], i - 1)], y_c)

            def iteration(op, i, main=True, first=True, second=True):
                pieces = {c: [] for c in range(CH)}
                if main:
                    for c, piece in zip((1, 2, 3, 4, 5, 6, 8, 9, 10, 12, 13, 14), attention(op, i)):
                        pieces[c].append(piece)
                if first:
                    p = layer1(op, i - 1)
                    pieces[1].append(p["silu_y"])
                    for c, n in ((4, "residual"), (6, "norm_mean"), (8, "norm_var"), (11, "gates"), (11, "mix"),
                                 (13, "ffn_in"), (15, "ffn_out")):
                        pieces[c].append(p[n])
                    pieces[10].append(lambda: table(op, "exp_and_others"))
                if second:
                    p = layer1(op, i - 2)
                    pieces[1].append(lambda: table(op, "natural_log_exp_and_others"))
                    pieces[1].append(p["recur"])
                    pieces[3].append(p["output"])
                for c in range(CH):
                    if main:
                        chunk_logits(op, i, c)
                    if c >= 2 and main:
                        chunk_y(op, i, c - 2)
                    elif c < 2 and first:
                        chunk_y(op, i - 1, CH - 2 + c)
                        if c == 1:
                            y_copy(op, i - 1)
                    for piece in pieces[c]:
                        piece()

            def phase2(op, eng):
                op(DVE, lambda e: e.memset(XP[:, 0:1], 0.0), done=s_zero)
                op(POOL, lambda e: e.nop(), [(s_zero, 0)])
                iteration(op, 0, first=False, second=False)
                iteration(op, 1, second=False)
                with eng.Fori(2, NB) as i:
                    iteration(op, i)
                iteration(op, NB, main=False)
                iteration(op, NB + 1, main=False, first=False)
                op(SP, lambda e: e.nop(), [(S["out_dma"], NB - 1)])
            s_zero = stage("zero_column", DVE)
            phase(phase2, side)


def kernel(**inputs):
    import concourse.bacc as bacc
    from concourse.bass_utils import run_bass_kernel_spmd

    a = {k: np.asarray(v) for k, v in inputs.items()}
    x = a["L0_attn_inputs"]
    tokens, d = x.shape[0] * x.shape[1], x.shape[2]
    x = x.reshape(tokens, d)
    vectors = [a["L0_attn_bq"], a["L1_attn_b_ig"], a["L1_attn_b_rg"], a["L1_attn_lam"],
               a["L1_attn_h0"].reshape(-1), a["L1_attn_norm_w"], a["L1_ffn_mu_r"], a["L1_ffn_mu_k"]]
    weights = [a["L0_attn_Wq"], a["L1_attn_W_in"].T, a["L1_attn_W_ig"].T, a["L1_attn_W_rg"].T,
               a["L1_attn_W_out"].T, a["L1_ffn_W_r"].T, a["L1_ffn_W_k"].T, a["L1_ffn_W_v"].T]
    arrays = {
        "x": x,
        "xT": x.T,
        "phiT": a["L0_ffn_phi_w"].T,
        "phi_b": a["L0_ffn_phi_b"].reshape(1, -1),
        "phi_b_cols": a["L0_ffn_phi_b"].reshape(-1, P).T,
        "expert_w": a["L0_ffn_expert_w"].transpose(1, 0, 2),
        "expert_b": a["L0_ffn_expert_b"],
        "weights": np.stack(weights, axis=1),
        "vectors": np.stack(vectors, axis=1),
    }
    nc = bacc.Bacc("TRN2", target_bir_lowering=False, num_devices=1)
    feed, t = {}, {}
    for name, value in arrays.items():
        value = np.ascontiguousarray(value)
        feed[f"in_{name}"] = value
        t[name] = nc.dram_tensor(f"in_{name}", value.shape, mybir.dt.from_np(value.dtype), kind="ExternalInput").ap()
    t["out"] = nc.dram_tensor("out_t", (d, tokens), F32, kind="ExternalOutput").ap()
    build(nc, t)
    r = run_bass_kernel_spmd(nc, [feed], core_ids=[0])
    out = r.results[0]["out_t"]
    return np.ascontiguousarray(out.T).reshape(inputs["L0_attn_inputs"].shape)
```

```python
from contextlib import ExitStack

import concourse.bass as bass
import concourse.mybir as mybir
import numpy as np

F32 = mybir.dt.float32
F32R = mybir.dt.float32r
BF16 = mybir.dt.bfloat16
ALU = mybir.AluOpType
ACT = mybir.ActivationFunctionType
AX_X = mybir.AxisListType.X

P = 128
TILE = 128
BANK = 512
PE, ACTE, DVE, POOL, SP = "tensor", "scalar", "vector", "gpsimd", "sync"

V_BQ, V_BIG, V_BRG, V_LAM, V_H0, V_NORM, V_MUR, V_MUK = range(8)
W_Q, W_IN, W_IG, W_RG, W_OUT, W_R, W_K, W_V = range(8)


class Stage:

    def __init__(self, sem, producer, inc=1, credit=0):
        self.sem, self.producer, self.inc, self.credit = sem, producer, inc, credit

    def after(self, unit):
        return (unit + 1) * self.inc + self.credit


class Steps:

    def __init__(self, engine, name):
        self.engine, self.name = engine, name

    def __call__(self, who, make, waits=(), done=None):
        if who != self.name:
            return
        for stage, unit in waits:
            value = stage.after(unit)
            if isinstance(value, int) and value <= stage.credit:
                continue
            self.engine.wait_ge(stage.sem, value)
        instruction = make(self.engine)
        if done is not None:
            instruction.then_inc(done.sem, done.inc)


def build(nc, t):
    TOK = t["x"].shape[0]
    NT = TOK // TILE
    SLOTS = t["phiT"].shape[1]
    NEXP = t["expert_b"].shape[0]
    NP = SLOTS // NEXP
    HALVES = 2
    HS = SLOTS // HALVES
    HN = NEXP // HALVES
    SEQ = 512
    NB = TOK // SEQ
    TPB = SEQ // TILE
    CH = SLOTS // P
    EPC = P // NP
    G = 2 * NP
    assert HN == NP == 32 and HS == 2 * BANK and SEQ == BANK

    root = ExitStack()

    def sb(stack, name, shape, dt=F32):
        return stack.enter_context(nc.sbuf_tensor(name, shape, dt))

    def psum(stack, name, shape, dt=F32):
        return stack.enter_context(nc.psum_tensor(name, shape, dt))

    def stage(name, producer, inc=1, credit=0):
        return Stage(root.enter_context(nc.semaphore(name)), producer, inc, credit)

    def phase(program, stages=()):
        with nc.Block() as block:
            for name, part in ((SP, block.sync), (PE, block.tensor), (ACTE, block.scalar), (DVE, block.vector),
                               (POOL, block.gpsimd)):
                def engine_part(engine, name=name):
                    for s in stages:
                        if s.credit and s.producer == name:
                            engine.sem_inc(s.sem, s.credit)
                    program(Steps(engine, name), engine)
                part(engine_part)

    with root:
        XT = sb(root, "xn_transposed", [P, NT, 2, TILE], F32R)
        PHI = sb(root, "phi_transposed", [P, 2, SLOTS], F32R)
        LSE = sb(root, "lse_over_experts", [3 * NP, TOK], BF16)
        YHI = sb(root, "expert_out_high", [P, CH, P], F32R)
        YLO = sb(root, "expert_out_low", [P, CH, P], F32R)
        WRAW = sb(root, "weights", [P, 8, P])
        WHI = sb(root, "weights_high", [P, 4, P], F32R)
        WLO = sb(root, "weights_low", [P, 4, P], F32R)
        VEC = sb(root, "vectors", [P, 8])
        VX = sb(root, "derived_vectors", [P, 8])
        IDENT = sb(root, "identity", [P, P])
        IDENTB = sb(root, "identity_bf16", [P, P], BF16)
        MEAN = sb(root, "ones_over_width", [P, P])
        MINUS_P = sb(root, "minus_slot_pick", [3 * NP, P], BF16)
        EPS = sb(root, "epsilons", [P, 5])

        def hi_f32(ap):
            return ap.bitcast(F32)

        XND = nc.dram_tensor("xn_rows", (TOK, P), F32).ap()
        xnd = XND.rearrange("(n p) d -> p n d", p=P)
        both = ExitStack()
        SM = sb(both, "slot_max", [P, HALVES, NT, NP])
        SS = sb(both, "slot_sum", [P, HALVES, NT, NP])
        XTT = sb(both, "x_tilde", [P, SLOTS])
        front = ExitStack()
        S1M = sb(front, "shift_experts", [G, HS], F32R)
        S2M = sb(front, "shift_experts_to_slots", [G, HS], F32R)
        with ExitStack() as ph:
            XN = [SM[:, :, :, :].rearrange("q h t p -> q (h t p)").rearrange("q (n d) -> q n d", d=P),
                  SS[:, :, :, :].rearrange("q h t p -> q (h t p)").rearrange("q (n d) -> q n d", d=P)]
            xn = lambda k: XN[k // (NT // 2)][:, k % (NT // 2), :]
            phi_raw = XTT
            brow = sb(ph, "bias_row", [1, SLOTS])
            bone = sb(ph, "bias_factor", [1, P])
            shifts = [sb(ph, f"shift_raw{k}", [G, HS]) for k in range(2)]
            stats = sb(ph, "stats", [P, NT, 6])
            mv = sb(ph, "mean_var", [P, NT, 2])
            std = sb(ph, "std", [P, NT])
            rstd = sb(ph, "rstd", [P, NT])
            nmr = sb(ph, "minus_mean_rstd", [P, NT])
            lam2 = sb(ph, "lam_work", [P, 8])
            tp = [psum(ph, f"tp{k}", [P, BANK]) for k in range(2)]
            pc = [psum(ph, f"phi_mean{k}", [P, BANK]) for k in range(4)]
            wc = psum(ph, "wq_mean", [P, P])

            s_x = [stage(f"p0_x{k}", SP, 16) for k in range(4)]
            s_w = stage("p0_weights", SP, 16)
            s_b = stage("p0_bias", SP, 16)
            s_pc = stage("p0_phi_mean", PE)
            s_ps = stage("p0_phi_shifted", DVE)
            s_ph = stage("p0_phi_high", ACTE)
            s_pl = stage("p0_phi_low", POOL)
            s_phi = stage("p0_phi", SP, 16)
            s_xnd = stage("p0_xn_stored", SP, 16)
            s_id = stage("p0_identity", POOL)
            s_dve = stage("p0_vector", DVE)
            s_std = stage("p0_std", ACTE)
            s_bn = stage("p0_stats", DVE)
            s_nrm = stage("p0_normalised_vector", DVE)
            s_nra = stage("p0_normalised_scalar", ACTE)
            s_tp = stage("p0_transposed", PE)
            s_hi = stage("p0_high", ACTE)
            s_lo = stage("p0_low", DVE)
            s_lam = stage("p0_lam", ACTE)
            QX = NT // 4

            def phase0(op, eng):
                for k in range(4):
                    op(SP, lambda e, k=k: e.dma_start(
                        XN[k // 2][:, k % 2 * QX:(k % 2 + 1) * QX, :],
                        t["x"].rearrange("(n p) d -> p n d", p=P)[:, k * QX:(k + 1) * QX, :]), done=s_x[k])
                op(ACTE, lambda e: e.dma_start(phi_raw[:, :], t["phiT"]), done=s_phi)
                op(ACTE, lambda e: e.dma_start(brow[:, :], t["phi_b"]), done=s_b)
                op(ACTE, lambda e: e.dma_start(WRAW[:, :, :], t["weights"]), done=s_w)
                op(ACTE, lambda e: e.dma_start(VEC[:, :], t["vectors"]), done=s_w)

                made = [0]

                def pattern(dst, fill, step):
                    op(POOL, lambda e: e.affine_select(out=dst, in_=dst, compare_op=ALU.not_equal, fill=fill,
                                                       base=0, pattern=step, channel_multiplier=1),
                       [(s_id, made[0] - 1)], s_id)
                    made[0] += 1
                for dst in (IDENT, IDENTB, *shifts, MINUS_P):
                    op(POOL, lambda e, dst=dst: e.memset(dst[:, :], 0.0), done=s_id)
                    made[0] += 1
                pattern(IDENT[:, :], 1.0, [[-1, P]])
                pattern(IDENTB[:, :], 1.0, [[-1, P]])
                for m, rows, fill, step in ((shifts[0], 0, -1.0, [[-1, HN], [0, NP]]),
                                            (shifts[1], 0, 1.0, [[-1, HN], [0, NP]]),
                                            (shifts[1], HN, -1.0, [[0, HN], [-1, NP]])):
                    pattern(m[rows:rows + 32, :].rearrange("r (n p) -> r n p", p=NP), fill, step)
                for part in range(3):
                    pattern(MINUS_P[part * NP:(part + 1) * NP, :].rearrange("r (j p) -> r j p", p=NP),
                            -1.0, [[0, EPC], [-1, NP]])

                n = [0]

                def vec(make, waits=(), chain=True):
                    op(DVE, make, list(waits) + ([(s_dve, n[0] - 1)] if chain and n[0] else []), s_dve)
                    n[0] += 1
                vec(lambda e: e.memset(MEAN[:, :], 1.0 / P), chain=False)
                vec(lambda e: e.memset(bone[:, :], -1.0 / P), chain=False)
                vec(lambda e: e.memset(EPS[:, 0:1], 1e-5), chain=False)
                vec(lambda e: e.memset(EPS[:, 1:2], 1e-6), chain=False)
                vec(lambda e: e.memset(EPS[:, 2:3], 1e-8), chain=False)
                vec(lambda e: e.memset(EPS[:, 3:4], 0.0), chain=False)
                vec(lambda e: e.memset(EPS[:, 4:5], 1.0), chain=False)
                eps_ready = n[0] - 1
                rstd_ready = [0] * 4

                def part(q):
                    return slice(q * QX, (q + 1) * QX)

                def statistics(q):
                    base = 2 * QX * q
                    for k in range(QX):
                        op(DVE, lambda e, k=k: e.bn_stats(stats[:, q * QX + k, :], xn(q * QX + k)), [(s_x[q], 0)], s_bn)
                    for k in range(QX):
                        op(DVE, lambda e, k=k: e.bn_aggr(mv[:, q * QX + k, :], stats[:, q * QX + k, :]),
                           [(s_bn, base + k)], s_bn)
                    op(ACTE, lambda e: e.activation(std[:, part(q)], mv[:, part(q), 1], ACT.Sqrt, bias=EPS[:, 0:1]),
                       [(s_bn, base + 2 * QX - 1), (s_dve, eps_ready)], s_std)

                def inverse(q):
                    vec(lambda e: e.reciprocal(rstd[:, part(q)], std[:, part(q)]), [(s_std, q)], chain=False)
                    vec(lambda e: e.scalar_tensor_tensor(nmr[:, part(q)], mv[:, part(q), 0], -1.0, rstd[:, part(q)],
                                                         ALU.mult, ALU.mult))
                    rstd_ready[q] = n[0] - 1

                def normalise(g):
                    ready = [(s_dve, rstd_ready[g // 4])]
                    for j in range(2):
                        k = g * TPB + j
                        op(DVE, lambda e, k=k: e.tensor_scalar(
                            xn(k), xn(k), mv[:, k, 0:1], rstd[:, k:k + 1], ALU.subtract, ALU.mult), ready, s_nrm)
                        k = g * TPB + 2 + j
                        op(ACTE, lambda e, k=k: e.activation(
                            xn(k), xn(k), ACT.Identity, bias=nmr[:, k:k + 1], scale=rstd[:, k:k + 1]), ready, s_nra)
                    for j in range(TPB):
                        k = g * TPB + j
                        op(PE, lambda e, k=k, j=j: e.transpose(
                            tp[g % 2][:, j * TILE:(j + 1) * TILE], xn(k), IDENT[:, :]),
                           [(s_nrm if j < 2 else s_nra, 2 * g + j % 2), (s_id, 5), (s_lo, g - 2)], s_tp)

                def split(g):
                    view = tp[g % 2][:, :].rearrange("p (n k) -> p n k", k=TILE)
                    tiles = slice(g * TPB, (g + 1) * TPB)
                    op(ACTE, lambda e: e.activation(XT[:, tiles, 0, :], view, ACT.Identity, bias=EPS[:, 4:5]),
                       [(s_tp, (g + 1) * TPB - 1)], s_hi)
                    op(DVE, lambda e: e.scalar_tensor_tensor(XT[:, tiles, 1, :], view, 1.0, hi_f32(XT[:, tiles, 0, :]),
                                                             ALU.add, ALU.subtract), [(s_hi, g)], s_lo)

                for k in range(4):
                    cols = slice(k * BANK, (k + 1) * BANK)
                    op(PE, lambda e, k=k, cols=cols: e.matmul(pc[k][:, :], MEAN[:, :], phi_raw[:, cols],
                                                              start=True, stop=False), [(s_phi, 0), (s_dve, 1)])
                    op(PE, lambda e, k=k, cols=cols: e.matmul(pc[k][:, :], bone[:, :], brow[:, cols],
                                                              start=False, stop=True), [(s_b, 0)], s_pc)
                op(PE, lambda e: e.matmul(wc[:, :], MEAN[:, :], WRAW[:, W_Q, :], start=True, stop=True),
                   [(s_w, 1)], s_pc)

                def shift_phi():
                    for k in range(4):
                        cols = slice(k * BANK, (k + 1) * BANK)
                        op(DVE, lambda e, k=k, cols=cols: e.tensor_tensor(
                            phi_raw[:, cols], phi_raw[:, cols], pc[k][:, :], ALU.subtract), [(s_pc, k)], s_ps)
                        op(ACTE, lambda e, cols=cols: e.activation(PHI[:, 0, cols], phi_raw[:, cols], ACT.Copy),
                           [(s_ps, k)], s_ph)
                        op(POOL, lambda e, cols=cols: e.tensor_tensor(
                            PHI[:, 1, cols], phi_raw[:, cols], hi_f32(PHI[:, 0, cols]), ALU.subtract),
                           [(s_ph, k), (s_id, made[0] - 1)], s_pl)
                    op(DVE, lambda e: e.tensor_tensor(WRAW[:, W_Q, :], WRAW[:, W_Q, :], wc[:, :], ALU.subtract),
                       [(s_pc, 4)], s_ps)
                    op(ACTE, lambda e: e.activation(WHI[:, :, :], WRAW[:, 0:4, :], ACT.Copy), [(s_ps, 4)], s_ph)
                    op(POOL, lambda e: e.tensor_tensor(WLO[:, :, :], WRAW[:, 0:4, :], hi_f32(WHI[:, :, :]),
                                                       ALU.subtract), [(s_ph, 4)], s_pl)

                statistics(0)
                statistics(1)
                inverse(0)
                for g in range(NB + 1):
                    if g == 2:
                        shift_phi()
                    if g % 4 == 2 and g < 8:
                        statistics(g // 4 + 2)
                    if g % 4 == 3 and g < 12:
                        inverse(g // 4 + 1)
                    if g < NB:
                        normalise(g)
                    if g > 0:
                        split(g - 1)
                for k in range(4):
                    op(SP, lambda e, k=k: e.dma_start(
                        xnd[:, k * QX:(k + 1) * QX, :], XN[k // 2][:, k % 2 * QX:(k % 2 + 1) * QX, :]),
                       [(s_nrm, (k + 1) * QX // 2 - 1), (s_nra, (k + 1) * QX // 2 - 1)], s_xnd)

                for raw, dst in zip(shifts, (S1M, S2M)):
                    vec(lambda e, raw=raw, dst=dst: e.tensor_copy(dst[:, :], raw[:, :]), [(s_id, made[0] - 1)])
                vec(lambda e: e.tensor_scalar(WRAW[:, W_OUT, :], WRAW[:, W_OUT, :], VEC[:, V_NORM:V_NORM + 1], None,
                                              ALU.mult), [(s_w, 1)])
                vec(lambda e: e.tensor_scalar(VX[:, 0:1], VEC[:, V_BIG:V_BIG + 1], 0.5, None, ALU.mult))
                vec(lambda e: e.tensor_scalar(VX[:, 1:2], VEC[:, V_BRG:V_BRG + 1], 0.5, None, ALU.mult))
                vec(lambda e: e.tensor_scalar(VX[:, 3:5], VEC[:, V_MUR:V_MUK + 1], -1.0, 1.0, ALU.mult, ALU.add))
                op(ACTE, lambda e: e.activation(lam2[:, 0:1], VEC[:, V_LAM:V_LAM + 1], ACT.Exp, scale=-1.0),
                   [(s_w, 1)], s_lam)
                vec(lambda e: e.tensor_scalar(lam2[:, 1:2], lam2[:, 0:1], 1.0, None, ALU.add), [(s_lam, 0)])
                vec(lambda e: e.reciprocal(lam2[:, 2:3], lam2[:, 1:2]))
                vec(lambda e: e.tensor_scalar(lam2[:, 4:5], lam2[:, 2:3], 1e-8, None, ALU.add))
                lam_ready = n[0] - 1
                op(ACTE, lambda e: e.activation(lam2[:, 3:4], lam2[:, 4:5], ACT.Ln), [(s_dve, lam_ready)], s_lam)
                vec(lambda e: e.tensor_scalar(VX[:, 2:3], lam2[:, 3:4], 4.0, None, ALU.mult), [(s_lam, 1)])
                op(SP, lambda e: e.nop(), [(s_xnd, 3)])
            phase(phase0)

        with ExitStack() as ph:
            xs = [sb(ph, f"xs{b}", [P, 2, TILE], F32R) for b in range(2)]
            xns = [sb(ph, f"xns{b}", [P, P]) for b in range(2)]
            mx = [sb(ph, f"mx{b}", [P, G]) for b in range(2)]
            mr = [sb(ph, f"mr{b}", [P, G], F32R) for b in range(2)]
            mt = [sb(ph, f"mt{b}", [G, TILE], F32R) for b in range(2)]
            ed = [sb(ph, f"ed{b}", [P, HS]) for b in range(2)]
            ec = [sb(ph, f"ec{b}", [P, HS]) for b in range(2)]
            dd = [sb(ph, f"dd{b}", [P, HS]) for b in range(2)]
            cs = [sb(ph, f"cs{b}", [P, HS // 2]) for b in range(2)]
            zd = [sb(ph, f"zd{b}", [P, HN]) for b in range(2)]
            rz = [sb(ph, f"rz{b}", [P, HN]) for b in range(2)]
            lg = [psum(ph, f"lg{b}", [P, HS]) for b in range(2)]
            acc = [psum(ph, f"acc{k}", [P, BANK]) for k in range(2)]
            tr = [psum(ph, f"tr{b}", [G, TILE]) for b in range(2)]

            s_xs = [stage(f"p1_xs{b}", SP, 16) for b in range(2)]
            s_xns = [stage(f"p1_xns{b}", SP, 16) for b in range(2)]
            s_l = [stage(f"p1_logits{k}", PE) for k in range(2)]
            s_mx = stage("p1_max", DVE)
            s_mm = stage("p1_max_rounded", ACTE)
            s_tr = stage("p1_max_transposed", PE)
            s_mt = stage("p1_max_transposed_copied", ACTE)
            s_s1 = [stage(f"p1_shift1{k}", PE) for k in range(2)]
            s_ed = [stage(f"p1_exp_experts{k}", ACTE) for k in range(2)]
            s_s2 = [stage(f"p1_shift2{k}", PE) for k in range(2)]
            s_ec = [stage(f"p1_exp_slots{k}", ACTE) for k in range(2)]
            s_zd = stage("p1_expert_sum", DVE)
            s_rz = stage("p1_expert_sum_inverse", DVE)
            s_cs = stage("p1_slot_half_sum", POOL)
            s_sm = stage("p1_slot_shift_kept", ACTE)
            s_dd = [stage(f"p1_dispatch{k}", POOL) for k in range(2)]
            s_ss = stage("p1_slot_sum", DVE)
            s_xa = [stage(f"p1_x_tilde{k}", PE) for k in range(2)]
            s_ev = stage("p1_x_tilde_copied", ACTE)

            def by_parity(s, u, b):
                class Halved:
                    sem, credit = s[b].sem, 0
                    after = staticmethod(lambda _: (u - b) // 2 * 16 + 16 if isinstance(u, int)
                                         else (u - b) * 8 + 16)
                return (Halved, 0)

            def slot(op, h, u, v, first, last, u_ok=True, v_ok=True, w_ok=True, s_ok=True,
                     xs_ok=True):
                a = h * NT + u
                b, c = v, 1 - v
                half = h * HS

                if xs_ok:
                    op(SP, lambda e: e.dma_start(hi_f32(xs[c][:, :, :]), hi_f32(
                        XT[:, bass.ds(u + 1, 1), :, :].rearrange("q o a k -> q (o a) k"))),
                       [(s_l[1], a - 1)], s_xs[c])
                if v_ok:
                    op(SP, lambda e: e.dma_start(xns[c][:, :], XND[bass.ds((u - 1) * TILE, TILE), :]),
                       [(s_xa[1], a - 3)], s_xns[c])

                def logits(k):
                    cols = slice(half + k * BANK, half + (k + 1) * BANK)
                    out = lg[b][:, k * BANK:(k + 1) * BANK]
                    op(PE, lambda e: e.matmul(out, xs[b][:, 0, :], PHI[:, 0, cols], start=True, stop=False),
                       [by_parity(s_xs, a, b), (s_ec[k], a - 2)])
                    op(PE, lambda e: e.matmul(out, xs[b][:, 0, :], PHI[:, 1, cols], start=False, stop=False))
                    op(PE, lambda e: e.matmul(out, xs[b][:, 1, :], PHI[:, 0, cols], start=False, stop=True),
                       done=s_l[k])

                def shift(k, matrix, waits, done):
                    cols = slice(k * BANK, (k + 1) * BANK)
                    op(PE, lambda e: e.matmul(lg[c][:, cols], mt[c][:, :], matrix[:, cols], start=False, stop=True,
                                              skip_group_check=True), waits, done)

                def x_tilde(k):
                    cols = slice(k * BANK, (k + 1) * BANK)
                    op(PE, lambda e: e.matmul(acc[k][:, :], xns[b][:, :], dd[b][:, cols], start=first, stop=last,
                                              skip_group_check=True),
                       [by_parity(s_xns, a - 2, b), (s_dd[k], a - 2)] + ([(s_ev, 2 * h - 1)] if first else []),
                       s_xa[k])

                if u_ok:
                    logits(0)
                if v_ok:
                    op(PE, lambda e: e.matmul(tr[c][:, :], hi_f32(mr[c][:, :]), IDENT[:, :], start=True, stop=True),
                       [(s_mm, a - 1), (s_mt, a - 3)], s_tr)
                if u_ok:
                    logits(1)
                if v_ok:
                    shift(0, S1M, [(s_mt, a - 1)], s_s1[0])
                    shift(1, S1M, [], s_s1[1])
                if w_ok:
                    x_tilde(0)
                if v_ok:
                    shift(0, S2M, [(s_ed[0], a - 1)], s_s2[0])
                    shift(1, S2M, [(s_ed[1], a - 1)], s_s2[1])
                if w_ok:
                    x_tilde(1)

                if v_ok:
                    op(ACTE, lambda e: e.activation(mt[c][:, :], tr[c][:, :], ACT.Copy),
                       [(s_tr, a - 1), (s_s2[1], a - 3)], s_mt)
                    for k in range(2):
                        cols = slice(k * BANK, (k + 1) * BANK)
                        op(ACTE, lambda e, k=k, cols=cols: e.activation(ed[c][:, cols], lg[c][:, cols], ACT.Exp),
                           [(s_s1[k], a - 1), (s_dd[k], a - 3), (s_zd, a - 3)], s_ed[k])
                    for k in range(2):
                        cols = slice(k * BANK, (k + 1) * BANK)
                        op(ACTE, lambda e, k=k, cols=cols: e.activation(ec[c][:, cols], lg[c][:, cols], ACT.Exp),
                           [(s_s2[k], a - 1), (s_cs, 2 * (a - 3))], s_ec[k])

                if u_ok:
                    op(ACTE, lambda e: e.activation(mr[b][:, :], mx[b][:, :], ACT.Copy),
                       [(s_mx2, a), (s_mx, 2 * a + 1), (s_tr, a - 2), (s_sm, a - 2)], s_mm)
                    op(ACTE, lambda e: e.activation(
                        SM[:, h, bass.ds(u, 1), :].rearrange("q o p -> q (o p)"), hi_f32(mr[b][:, HN:G]), ACT.Copy),
                       [(s_mm, a)], s_sm)

                def bank_max(k):
                    op(DVE, lambda e: e.tensor_reduce(
                        mx[b][:, k * HN // 2:(k + 1) * HN // 2],
                        lg[b][:, k * BANK:(k + 1) * BANK].rearrange("q (n p) -> q n p", p=NP), AX_X, ALU.max),
                       [(s_l[k], a), (s_mm, a - 2)], s_mx)
                if u_ok:
                    bank_max(0)
                if s_ok:
                    op(DVE, lambda e: e.tensor_reduce(
                        SS[:, h, bass.ds(u - 3, 1), :].rearrange("q o p -> q (o p)"),
                        cs[c][:, 0:BANK // 2].rearrange("q (n p) -> q p n", p=NP), AX_X, ALU.add),
                       [(s_cs, 2 * (a - 3) + 1)], s_ss)
                if u_ok:
                    bank_max(1)
                    op(DVE, lambda e: e.tensor_reduce(
                        mx[b][:, HN:G], lg[b][:, :].rearrange("q (n p) -> q p n", p=NP), AX_X, ALU.max), [], s_mx2)
                if v_ok:
                    op(DVE, lambda e: e.tensor_reduce(
                        zd[c][:, :], ed[c][:, :].rearrange("q (n p) -> q n p", p=NP), AX_X, ALU.add),
                       [(s_ed[0], a - 1), (s_ed[1], a - 1)], s_zd)
                    op(DVE, lambda e: e.reciprocal(rz[c][:, :], zd[c][:, :]),
                       [(s_zd, a - 1), (s_dd[1], a - 3)], s_rz)

                if v_ok:
                    for k in range(2):
                        cols = slice(k * BANK, (k + 1) * BANK)
                        op(POOL, lambda e, k=k, cols=cols: e.tensor_tensor(
                            dd[c][:, cols].rearrange("q (n p) -> q n p", p=NP),
                            ed[c][:, cols].rearrange("q (n p) -> q n p", p=NP),
                            rz[c][:, k * HN // 2:(k + 1) * HN // 2].unsqueeze(2).broadcast_to([P, HN // 2, NP]),
                            ALU.mult), [(s_rz, a - 1), (s_xa[k], a - 3)], s_dd[k])
                    op(POOL, lambda e: e.tensor_tensor(cs[c][:, :], ec[c][:, 0:BANK], ec[c][:, BANK:HS], ALU.add),
                       [(s_ec[0], a - 1), (s_ec[1], a - 1), (s_ss, a - 3)], s_cs)
                    op(POOL, lambda e: e.tensor_tensor(cs[c][:, 0:BANK // 2], cs[c][:, 0:BANK // 2],
                                                       cs[c][:, BANK // 2:BANK], ALU.add),
                       [(s_cs, 2 * (a - 1))], s_cs)

            s_mx2 = stage("p1_slot_max", DVE)

            UNROLL = 4

            def phase1(op, eng):
                for h in range(HALVES):
                    op(SP, lambda e: e.dma_start(hi_f32(xs[0][:, :, :]), hi_f32(XT[:, 0, :, :])),
                       [(s_l[1], h * NT - 2)], s_xs[0])
                    for u in range(4):
                        slot(op, h, u, u % 2, u == 2, False, v_ok=u >= 1, w_ok=u >= 2, s_ok=u >= 3)
                    with eng.Fori(4, NT - 4, UNROLL) as u:
                        for v in range(UNROLL):
                            slot(op, h, u + v, v % 2, False, False)
                    for u in range(NT - 4, NT + 3):
                        slot(op, h, u, u % 2, False, u == NT + 1, u_ok=u < NT, v_ok=u <= NT, w_ok=u <= NT + 1,
                             xs_ok=u < NT - 1)
                    for k in range(2):
                        op(ACTE, lambda e, k=k, h=h: e.activation(
                            XTT[:, h * HS + k * BANK:h * HS + (k + 1) * BANK], acc[k][:, :], ACT.Copy),
                           [(s_xa[k], (h + 1) * NT - 1)], s_ev)
            phase(phase1)
        front.close()

        with ExitStack() as ph:
            W2 = NT * NP
            m0, m1 = (SM[:, h, :, :].rearrange("q t p -> q (t p)") for h in range(2))
            z0, z1 = (SS[:, h, :, :].rearrange("q t p -> q (t p)") for h in range(2))
            mj = sb(ph, "m_joined", [P, W2])
            l3 = SM[:, :, :, :].rearrange("q h t p -> q (h t p)").bitcast(BF16)[:, 0:NT * 3 * NP]\
                .rearrange("q (t a p) -> q t a p", a=3, p=NP)
            EG = 8
            ew = [sb(ph, f"expert_w{k}", [P, EG, P]) for k in range(2)]
            eb = sb(ph, "expert_b", [P, CH, P])
            xc = sb(ph, "xc", [P, SLOTS])
            sq = sb(ph, "sq", [P, SLOTS])
            yf = sq[:, :].rearrange("q (c h) -> q c h", h=P)
            pm = [psum(ph, f"pm{k}", [P, BANK]) for k in range(4)]
            py = [psum(ph, f"py{k}", [P, BANK]) for k in range(2)]
            pt = [psum(ph, f"pt{k}", [3 * NP, 8, TILE], BF16) for k in range(2)]
            s_ew = stage("pb_expert_b", SP, 16)
            s_ewg = [stage(f"pb_expert_w{k}", SP, 16) for k in range(2)]
            s_v = stage("pb_vector", DVE)
            s_a = stage("pb_scalar", ACTE)
            s_p = stage("pb_tensor", PE)
            s_lt = stage("pb_lse_transposed", PE)
            s_lc = stage("pb_lse_copied", ACTE)

            def phase1b(op, eng):
                nv, na, npe = [0], [0], [0]

                def vec(make, waits=()):
                    op(DVE, make, waits, s_v)
                    nv[0] += 1
                    return (s_v, nv[0] - 1)

                def act(make, waits=()):
                    op(ACTE, make, waits, s_a)
                    na[0] += 1
                    return (s_a, na[0] - 1)

                def pe(make, waits=()):
                    op(PE, make, waits, s_p)
                    npe[0] += 1
                    return (s_p, npe[0] - 1)

                def load_experts(g):
                    op(SP, lambda e: e.dma_start(ew[g % 2][:, :, :], t["expert_w"][:, g * EG:(g + 1) * EG, :]),
                       [ys[(g - 1) * EG // EPC - 1]] if g >= 2 else (), s_ewg[g % 2])
                for g in range(2):
                    load_experts(g)
                for j in range(EPC):
                    op(SP, lambda e, j=j: e.dma_start(
                        eb[j * NP:(j + 1) * NP, :, :],
                        t["expert_b"].rearrange("(c j) h -> j c h", j=EPC)[j:j + 1, :, :].broadcast_to([NP, CH, P])),
                       done=s_ew)
                quarter = [slice(q * BANK, (q + 1) * BANK) for q in range(4)]
                ys = {}
                clip, mean, cen, squ, var, ln, rs, hat, th = ({} for _ in range(9))
                for q, cols in enumerate(quarter):
                    clip[q] = vec(lambda e, cols=cols: e.tensor_scalar(XTT[:, cols], XTT[:, cols], -33000.0, 65000.0,
                                                                       ALU.max, ALU.min))
                for q, cols in enumerate(quarter):
                    mean[q] = pe(lambda e, cols=cols, q=q: e.matmul(pm[q][:, :], MEAN[:, :], XTT[:, cols],
                                                                    start=True, stop=True), [clip[q]])
                for q, cols in enumerate(quarter):
                    cen[q] = vec(lambda e, cols=cols, q=q: e.tensor_tensor(xc[:, cols], XTT[:, cols], pm[q][:, :],
                                                                           ALU.subtract), [mean[q]])
                    squ[q] = act(lambda e, cols=cols: e.activation(sq[:, cols], xc[:, cols], ACT.Square), [cen[q]])
                for q, cols in enumerate(quarter):
                    var[q] = pe(lambda e, cols=cols, q=q: e.matmul(pm[q][:, :], MEAN[:, :], sq[:, cols],
                                                                   start=True, stop=True), [squ[q]])
                jm = vec(lambda e: e.tensor_tensor(mj[:, :], m0, m1, ALU.max))
                d0 = vec(lambda e: e.tensor_tensor(m0, m0, mj[:, :], ALU.subtract), [jm])
                d1 = vec(lambda e: e.tensor_tensor(m1, m1, mj[:, :], ALU.subtract), [jm])
                e0 = act(lambda e: e.activation(m0, m0, ACT.Exp), [d0])
                e1 = act(lambda e: e.activation(m1, m1, ACT.Exp), [d1])
                for q, cols in enumerate(quarter):
                    ln[q] = act(lambda e, cols=cols, q=q: e.activation(sq[:, cols], pm[q][:, :], ACT.Ln,
                                                                       bias=EPS[:, 0:1]), [var[q]])
                for q, cols in enumerate(quarter):
                    rs[q] = act(lambda e, cols=cols: e.activation(sq[:, cols], sq[:, cols], ACT.Exp, scale=-0.5),
                                [ln[q]])
                p0 = vec(lambda e: e.tensor_tensor(z0, z0, m0, ALU.mult), [e0])
                p1 = vec(lambda e: e.tensor_tensor(z1, z1, m1, ALU.mult), [e1])
                js = vec(lambda e: e.tensor_tensor(z0, z0, z1, ALU.add), [p0, p1])
                jl = act(lambda e: e.activation(z1, z0, ACT.Ln), [js])
                for q, cols in enumerate(quarter):
                    hat[q] = vec(lambda e, cols=cols: e.tensor_tensor(xc[:, cols], xc[:, cols], sq[:, cols], ALU.mult),
                                 [rs[q]])
                for q, cols in enumerate(quarter):
                    th[q] = act(lambda e, cols=cols: e.activation(XTT[:, cols], xc[:, cols], ACT.Tanh), [hat[q]])
                lse = vec(lambda e: e.tensor_tensor(mj[:, :], mj[:, :], z1, ALU.add), [jl])
                tp3 = mj[:, :].rearrange("q (t p) -> q t p", p=NP)
                r3 = z0.rearrange("q (t p) -> q t p", p=NP)
                l_hi = vec(lambda e: e.tensor_copy(l3[:, :, 0, :], tp3), [lse])
                l_r = vec(lambda e: e.tensor_tensor(r3, tp3, l3[:, :, 0, :], ALU.subtract), [l_hi])
                l_mid = vec(lambda e: e.tensor_copy(l3[:, :, 1, :], r3), [l_r])
                l_lo = vec(lambda e: e.tensor_tensor(l3[:, :, 2, :], r3, l3[:, :, 1, :], ALU.subtract), [l_mid])
                for c in range(CH):
                    for j in range(EPC):
                        n = c * EPC + j
                        op(PE, lambda e, c=c, j=j, n=n: e.matmul(
                            py[c % 2][j * NP:(j + 1) * NP, 0:P], XTT[:, n * NP:(n + 1) * NP], ew[n // EG % 2][:, n % EG, :],
                            start=True, stop=True),
                           [(s_ewg[n // EG % 2], n // EG // 2), th[c * P // BANK]] + ([ys[c - 2]] if c >= 2 else [])
                           if j == 0 else (), s_p if j == EPC - 1 else None)
                    npe[0] += 1
                    yp = (s_p, npe[0] - 1)
                    ys[c] = vec(lambda e, c=c: e.tensor_tensor(yf[:, c, :], py[c % 2][:, 0:P], eb[:, c, :], ALU.add),
                                [yp, (s_ew, EPC - 1)])
                    if (c + 1) % (EG // EPC) == 0 and (c + 1) // (EG // EPC) + 1 < NEXP // EG:
                        load_experts((c + 1) // (EG // EPC) + 1)
                quads = [slice(c, c + 4) for c in range(0, CH, 4)]
                for n, cc in enumerate(quads):
                    yh = act(lambda e, cc=cc: e.activation(YHI[:, cc, :], yf[:, cc, :], ACT.Copy), [ys[cc.stop - 1]])
                    vec(lambda e, cc=cc: e.tensor_tensor(YLO[:, cc, :], yf[:, cc, :], hi_f32(YHI[:, cc, :]),
                                                         ALU.subtract), [yh])
                for g in range(NT // 8):
                    for k in range(8):
                        op(PE, lambda e, g=g, k=k: e.transpose(
                            pt[g % 2][:, k, :], l3[:, 8 * g + k, :, :].rearrange("q a p -> q (a p)"), IDENTB[:, :]),
                           [l_lo, (s_lc, g - 2)] if k == 0 else (), s_lt if k == 7 else None)
                    op(ACTE, lambda e, g=g: e.activation(
                        LSE[:, g * 8 * TILE:(g + 1) * 8 * TILE].rearrange("r (k n) -> r k n", n=TILE),
                        pt[g % 2][:, :, :], ACT.Copy), [(s_lt, g)], s_lc)
            phase(phase1b)
        both.close()

        with ExitStack() as ph:
            LAG = 3
            RC = 4
            cf = [sb(ph, f"cf{k}", [P, SEQ]) for k in range(2)]
            chi = [sb(ph, f"chi{k}", [P, SEQ], F32R) for k in range(RC)]
            clo = [sb(ph, f"clo{k}", [P, SEQ], F32R) for k in range(RC)]
            yt = sb(ph, "yt", [P, SEQ])
            names = ("qf", "e0", "e1", "e2", "e3", "st", "xraw", "ty", "x1", "xc", "x1k",
                     "ti", "tg", "aa", "a2", "hh", "xr", "xk", "kr", "f1")
            B = {n: sb(ph, "b_" + n, [P, SEQ]) for n in names}
            XP = sb(ph, "xn1", [P, SEQ + 1])
            R = {n: sb(ph, "r_" + n, [P, SEQ], F32R) for n in ("qh", "ql", "vh", "vl", "xh", "xl")}
            pth = [sb(ph, f"pth{k}", [P, SEQ], F32R) for k in range(2)]
            ptl = [sb(ph, f"ptl{k}", [P, SEQ], F32R) for k in range(2)]
            nmx = sb(ph, "nmx", [P, 4 * TPB])

            lgp = [psum(ph, f"lgp{k}", [P, SEQ]) for k in range(2)]
            yac = psum(ph, "yac", [P, SEQ])
            at = [psum(ph, f"at{k}", [P, SEQ]) for k in range(2)]
            lp = [psum(ph, f"lp{k}", [P, SEQ]) for k in range(3)]

            c_l = stage("c_logits", PE)
            c_e = stage("c_exp", ACTE)
            c_h = stage("c_high", DVE)
            c_s = stage("c_low", POOL)
            c_y = stage("c_y", PE)
            side = []

            def once(name, producer, inc=1, credit=1):
                s = stage(name, producer, inc, credit)
                side.append(s)
                return s
            y_c = once("y_copied", ACTE)
            ALL = dict(
                q_p=PE, q_f=ACTE, q_h=DVE, q_l=DVE, v_p=PE, v_h=ACTE, v_l=DVE,
                o_c=ACTE,
                xr_dma=SP, out_dma=SP,
                t_y=ACTE, u_y=DVE, us=POOL, res=DVE, x1k=ACTE, mn=PE, xc=DVE, sq=ACTE, vr=PE, ln=ACTE, rs=ACTE, xn=DVE,
                xh=DVE, xl=DVE, p_r=PE, p_i=PE, p_x=PE, t_r=ACTE, t_i=ACTE, a=ACTE, ix=DVE, a2=ACTE, om=DVE,
                sl=ACTE, sr=ACTE, gt=DVE, hh=DVE, hq=ACTE, hm=PE, hl=ACTE, hr=ACTE, po=PE, o1=DVE,
                wr=POOL, wk=POOL, xr=DVE, xk=DVE, pr=PE, pk=PE, tr2=ACTE, kr=ACTE, ka=ACTE, pv=PE, f1=DVE,
                tf=ACTE, f2=DVE, f3=DVE, f4=DVE)
            FOUR = dict(s=PE, m=DVE, n=DVE, x=ACTE, z=DVE, p=DVE, w=PE, k=PE, kh=ACTE, kl=DVE)
            S4 = {n: stage("a_" + n, who) for n, who in FOUR.items()}
            S = {n: once("b_" + n, who, credit=16 if who == SP else 1, inc=16 if who == SP else 1)
                 for n, who in ALL.items()}

            def tiles_of(i, part):
                return XT[:, bass.ds(i * TPB, TPB), part, :]

            def chunk_logits(op, i, c):
                g = i * CH + c
                cols = slice(c * P, (c + 1) * P)
                out = lgp[c % 2][:, :]
                op(PE, lambda e: e.matmul(out, MINUS_P[:, :], LSE[:, bass.ds(i * SEQ, SEQ)], start=True, stop=False),
                   [(c_e, g - 2)])
                op(PE, lambda e: e.matmul(out, PHI[:, 0, cols], tiles_of(i, 0), start=False, stop=False))
                op(PE, lambda e: e.matmul(out, PHI[:, 0, cols], tiles_of(i, 1), start=False, stop=False))
                op(PE, lambda e: e.matmul(out, PHI[:, 1, cols], tiles_of(i, 0), start=False, stop=True), done=c_l)
                op(ACTE, lambda e: e.activation(cf[c % 2][:, :], out, ACT.Exp),
                   [(c_l, g), (c_s, g - 2)], c_e)
                op(DVE, lambda e: e.tensor_copy(chi[c % RC][:, :], cf[c % 2][:, :]),
                   [(c_e, g), (c_y, g - RC)], c_h)
                op(POOL, lambda e: e.tensor_tensor(clo[c % RC][:, :], cf[c % 2][:, :], hi_f32(chi[c % RC][:, :]),
                                                  ALU.subtract), [(c_h, g)], c_s)

            def chunk_y(op, i, c):
                g = i * CH + c
                op(PE, lambda e: e.matmul(yac[:, :], YHI[:, c, :], chi[c % RC][:, :], start=c == 0, stop=False),
                   [(c_h, g)] + ([(y_c, i - 1)] if c == 0 else []))
                op(PE, lambda e: e.matmul(yac[:, :], YLO[:, c, :], chi[c % RC][:, :], start=False, stop=False))
                op(PE, lambda e: e.matmul(yac[:, :], YHI[:, c, :], clo[c % RC][:, :], start=False, stop=c == CH - 1),
                   [(c_s, g)], c_y)

            def three(op, out, w, hi, lo, waits, done):
                op(PE, lambda e: e.matmul(out, WHI[:, w, :], hi(), start=True, stop=False), waits)
                op(PE, lambda e: e.matmul(out, WHI[:, w, :], lo(), start=False, stop=False))
                op(PE, lambda e: e.matmul(out, WLO[:, w, :], hi(), start=False, stop=True), done=done)

            def attention(op, i):
                j = lambda n, back=0: (S[n], i - back)
                q = lambda n, k, back=0: (S4[n], (i - back) * TPB + k)
                scale = float(P) ** -0.5
                steps = {}

                def project():
                    three(op, at[0][:, :], W_Q, lambda: tiles_of(i, 0), lambda: tiles_of(i, 1), [j("o_c", 1)], S["q_p"])
                    op(ACTE, lambda e: e.activation(B["qf"][:, :], at[0][:, :], ACT.Identity,
                                                    bias=VEC[:, V_BQ:V_BQ + 1]), [j("q_p"), j("v_p", 1)], S["q_f"])

                def project_split():
                    op(DVE, lambda e: e.tensor_copy(R["qh"][:, :], B["qf"][:, :]), [j("q_f"), q("s", TPB-1, 1)], S["q_h"])
                    op(DVE, lambda e: e.tensor_tensor(R["ql"][:, :], B["qf"][:, :], hi_f32(R["qh"][:, :]),
                                                      ALU.subtract), [j("q_h")], S["q_l"])

                def values():
                    for k in range(TPB):
                        cols = slice(k * TILE, (k + 1) * TILE)
                        op(PE, lambda e, cols=cols: e.transpose(at[1][:, cols], B["qf"][:, cols], IDENT[:, :]),
                           [j("q_f"), q("kl", TPB-1, 1)] if k == 0 else (), S["v_p"] if k == TPB - 1 else None)

                def values_split():
                    op(ACTE, lambda e: e.activation(R["vh"][:, :], at[1][:, :], ACT.Copy), [j("v_p"), q("w", TPB-1, 1)], S["v_h"])
                    op(DVE, lambda e: e.tensor_tensor(R["vl"][:, :], at[1][:, :], hi_f32(R["vh"][:, :]), ALU.subtract),
                       [j("v_h")], S["v_l"])
                steps.update(project=project, project_split=project_split, values=values, values_split=values_split)

                def block(r):
                    rows = slice(r * TILE, (r + 1) * TILE)
                    bank = at[r % 2][:, :]
                    free = [j("q_f"), j("v_l"), q("x", 0), q("x", 1)]
                    m, nm, z, rz_ = (nmx[:, 4 * r + k:4 * r + k + 1] for k in range(4))
                    E = B[f"e{r}"][:, :]

                    def scores():
                        op(PE, lambda e: e.matmul(bank, R["qh"][:, rows], R["qh"][:, :], start=True, stop=False),
                           [j("q_h"), free[r]])
                        op(PE, lambda e: e.matmul(bank, R["qh"][:, rows], R["ql"][:, :], start=False, stop=False),
                           [j("q_l")])
                        op(PE, lambda e: e.matmul(bank, R["ql"][:, rows], R["qh"][:, :], start=False, stop=True),
                           done=S4["s"])
                        op(DVE, lambda e: e.tensor_reduce(m, bank, AX_X, ALU.max), [q("s", r)], S4["m"])
                        op(DVE, lambda e: e.tensor_scalar(nm, m, -scale, None, ALU.mult), [q("m", r), q("x", r, 1)],
                           S4["n"])

                    def exponential():
                        op(ACTE, lambda e: e.activation(E, bank, ACT.Exp, bias=nm, scale=scale, accum_out=z),
                           [q("n", r), q("k", TPB-1, 1), q("z", r, 1)], S4["x"])

                    def weights():
                        op(DVE, lambda e: e.reciprocal(rz_, z), [q("x", r), q("p", r, 1)], S4["z"])
                        op(DVE, lambda e: e.tensor_scalar(E, E, rz_, None, ALU.mult), [q("z", r)], S4["p"])

                    k = r
                    keys = rows

                    def turn():
                        for r in range(TPB):
                            op(PE, lambda e, r=r: e.transpose(at[1][:, r * TILE:(r + 1) * TILE], B[f"e{r}"][:, keys],
                                                              IDENT[:, :]),
                               [q("p", r)] + ([q("x", 3) if k == 0 else q("kl", k - 1)] if r == 0 else []),
                               S4["k"] if r == TPB - 1 else None)

                    def turn_split():
                        op(ACTE, lambda e: e.activation(pth[k % 2][:, :], at[1][:, :], ACT.Copy),
                           [q("k", k), q("w", k-2) if k >= 2 else q("w", k+2, 1)], S4["kh"])
                        op(DVE, lambda e: e.tensor_tensor(ptl[k % 2][:, :], at[1][:, :], hi_f32(pth[k % 2][:, :]),
                                                          ALU.subtract), [q("kh", k)], S4["kl"])

                    def weigh():
                        for n, (v, pt_, after) in enumerate(((R["vh"], pth, "kh"), (R["vl"], pth, "kh"),
                                                             (R["vh"], ptl, "kl"))):
                            op(PE, lambda e, v=v, pt_=pt_, n=n: e.matmul(
                                at[0][:, :], v[:, keys], pt_[k % 2][:, :], start=k == 0 and n == 0,
                                stop=k == TPB - 1 and n == 2),
                               [q(after, k)] + ([j("v_l"), q("x", 2)] if k == 0 and n == 0 else []),
                               S4["w"] if n == 2 else None)
                    steps.update({f"{f.__name__}{r}": f for f in (scores, exponential, weights, turn, turn_split, weigh)})
                for r in range(TPB):
                    block(r)

                def attended():
                    op(ACTE, lambda e: e.activation(B["st"][:, :], at[0][:, :], ACT.Copy),
                       [q("w", TPB-1), (S["us"], i - 1)], S["o_c"])
                steps.update(attended=attended)
                return steps

            def layer1(op, i):
                j = lambda n, back=0: (S[n], i - back)
                one = lambda v, k: v[:, k:k + 1]
                x_in = XP[:, 1:SEQ + 1]
                x_prev = XP[:, 0:SEQ]

                def tt(who, out, a, b, f, waits, done):
                    op(who, lambda e: e.tensor_tensor(out[:, :], a[:, :], b[:, :], f), waits, S[done])

                def af(out, in_, func, waits, done, **kw):
                    op(ACTE, lambda e: e.activation(out[:, :], in_[:, :], func, **kw), waits, S[done])

                def y_copy():
                    op(ACTE, lambda e: e.activation(yt[:, :], yac[:, :], ACT.Copy),
                       [(c_y, i * CH + CH - 1), j("u_y", 1)], y_c)
                    af(B["ty"], yt, ACT.Tanh, [(y_c, i), j("xn", 1)], "t_y", scale=0.5)

                def silu_y():
                    op(DVE, lambda e: e.scalar_tensor_tensor(B["ty"][:, :], B["ty"][:, :], 1.0, yt[:, :],
                                                             ALU.add, ALU.mult), [j("t_y")], S["u_y"])
                    tt(POOL, B["ty"], B["ty"], B["st"], ALU.mult, [j("u_y"), (S["o_c"], i)], "us")

                def residual():
                    op(SP, lambda e: e.dma_start(B["xraw"][:, :], t["xT"][:, bass.ds(i * SEQ, SEQ)]),
                       [j("res", 1)], S["xr_dma"])
                    op(DVE, lambda e: e.scalar_tensor_tensor(B["x1"][:, :], B["ty"][:, :], 0.5, B["xraw"][:, :],
                                                             ALU.mult, ALU.add),
                       [j("us"), j("xr_dma"), j("x1k", 1)], S["res"])

                def keep():
                    af(B["x1k"], B["x1"], ACT.Copy, [j("res"), j("f4", 1)], "x1k")

                def mean():
                    op(PE, lambda e: e.matmul(lp[0][:, :], MEAN[:, :], B["x1"][:, :], start=True, stop=True),
                       [j("res"), j("f1", 1)], S["mn"])
                    tt(DVE, B["xc"], B["x1"], lp[0], ALU.subtract, [j("mn"), j("xn", 1)], "xc")

                def squares():
                    af(B["ty"], B["xc"], ACT.Square, [j("xc")], "sq")

                def variance():
                    op(PE, lambda e: e.matmul(lp[1][:, :], MEAN[:, :], B["ty"][:, :], start=True, stop=True),
                       [j("sq"), j("ix", 1), j("hl", 1)], S["vr"])

                def deviation():
                    af(B["ty"], lp[1], ACT.Ln, [j("vr")], "ln", bias=one(EPS, 0))
                    af(B["ty"], B["ty"], ACT.Exp, [j("ln")], "rs", scale=-0.5)

                def normalise():
                    op(DVE, lambda e: e.tensor_tensor(x_in, B["xc"][:, :], B["ty"][:, :], ALU.mult),
                       [j("rs"), j("wk", 1)], S["xn"])

                def normalised_split():
                    op(DVE, lambda e: e.tensor_copy(R["xh"][:, :], x_in), [j("xn"), j("p_x", 1)], S["xh"])
                    op(DVE, lambda e: e.tensor_tensor(R["xl"][:, :], x_in, hi_f32(R["xh"][:, :]), ALU.subtract),
                       [j("xh")], S["xl"])

                hi, lo = (lambda: R["xh"][:, :]), (lambda: R["xl"][:, :])

                def decay_gate():
                    three(op, lp[2][:, :], W_RG, hi, lo, [j("xl"), j("o1", 1)], S["p_r"])

                def decay_tanh():
                    af(B["tg"], lp[2], ACT.Tanh, [j("p_r"), j("a", 1)], "t_r", scale=0.5, bias=one(VX, 1))

                def decay():
                    af(B["aa"], B["tg"], ACT.Exp, [j("t_r"), j("f4", 1)], "a", scale=one(VX, 2), bias=one(VX, 2))
                    af(B["a2"], B["aa"], ACT.Square, [j("a"), j("hm", 1)], "a2")

                def input_gate():
                    three(op, lp[0][:, :], W_IG, hi, lo, [j("xc")], S["p_i"])

                def input_tanh():
                    af(B["ti"], lp[0], ACT.Tanh, [j("p_i"), j("out_dma", 1)], "t_i", scale=0.5, bias=one(VX, 0))

                def input_product():
                    three(op, lp[1][:, :], W_IN, hi, lo, [j("ln")], S["p_x"])

                def gated():
                    op(DVE, lambda e: e.scalar_tensor_tensor(B["ti"][:, :], B["ti"][:, :], 1.0, lp[1][:, :],
                                                             ALU.add, ALU.mult), [j("t_i"), j("p_x")], S["ix"])
                    op(DVE, lambda e: e.tensor_scalar(B["a2"][:, :], B["a2"][:, :], -1.0, 1.0, ALU.mult, ALU.add),
                       [j("a2")], S["om"])

                def mix_previous():
                    for n, dst in ((0, "wr"), (1, "wk")):
                        op(POOL, lambda e, n=n: e.tensor_tensor(
                            B["xr" if n == 0 else "xk"][:, :], x_prev, one(VX, 3 + n).broadcast_to([P, SEQ]),
                            ALU.mult),
                           [j("xn"), j("tf" if n == 0 else "pk", 1), j("f2", 1)], S[dst])

                def mix():
                    for n, k, src, dst in ((0, V_MUR, "xr", "xr"), (1, V_MUK, "xk", "xk")):
                        op(DVE, lambda e, k=k, src=src, dst=dst: e.scalar_tensor_tensor(
                            B[dst][:, :], x_in, one(VEC, k), B[src][:, :], ALU.mult, ALU.add),
                           [j("wr" if n == 0 else "wk")], S[dst])

                def ffn_r():
                    op(PE, lambda e: e.matmul(lp[0][:, :], WRAW[:, W_R, :], B["xr"][:, :], start=True, stop=True),
                       [j("xr"), j("t_i")], S["pr"])

                def ffn_r_tanh():
                    af(B["f1"], lp[0], ACT.Tanh, [j("pr"), j("f4", 1)], "tr2", scale=0.5)

                def ffn_k():
                    op(PE, lambda e: e.matmul(lp[2][:, :], WRAW[:, W_K, :], B["xk"][:, :], start=True, stop=True),
                       [j("xk"), j("t_r")], S["pk"])

                def ffn_k_squared():
                    af(B["kr"], lp[2], ACT.Relu, [j("pk"), j("f2", 1)], "kr")
                    af(B["kr"], B["kr"], ACT.Square, [j("kr")], "ka")

                def ffn_v():
                    op(PE, lambda e: e.matmul(lp[0][:, :], WRAW[:, W_V, :], B["kr"][:, :], start=True, stop=True),
                       [j("ka"), j("tr2")], S["pv"])

                def ffn():
                    op(DVE, lambda e: e.scalar_tensor_tensor(B["kr"][:, :], B["f1"][:, :], 1.0, lp[0][:, :],
                                                             ALU.add, ALU.mult), [j("pv"), j("ka")], S["f1"])

                def ffn_tanh():
                    af(B["xr"], B["kr"], ACT.Tanh, [j("f1"), j("pr")], "tf", scale=0.25)

                def ffn_silu():
                    op(DVE, lambda e: e.scalar_tensor_tensor(B["f1"][:, :], B["xr"][:, :], 1.0, B["kr"][:, :],
                                                             ALU.add, ALU.mult), [j("tf")], S["f2"])

                def input_scale():
                    af(B["a2"], B["a2"], ACT.Ln, [j("om")], "sl", bias=one(EPS, 1))
                    af(B["a2"], B["a2"], ACT.Exp, [j("sl")], "sr", scale=0.5)

                def scan():
                    op(DVE, lambda e: e.scalar_tensor_tensor(B["ti"][:, :], B["ti"][:, :], 0.5, B["a2"][:, :],
                                                             ALU.mult, ALU.mult), [j("sr"), j("ix")], S["gt"])
                    op(DVE, lambda e: e.tensor_tensor_scan(B["hh"][:, :], B["aa"][:, :], B["ti"][:, :],
                                                           one(VEC, V_H0), ALU.mult, ALU.add),
                       [j("gt"), j("a"), j("po", 1)], S["hh"])

                def state_squares():
                    af(B["a2"], B["hh"], ACT.Square, [j("hh")], "hq")

                def state_out():
                    op(PE, lambda e: e.matmul(lp[2][:, :], WRAW[:, W_OUT, :], B["hh"][:, :], start=True, stop=True),
                       [j("hh"), j("kr")], S["po"])

                def state_mean():
                    op(PE, lambda e: e.matmul(lp[1][:, :], MEAN[:, :], B["a2"][:, :], start=True, stop=True),
                       [j("hq"), j("ix")], S["hm"])

                def state_norm():
                    af(B["aa"], lp[1], ACT.Ln, [j("hm")], "hl", bias=one(EPS, 1))
                    af(B["aa"], B["aa"], ACT.Exp, [j("hl")], "hr", scale=-0.5)

                def output():
                    op(DVE, lambda e: e.tensor_tensor(B["aa"][:, :], lp[2][:, :], B["aa"][:, :], ALU.mult),
                       [j("po"), j("hr")], S["o1"])
                    op(DVE, lambda e: e.scalar_tensor_tensor(B["aa"][:, :], B["f1"][:, :], 0.25, B["aa"][:, :],
                                                             ALU.mult, ALU.mult), [j("o1"), j("f2")], S["f3"])
                    op(DVE, lambda e: e.tensor_tensor(B["ti"][:, :], B["aa"][:, :], B["x1k"][:, :], ALU.add),
                       [j("f3"), j("x1k")], S["f4"])
                    op(SP, lambda e: e.dma_start(t["out"][:, bass.ds(i * SEQ, SEQ)], B["ti"][:, :]),
                       [j("f4")], S["out_dma"])

                def table_tanh():
                    op(ACTE, lambda e: e.preload_act_table_set("exp_and_others"))

                def table_ln():
                    op(ACTE, lambda e: e.preload_act_table_set("natural_log_exp_and_others"))

                return {f.__name__: f for f in (
                    y_copy, silu_y, residual, keep, mean, squares, variance, deviation, normalise, normalised_split,
                    decay_gate, decay_tanh, decay, input_gate, input_tanh, input_product, gated, mix_previous, mix,
                    ffn_r, ffn_r_tanh, ffn_k, ffn_k_squared, ffn_v, ffn, ffn_tanh, ffn_silu, input_scale, scan,
                    state_squares, state_out, state_mean, state_norm, output, table_tanh, table_ln)}

            BEFORE, AFTER = False, True
            SCHEDULE = [
                (0, 0, AFTER, "project"),
                (0, 1, BEFORE, "project_split"),
                (0, 1, AFTER, "values"),
                (0, 2, BEFORE, "values_split"),
                (0, 2, AFTER, "scores0"),
                (0, 3, AFTER, "exponential0"),
                (0, 4, BEFORE, "weights0"),
                (0, 3, AFTER, "scores1"),
                (0, 4, AFTER, "exponential1"),
                (0, 5, BEFORE, "weights1"),
                (0, 4, AFTER, "scores2"),
                (0, 5, AFTER, "exponential2"),
                (0, 6, BEFORE, "weights2"),
                (0, 5, AFTER, "scores3"),
                (0, 6, AFTER, "exponential3"),
                (0, 7, BEFORE, "weights3"),
                (0, 8, AFTER, "turn0"),
                (0, 9, BEFORE, "turn_split0"),
                (0, 9, AFTER, "weigh0"),
                (0, 10, AFTER, "turn1"),
                (0, 11, BEFORE, "turn_split1"),
                (0, 11, AFTER, "weigh1"),
                (0, 12, AFTER, "turn2"),
                (0, 13, BEFORE, "turn_split2"),
                (0, 13, AFTER, "weigh2"),
                (0, 14, AFTER, "turn3"),
                (0, 15, BEFORE, "turn_split3"),
                (0, 15, AFTER, "weigh3"),
                (1, 0, BEFORE, "attended"),
                (1, 2, AFTER, "y_copy"),
                (1, 2, AFTER, "table_ln"),
                (1, 3, BEFORE, "silu_y"),
                (1, 4, AFTER, "residual"),
                (1, 6, AFTER, "mean"),
                (1, 7, BEFORE, "squares"),
                (1, 7, AFTER, "variance"),
                (1, 8, BEFORE, "deviation"),
                (1, 8, AFTER, "normalise"),
                (1, 8, AFTER, "table_tanh"),
                (1, 9, BEFORE, "normalised_split"),
                (1, 9, BEFORE, "mix_previous"),
                (1, 9, AFTER, "decay_gate"),
                (1, 10, BEFORE, "decay_tanh"),
                (1, 10, BEFORE, "mix"),
                (1, 10, BEFORE, "keep"),
                (1, 10, AFTER, "decay"),
                (1, 10, AFTER, "input_gate"),
                (1, 11, BEFORE, "input_tanh"),
                (1, 11, AFTER, "input_product"),
                (1, 12, BEFORE, "gated"),
                (1, 12, AFTER, "ffn_r"),
                (1, 13, BEFORE, "ffn_r_tanh"),
                (1, 13, AFTER, "ffn_k"),
                (1, 14, BEFORE, "ffn_k_squared"),
                (1, 14, AFTER, "ffn_v"),
                (1, 15, BEFORE, "ffn"),
                (1, 15, AFTER, "ffn_tanh"),
                (2, 0, BEFORE, "ffn_silu"),
                (2, 3, BEFORE, "input_scale"),
                (2, 3, AFTER, "scan"),
                (2, 4, AFTER, "state_squares"),
                (2, 5, AFTER, "state_out"),
                (2, 5, AFTER, "state_mean"),
                (2, 6, BEFORE, "state_norm"),
                (2, 6, BEFORE, "output"),
            ]

            def iteration(op, i, lags=(0, 1, 2)):
                steps = {lag: {**attention(op, i - lag), **layer1(op, i - lag)} for lag in lags}

                def place(c, where):
                    for lag, chunk, side_, name in SCHEDULE:
                        if lag in lags and chunk == c and side_ == where:
                            steps[lag][name]()
                for c in range(CH):
                    place(c, BEFORE)
                    if 0 in lags:
                        chunk_logits(op, i, c)
                    if c >= LAG and 0 in lags:
                        chunk_y(op, i, c - LAG)
                    elif c < LAG and 1 in lags:
                        chunk_y(op, i - 1, CH - LAG + c)
                    place(c, AFTER)

            def phase2(op, eng):
                op(DVE, lambda e: e.memset(XP[:, 0:1], 0.0), done=s_zero)
                op(POOL, lambda e: e.nop(), [(s_zero, 0)])
                iteration(op, 0, (0,))
                iteration(op, 1, (0, 1))
                with eng.Fori(2, NB) as i:
                    iteration(op, i)
                iteration(op, NB, (1, 2))
                iteration(op, NB + 1, (2,))
                op(SP, lambda e: e.nop(), [(S["out_dma"], NB - 1)])
            s_zero = stage("zero_column", DVE)
            phase(phase2, side)


def kernel(**inputs):
    import concourse.bacc as bacc
    from concourse.bass_utils import run_bass_kernel_spmd

    a = {k: np.asarray(v) for k, v in inputs.items()}
    x = a["L0_attn_inputs"]
    tokens, d = x.shape[0] * x.shape[1], x.shape[2]
    x = x.reshape(tokens, d)
    vectors = [a["L0_attn_bq"], a["L1_attn_b_ig"], a["L1_attn_b_rg"], a["L1_attn_lam"],
               a["L1_attn_h0"].reshape(-1), a["L1_attn_norm_w"], a["L1_ffn_mu_r"], a["L1_ffn_mu_k"]]
    weights = [a["L0_attn_Wq"], a["L1_attn_W_in"].T, a["L1_attn_W_ig"].T, a["L1_attn_W_rg"].T,
               a["L1_attn_W_out"].T, a["L1_ffn_W_r"].T, a["L1_ffn_W_k"].T, a["L1_ffn_W_v"].T]
    arrays = {
        "x": x,
        "xT": x.T,
        "phiT": a["L0_ffn_phi_w"].T,
        "phi_b": a["L0_ffn_phi_b"].reshape(1, -1),
        "expert_w": a["L0_ffn_expert_w"].transpose(1, 0, 2),
        "expert_b": a["L0_ffn_expert_b"],
        "weights": np.stack(weights, axis=1),
        "vectors": np.stack(vectors, axis=1),
    }
    nc = bacc.Bacc("TRN2", target_bir_lowering=False, num_devices=1)
    feed, t = {}, {}
    for name, value in arrays.items():
        value = np.ascontiguousarray(value)
        feed[f"in_{name}"] = value
        t[name] = nc.dram_tensor(f"in_{name}", value.shape, mybir.dt.from_np(value.dtype), kind="ExternalInput").ap()
    t["out"] = nc.dram_tensor("out_t", (d, tokens), F32, kind="ExternalOutput").ap()
    build(nc, t)
    r = run_bass_kernel_spmd(nc, [feed], core_ids=[0])
    out = r.results[0]["out_t"]
    return np.ascontiguousarray(out.T).reshape(inputs["L0_attn_inputs"].shape)
```

```python
from contextlib import ExitStack

import concourse.bass as bass
import concourse.mybir as mybir
import numpy as np

F32 = mybir.dt.float32
F32R = mybir.dt.float32r
BF16 = mybir.dt.bfloat16
ALU = mybir.AluOpType
ACT = mybir.ActivationFunctionType
AX_X = mybir.AxisListType.X

P = 128
TILE = 128
BANK = 512
PE, ACTE, DVE, POOL, SP = "tensor", "scalar", "vector", "gpsimd", "sync"

V_BQ, V_BIG, V_BRG, V_LAM, V_H0, V_NORM, V_MUR, V_MUK = range(8)
W_Q, W_IN, W_IG, W_RG, W_OUT, W_R, W_K, W_V = range(8)


class Stage:

    def __init__(self, sem, producer, inc=1, credit=0):
        self.sem, self.producer, self.inc, self.credit = sem, producer, inc, credit

    def after(self, unit):
        return (unit + 1) * self.inc + self.credit


class Steps:

    def __init__(self, engine, name):
        self.engine, self.name = engine, name

    def __call__(self, who, make, waits=(), done=None):
        if who != self.name:
            return
        for stage, unit in waits:
            value = stage.after(unit)
            if isinstance(value, int) and value <= stage.credit:
                continue
            self.engine.wait_ge(stage.sem, value)
        instruction = make(self.engine)
        if done is not None:
            instruction.then_inc(done.sem, done.inc)


def build(nc, t):
    TOK = t["x"].shape[0]
    NT = TOK // TILE
    SLOTS = t["phiT"].shape[1]
    NEXP = t["expert_b"].shape[0]
    NP = SLOTS // NEXP
    HALVES = 2
    HS = SLOTS // HALVES
    HN = NEXP // HALVES
    SEQ = 512
    NB = TOK // SEQ
    TPB = SEQ // TILE
    CH = SLOTS // P
    EPC = P // NP
    G = 2 * NP
    assert HN == NP == 32 and HS == 2 * BANK and SEQ == BANK

    root = ExitStack()

    def sb(stack, name, shape, dt=F32):
        return stack.enter_context(nc.sbuf_tensor(name, shape, dt))

    def psum(stack, name, shape, dt=F32):
        return stack.enter_context(nc.psum_tensor(name, shape, dt))

    def stage(name, producer, inc=1, credit=0):
        return Stage(root.enter_context(nc.semaphore(name)), producer, inc, credit)

    def phase(program, stages=()):
        with nc.Block() as block:
            for name, part in ((SP, block.sync), (PE, block.tensor), (ACTE, block.scalar), (DVE, block.vector),
                               (POOL, block.gpsimd)):
                def engine_part(engine, name=name):
                    for s in stages:
                        if s.credit and s.producer == name:
                            engine.sem_inc(s.sem, s.credit)
                    program(Steps(engine, name), engine)
                part(engine_part)

    with root:
        XT = sb(root, "xn_transposed", [P, NT, 2, TILE], F32R)
        PHI = sb(root, "phi_transposed", [P, 2, SLOTS], F32R)
        LSE = sb(root, "lse_over_experts", [3 * NP, TOK], BF16)
        YHI = sb(root, "expert_out_high", [P, CH, P], F32R)
        YLO = sb(root, "expert_out_low", [P, CH, P], F32R)
        WRAW = sb(root, "weights", [P, 8, P])
        WHI = sb(root, "weights_high", [P, 4, P], F32R)
        WLO = sb(root, "weights_low", [P, 4, P], F32R)
        VEC = sb(root, "vectors", [P, 8])
        VX = sb(root, "derived_vectors", [P, 8])
        IDENT = sb(root, "identity", [P, P])
        IDENTB = sb(root, "identity_bf16", [P, P], BF16)
        MEAN = sb(root, "ones_over_width", [P, P])
        MINUS_P = sb(root, "minus_slot_pick", [3 * NP, P], BF16)
        EPS = sb(root, "epsilons", [P, 5])

        def hi_f32(ap):
            return ap.bitcast(F32)

        XND = nc.dram_tensor("xn_rows", (TOK, P), F32).ap()
        xnd = XND.rearrange("(n p) d -> p n d", p=P)
        STATS = nc.dram_tensor("slot_statistics", (P, 2, HALVES, NT, NP), F32).ap()
        s_store = stage("statistics_stored", SP, 16)
        s_join = stage("lse_step", "several")
        JOIN_STEPS = 13
        both = ExitStack()
        SM = sb(both, "slot_max", [P, HALVES, NT, NP])
        SS = sb(both, "slot_sum", [P, HALVES, NT, NP])
        XTT = sb(both, "x_tilde", [P, SLOTS])
        front = ExitStack()
        S1M = sb(front, "shift_experts", [G, HS], F32R)
        S2M = sb(front, "shift_experts_to_slots", [G, HS], F32R)
        with ExitStack() as ph:
            XN = [SM[:, :, :, :].rearrange("q h t p -> q (h t p)").rearrange("q (n d) -> q n d", d=P),
                  SS[:, :, :, :].rearrange("q h t p -> q (h t p)").rearrange("q (n d) -> q n d", d=P)]
            xn = lambda k: XN[k // (NT // 2)][:, k % (NT // 2), :]
            phi_raw = XTT
            brow = sb(ph, "bias_row", [1, SLOTS])
            bone = sb(ph, "bias_factor", [1, P])
            shifts = [sb(ph, f"shift_raw{k}", [G, HS]) for k in range(2)]
            stats = sb(ph, "stats", [P, NT, 6])
            mv = sb(ph, "mean_var", [P, NT, 2])
            std = sb(ph, "std", [P, NT])
            rstd = sb(ph, "rstd", [P, NT])
            nmr = sb(ph, "minus_mean_rstd", [P, NT])
            tp = [psum(ph, f"tp{k}", [P, BANK]) for k in range(3)]
            pc = [psum(ph, f"phi_mean{k}", [P, BANK]) for k in range(4)]
            wc = psum(ph, "wq_mean", [P, P])

            s_x = [stage(f"p0_x{k}", SP, 16) for k in range(4)]
            s_w = stage("p0_weights", SP, 16)
            s_b = stage("p0_bias", SP, 16)
            s_pc = stage("p0_phi_mean", PE)
            s_ps = stage("p0_phi_shifted", DVE)
            s_ph = stage("p0_phi_high", ACTE)
            s_pl = stage("p0_phi_low", POOL)
            s_phi = stage("p0_phi", SP, 16)
            s_xnd = [stage(f"p0_xn_stored{k}", SP, 16) for k in range(4)]
            s_id = stage("p0_identity", POOL)
            s_dve = stage("p0_vector", DVE)
            s_std = stage("p0_std", ACTE)
            s_bn = stage("p0_stats", DVE)
            s_nrm = stage("p0_normalised_vector", DVE)
            s_nra = stage("p0_normalised_scalar", ACTE)
            s_nrp = stage("p0_normalised_gpsimd", POOL)
            s_tp = stage("p0_transposed", PE)
            s_hi = stage("p0_high", ACTE)
            s_lo = stage("p0_low", DVE)
            QX = NT // 4

            def phase0(op, eng):
                for k in range(4):
                    op(SP, lambda e, k=k: e.dma_start(
                        XN[k // 2][:, k % 2 * QX:(k % 2 + 1) * QX, :],
                        t["x"].rearrange("(n p) d -> p n d", p=P)[:, k * QX:(k + 1) * QX, :]), done=s_x[k])
                op(ACTE, lambda e: e.dma_start(phi_raw[:, :], t["phiT"]), done=s_phi)
                op(ACTE, lambda e: e.dma_start(brow[:, :], t["phi_b"]), done=s_b)
                op(ACTE, lambda e: e.dma_start(WRAW[:, :, :], t["weights"]), done=s_w)
                op(ACTE, lambda e: e.dma_start(VEC[:, :], t["vectors"]), done=s_w)

                made = [0]

                def pattern(dst, fill, step):
                    op(POOL, lambda e: e.affine_select(out=dst, in_=dst, compare_op=ALU.not_equal, fill=fill,
                                                       base=0, pattern=step, channel_multiplier=1),
                       [(s_id, made[0] - 1)], s_id)
                    made[0] += 1
                for dst in (IDENT, IDENTB, *shifts, MINUS_P):
                    op(POOL, lambda e, dst=dst: e.memset(dst[:, :], 0.0), done=s_id)
                    made[0] += 1
                pattern(IDENT[:, :], 1.0, [[-1, P]])
                pattern(IDENTB[:, :], 1.0, [[-1, P]])
                for m, rows, fill, step in ((shifts[0], 0, -1.0, [[-1, HN], [0, NP]]),
                                            (shifts[1], 0, 1.0, [[-1, HN], [0, NP]]),
                                            (shifts[1], HN, -1.0, [[0, HN], [-1, NP]])):
                    pattern(m[rows:rows + 32, :].rearrange("r (n p) -> r n p", p=NP), fill, step)
                for part in range(3):
                    pattern(MINUS_P[part * NP:(part + 1) * NP, :].rearrange("r (j p) -> r j p", p=NP),
                            -1.0, [[0, EPC], [-1, NP]])

                n = [0]

                def vec(make, waits=(), chain=True):
                    op(DVE, make, list(waits) + ([(s_dve, n[0] - 1)] if chain and n[0] else []), s_dve)
                    n[0] += 1
                vec(lambda e: e.memset(MEAN[:, :], 1.0 / P), chain=False)
                vec(lambda e: e.memset(bone[:, :], -1.0 / P), chain=False)
                vec(lambda e: e.memset(EPS[:, 0:1], 1e-5), chain=False)
                vec(lambda e: e.memset(EPS[:, 1:2], 1e-6), chain=False)
                vec(lambda e: e.memset(EPS[:, 2:3], 1e-8), chain=False)
                vec(lambda e: e.memset(EPS[:, 3:4], 0.0), chain=False)
                vec(lambda e: e.memset(EPS[:, 4:5], 1.0), chain=False)
                eps_ready = n[0] - 1
                rstd_ready = [0] * 4

                def part(q):
                    return slice(q * QX, (q + 1) * QX)

                def statistics(q):
                    base = 2 * QX * q
                    for k in range(QX):
                        op(DVE, lambda e, k=k: e.bn_stats(stats[:, q * QX + k, :], xn(q * QX + k)), [(s_x[q], 0)], s_bn)
                    for k in range(QX):
                        op(DVE, lambda e, k=k: e.bn_aggr(mv[:, q * QX + k, :], stats[:, q * QX + k, :]),
                           [(s_bn, base + k)], s_bn)
                    op(ACTE, lambda e: e.activation(std[:, part(q)], mv[:, part(q), 1], ACT.Sqrt, bias=EPS[:, 0:1]),
                       [(s_bn, base + 2 * QX - 1), (s_dve, eps_ready)], s_std)

                def inverse(q):
                    vec(lambda e: e.reciprocal(rstd[:, part(q)], std[:, part(q)]), [(s_std, q)], chain=False)
                    vec(lambda e: e.scalar_tensor_tensor(nmr[:, part(q)], mv[:, part(q), 0], -1.0, rstd[:, part(q)],
                                                         ALU.mult, ALU.mult))
                    rstd_ready[q] = n[0] - 1

                def normalise(g):
                    ready = [(s_dve, rstd_ready[g // 4])]
                    for j in range(2):
                        k = g * TPB + j
                        op(DVE, lambda e, k=k: e.tensor_scalar(
                            xn(k), xn(k), mv[:, k, 0:1], rstd[:, k:k + 1], ALU.subtract, ALU.mult), ready, s_nrm)
                    k = g * TPB + 2
                    op(ACTE, lambda e, k=k: e.activation(
                        xn(k), xn(k), ACT.Identity, bias=nmr[:, k:k + 1], scale=rstd[:, k:k + 1]), ready, s_nra)
                    k = g * TPB + 3
                    op(POOL, lambda e, k=k: e.tensor_scalar(
                        xn(k), xn(k), mv[:, k, 0:1], rstd[:, k:k + 1], ALU.subtract, ALU.mult),
                       ready + [(s_id, made[0] - 1)], s_nrp)
                    for j in range(TPB):
                        k = g * TPB + j
                        op(PE, lambda e, k=k, j=j: e.transpose(
                            tp[g % 3][:, j * TILE:(j + 1) * TILE], xn(k), IDENT[:, :]),
                           [(s_nrm, 2 * g + j) if j < 2 else (s_nra if j == 2 else s_nrp, g), (s_id, 5),
                            (s_lo, g - 3)], s_tp)

                def split(g):
                    view = tp[g % 3][:, :].rearrange("p (n k) -> p n k", k=TILE)
                    tiles = slice(g * TPB, (g + 1) * TPB)
                    op(ACTE, lambda e: e.activation(XT[:, tiles, 0, :], view, ACT.Identity, bias=EPS[:, 4:5]),
                       [(s_tp, (g + 1) * TPB - 1)], s_hi)
                    op(DVE, lambda e: e.scalar_tensor_tensor(XT[:, tiles, 1, :], view, 1.0, hi_f32(XT[:, tiles, 0, :]),
                                                             ALU.add, ALU.subtract), [(s_hi, g)], s_lo)

                def phi_mean(k):
                    cols = slice(k * BANK, (k + 1) * BANK)
                    op(PE, lambda e: e.matmul(pc[k][:, :], MEAN[:, :], phi_raw[:, cols], start=True, stop=False),
                       [(s_phi, 0), (s_dve, 1)])
                    op(PE, lambda e: e.matmul(pc[k][:, :], bone[:, :], brow[:, cols], start=False, stop=True),
                       [(s_b, 0)], s_pc)

                def shift_phi(k):
                    cols = slice(k * BANK, (k + 1) * BANK)
                    op(DVE, lambda e: e.tensor_tensor(phi_raw[:, cols], phi_raw[:, cols], pc[k][:, :], ALU.subtract),
                       [(s_pc, k)], s_ps)
                    op(ACTE, lambda e: e.activation(PHI[:, 0, cols], phi_raw[:, cols], ACT.Copy), [(s_ps, k)], s_ph)
                    op(POOL, lambda e: e.tensor_tensor(PHI[:, 1, cols], phi_raw[:, cols], hi_f32(PHI[:, 0, cols]),
                                                       ALU.subtract), [(s_ph, k), (s_id, made[0] - 1)], s_pl)

                def query_mean():
                    op(PE, lambda e: e.matmul(wc[:, :], MEAN[:, :], WRAW[:, W_Q, :], start=True, stop=True),
                       [(s_w, 1)], s_pc)

                def shift_weights():
                    op(DVE, lambda e: e.tensor_tensor(WRAW[:, W_Q, :], WRAW[:, W_Q, :], wc[:, :], ALU.subtract),
                       [(s_pc, 4)], s_ps)
                    op(ACTE, lambda e: e.activation(WHI[:, :, :], WRAW[:, 0:4, :], ACT.Copy), [(s_ps, 4)], s_ph)
                    op(POOL, lambda e: e.tensor_tensor(WLO[:, :, :], WRAW[:, 0:4, :], hi_f32(WHI[:, :, :]),
                                                       ALU.subtract), [(s_ph, 4)], s_pl)

                between = {1: [lambda: phi_mean(3), query_mean],
                           5: [*[lambda k=k: shift_phi(k) for k in range(4)], shift_weights]}
                for k in range(3):
                    phi_mean(k)
                statistics(0)
                statistics(1)
                inverse(0)
                for raw, dst in zip(shifts, (S1M, S2M)):
                    vec(lambda e, raw=raw, dst=dst: e.tensor_copy(dst[:, :], raw[:, :]), [(s_id, made[0] - 1)])
                vec(lambda e: e.tensor_scalar(WRAW[:, W_OUT, :], WRAW[:, W_OUT, :], VEC[:, V_NORM:V_NORM + 1], None,
                                              ALU.mult), [(s_w, 1)])
                vec(lambda e: e.tensor_scalar(VX[:, 0:1], VEC[:, V_BIG:V_BIG + 1], 0.5, None, ALU.mult))
                vec(lambda e: e.tensor_scalar(VX[:, 1:2], VEC[:, V_BRG:V_BRG + 1], 0.5, None, ALU.mult))
                vec(lambda e: e.tensor_scalar(VX[:, 3:5], VEC[:, V_MUR:V_MUK + 1], -1.0, 1.0, ALU.mult, ALU.add))
                for g in range(NB + 2):
                    if g % 4 == 2 and g < 8:
                        statistics(g // 4 + 2)
                    if g % 4 == 3 and g < 12:
                        inverse(g // 4 + 1)
                    if g < NB:
                        normalise(g)
                    if g >= 2:
                        split(g - 2)
                    for piece in between.get(g, ()):
                        piece()
                for k in range(4):
                    op(SP, lambda e, k=k: e.dma_start(
                        xnd[:, k * QX:(k + 1) * QX, :], XN[k // 2][:, k % 2 * QX:(k % 2 + 1) * QX, :]),
                       [(s_nrm, (k + 1) * QX // 2 - 1), (s_nra, (k + 1) * QX // 4 - 1),
                        (s_nrp, (k + 1) * QX // 4 - 1)], s_xnd[k])

            phase(phase0)

        with ExitStack() as ph:
            xs = [sb(ph, f"xs{b}", [P, 2, TILE], F32R) for b in range(2)]
            xns = [sb(ph, f"xns{b}", [P, P]) for b in range(2)]
            mx = [sb(ph, f"mx{b}", [P, G]) for b in range(2)]
            mr = [sb(ph, f"mr{b}", [P, G], F32R) for b in range(2)]
            mt = [sb(ph, f"mt{b}", [G, TILE], F32R) for b in range(2)]
            ed = [sb(ph, f"ed{b}", [P, HS]) for b in range(2)]
            ec = [sb(ph, f"ec{b}", [P, HS]) for b in range(2)]
            dd = [sb(ph, f"dd{b}", [P, HS]) for b in range(2)]
            cs = [sb(ph, f"cs{b}", [P, HS // 2]) for b in range(2)]
            zd = [sb(ph, f"zd{b}", [P, HN]) for b in range(2)]
            rz = [sb(ph, f"rz{b}", [P, HN]) for b in range(2)]
            lg = [psum(ph, f"lg{b}", [P, HS]) for b in range(2)]
            acc = [psum(ph, f"acc{k}", [P, BANK]) for k in range(2)]
            tr = [psum(ph, f"tr{b}", [G, TILE]) for b in range(2)]

            s_xs = [stage(f"p1_xs{b}", SP, 16) for b in range(2)]
            s_xns = [stage(f"p1_xns{b}", SP, 16) for b in range(2)]
            s_l = [stage(f"p1_logits{k}", PE) for k in range(2)]
            s_mx = stage("p1_max", DVE)
            s_mm = stage("p1_max_rounded", ACTE)
            s_tr = stage("p1_max_transposed", PE)
            s_mt = stage("p1_max_transposed_copied", ACTE)
            s_s1 = [stage(f"p1_shift1{k}", PE) for k in range(2)]
            s_ed = [stage(f"p1_exp_experts{k}", ACTE) for k in range(2)]
            s_s2 = [stage(f"p1_shift2{k}", PE) for k in range(2)]
            s_ec = [stage(f"p1_exp_slots{k}", ACTE) for k in range(2)]
            s_zd = stage("p1_expert_sum", DVE)
            s_rz = stage("p1_expert_sum_inverse", DVE)
            s_cs = stage("p1_slot_half_sum", POOL)
            s_sm = stage("p1_slot_shift_kept", ACTE)
            s_dd = [stage(f"p1_dispatch{k}", POOL) for k in range(2)]
            s_ss = stage("p1_slot_sum", DVE)
            s_xa = [stage(f"p1_x_tilde{k}", PE) for k in range(2)]
            s_ev = stage("p1_x_tilde_copied", ACTE)

            def by_parity(s, u, b):
                class Halved:
                    sem, credit = s[b].sem, 0
                    after = staticmethod(lambda _: (u - b) // 2 * 16 + 16 if isinstance(u, int)
                                         else (u - b) * 8 + 16)
                return (Halved, 0)

            def loaded(s, h, u, b):
                return by_parity(s, u + h * (NT - 4) - 4, b)

            def slot(op, h, u, v, u_ok=True, v_ok=True, w_ok=True, s_ok=True, xs_ok=True):
                a = h * NT + u
                b, c = v, 1 - v

                def unit(back):
                    return divmod(a - back, NT) if isinstance(a, int) else (h, u - back)

                def at_first(number, stages):
                    return [(s, 0) for s in stages] if isinstance(a, int) and a == number else []

                if xs_ok and not (isinstance(u, int) and unit(-1)[1] < 4):
                    op(SP, lambda e: e.dma_start(hi_f32(xs[c][:, :, :]), hi_f32(
                        XT[:, bass.ds(u + 1, 1), :, :].rearrange("q o a k -> q (o a) k"))),
                       [(s_l[1], a - 1)], s_xs[c])
                if v_ok:
                    op(SP, lambda e: e.dma_start(xns[c][:, :], XND[bass.ds(unit(1)[1] * TILE, TILE), :]),
                       [(s_xa[1], a - 3)] + at_first(1, s_xnd),
                       s_xns[c])

                def logits(k):
                    cols = slice(h * HS + k * BANK, h * HS + (k + 1) * BANK)
                    out = lg[b][:, k * BANK:(k + 1) * BANK]
                    static = isinstance(u, int) and u < 4
                    tile = XT[:, u, :, :] if static else xs[b][:, :, :]
                    op(PE, lambda e: e.matmul(out, tile[:, 0, :], PHI[:, 0, cols], start=True, stop=False),
                       ([] if static else [loaded(s_xs, h, u, b)]) + [(s_ec[k], a - 2)])
                    op(PE, lambda e: e.matmul(out, tile[:, 0, :], PHI[:, 1, cols], start=False, stop=False))
                    op(PE, lambda e: e.matmul(out, tile[:, 1, :], PHI[:, 0, cols], start=False, stop=True),
                       done=s_l[k])

                def shift(k, matrix, waits, done):
                    cols = slice(k * BANK, (k + 1) * BANK)
                    op(PE, lambda e: e.matmul(lg[c][:, cols], mt[c][:, :], matrix[:, cols], start=False, stop=True,
                                              skip_group_check=True), waits, done)

                def x_tilde(k):
                    cols = slice(k * BANK, (k + 1) * BANK)
                    hx, tile = unit(2)
                    first, last = (isinstance(a, int) and tile == end for end in (0, NT - 1))
                    op(PE, lambda e: e.matmul(acc[k][:, :], xns[b][:, :], dd[b][:, cols], start=first, stop=last,
                                              skip_group_check=True),
                       [by_parity(s_xns, a - 2, b), (s_dd[k], a - 2)] + ([(s_ev, 2 * hx - 1)] if first else []),
                       s_xa[k])

                if u_ok:
                    logits(0)
                if v_ok:
                    op(PE, lambda e: e.matmul(tr[c][:, :], hi_f32(mr[c][:, :]), IDENT[:, :], start=True, stop=True),
                       [(s_mm, a - 1), (s_mt, a - 3)], s_tr)
                if u_ok:
                    logits(1)
                if v_ok:
                    shift(0, S1M, [(s_mt, a - 1)], s_s1[0])
                    shift(1, S1M, [], s_s1[1])
                if w_ok:
                    x_tilde(0)
                if v_ok:
                    shift(0, S2M, [(s_ed[0], a - 1)], s_s2[0])
                    shift(1, S2M, [(s_ed[1], a - 1)], s_s2[1])
                if w_ok:
                    x_tilde(1)

                if v_ok:
                    op(ACTE, lambda e: e.activation(mt[c][:, :], tr[c][:, :], ACT.Copy),
                       [(s_tr, a - 1), (s_s2[1], a - 3)], s_mt)
                    for k in range(2):
                        cols = slice(k * BANK, (k + 1) * BANK)
                        op(ACTE, lambda e, k=k, cols=cols: e.activation(ed[c][:, cols], lg[c][:, cols], ACT.Exp),
                           [(s_s1[k], a - 1), (s_dd[k], a - 3), (s_zd, a - 3)], s_ed[k])
                    for k in range(2):
                        cols = slice(k * BANK, (k + 1) * BANK)
                        op(ACTE, lambda e, k=k, cols=cols: e.activation(ec[c][:, cols], lg[c][:, cols], ACT.Exp),
                           [(s_s2[k], a - 1), (s_cs, 2 * (a - 3))], s_ec[k])

                if u_ok:
                    op(ACTE, lambda e: e.activation(mr[b][:, :], mx[b][:, :], ACT.Copy),
                       [(s_mx2, a), (s_mx, 2 * a + 1), (s_tr, a - 2), (s_sm, a - 2)], s_mm)
                    op(ACTE, lambda e: e.activation(
                        SM[:, h, bass.ds(u, 1), :].rearrange("q o p -> q (o p)"), hi_f32(mr[b][:, HN:G]), ACT.Copy),
                       [(s_mm, a)] + at_first(0, s_xnd[:2]), s_sm)

                def bank_max(k):
                    op(DVE, lambda e: e.tensor_reduce(
                        mx[b][:, k * HN // 2:(k + 1) * HN // 2],
                        lg[b][:, k * BANK:(k + 1) * BANK].rearrange("q (n p) -> q n p", p=NP), AX_X, ALU.max),
                       [(s_l[k], a), (s_mm, a - 2)], s_mx)
                if u_ok:
                    bank_max(0)
                if u_ok:
                    bank_max(1)
                    op(DVE, lambda e: e.tensor_reduce(
                        mx[b][:, HN:G], lg[b][:, :].rearrange("q (n p) -> q p n", p=NP), AX_X, ALU.max), [], s_mx2)
                if v_ok:
                    op(DVE, lambda e: e.tensor_reduce(
                        zd[c][:, :], ed[c][:, :].rearrange("q (n p) -> q n p", p=NP), AX_X, ALU.add),
                       [(s_ed[0], a - 1), (s_ed[1], a - 1)], s_zd)
                if s_ok:
                    op(DVE, lambda e: e.tensor_reduce(
                        SS[:, unit(3)[0], bass.ds(unit(3)[1], 1), :].rearrange("q o p -> q (o p)"),
                        cs[c][:, 0:BANK // 2].rearrange("q (n p) -> q p n", p=NP), AX_X, ALU.add),
                       [(s_cs, 2 * (a - 3) + 1)] + at_first(3, s_xnd[2:]),
                       s_ss)
                if v_ok:
                    op(DVE, lambda e: e.reciprocal(rz[c][:, :], zd[c][:, :]),
                       [(s_zd, a - 1), (s_dd[1], a - 3)], s_rz)

                if v_ok:
                    for k in range(2):
                        cols = slice(k * BANK, (k + 1) * BANK)
                        op(POOL, lambda e, k=k, cols=cols: e.tensor_tensor(
                            dd[c][:, cols].rearrange("q (n p) -> q n p", p=NP),
                            ed[c][:, cols].rearrange("q (n p) -> q n p", p=NP),
                            rz[c][:, k * HN // 2:(k + 1) * HN // 2].unsqueeze(2).broadcast_to([P, HN // 2, NP]),
                            ALU.mult), [(s_rz, a - 1), (s_xa[k], a - 3)], s_dd[k])
                    op(POOL, lambda e: e.tensor_tensor(cs[c][:, :], ec[c][:, 0:BANK], ec[c][:, BANK:HS], ALU.add),
                       [(s_ec[0], a - 1), (s_ec[1], a - 1), (s_ss, a - 3)], s_cs)
                    op(POOL, lambda e: e.tensor_tensor(cs[c][:, 0:BANK // 2], cs[c][:, 0:BANK // 2],
                                                       cs[c][:, BANK // 2:BANK], ALU.add),
                       [(s_cs, 2 * (a - 1))], s_cs)

            s_mx2 = stage("p1_slot_max", DVE)

            UNROLL = 4

            def phase1(op, eng):
                op(ACTE, lambda e: e.preload_act_table_set("natural_log_exp_and_others"))
                def straight(a):
                    slot(op, a // NT, a % NT, a % 2, u_ok=a < HALVES * NT, v_ok=1 <= a <= HALVES * NT,
                         w_ok=2 <= a <= HALVES * NT + 1, s_ok=a >= 3, xs_ok=a < HALVES * NT - 1)
                    for h in range(HALVES):
                        if a - 2 == (h + 1) * NT - 1:
                            for k in range(2):
                                op(ACTE, lambda e, k=k, h=h: e.activation(
                                    XTT[:, h * HS + k * BANK:h * HS + (k + 1) * BANK], acc[k][:, :], ACT.Copy),
                                   [(s_xa[k], (h + 1) * NT - 1)], s_ev)

                for a in range(4):
                    straight(a)
                for h in range(HALVES):
                    with eng.Fori(4, NT - 4, UNROLL) as u:
                        for v in range(UNROLL):
                            slot(op, h, u + v, v % 2)
                    for a in range((h + 1) * NT - 4, (h + 1) * NT + (4 if h < HALVES - 1 else 3)):
                        straight(a)
                    if h == 0:
                        op(SP, lambda e: e.dma_start(STATS[:, 0, 0, :, :], SM[:, 0, :, :]), [(s_sm, NT - 1)], s_store)
                        op(SP, lambda e: e.dma_start(STATS[:, 1, 0, :, :], SS[:, 0, :, :]), [(s_ss, NT - 1)], s_store)
            phase(phase1)
        front.close()

        def join_steps(op, b, m, z, mj, l3, out, loaded, free=()):
            count = [0]

            def link(who, make, waits=(), signal=True):
                before = [(s_join, b * JOIN_STEPS + count[0] - 1)] if count[0] else []
                op(who, make, list(waits) + before, s_join if signal else None)
                count[0] += signal
            half = lambda v, k: v[:, k, :, :]
            both_ = mj.unsqueeze(1).broadcast_to([P, HALVES, TPB, NP])

            def shifts():
                link(DVE, lambda e: e.tensor_tensor(mj, half(m, 0), half(m, 1), ALU.max), loaded)
                link(DVE, lambda e: e.tensor_tensor(m, m, both_, ALU.subtract))

            def factors():
                link(ACTE, lambda e: e.activation(m, m, ACT.Exp))

            def sums():
                link(DVE, lambda e: e.tensor_tensor(z, z, m, ALU.mult))
                link(DVE, lambda e: e.tensor_tensor(half(z, 0), half(z, 0), half(z, 1), ALU.add))

            def logarithm():
                link(ACTE, lambda e: e.activation(half(z, 1), half(z, 0), ACT.Ln))

            def parts():
                link(DVE, lambda e: e.tensor_tensor(mj, mj, half(z, 1), ALU.add))
                link(DVE, lambda e: e.tensor_copy(l3[:, :, 0, :], mj))
                link(DVE, lambda e: e.tensor_tensor(half(z, 0), mj, l3[:, :, 0, :], ALU.subtract))
                link(DVE, lambda e: e.tensor_copy(l3[:, :, 1, :], half(z, 0)))
                link(DVE, lambda e: e.tensor_tensor(l3[:, :, 2, :], half(z, 0), l3[:, :, 1, :], ALU.subtract))

            def turned():
                for k in range(TPB):
                    link(PE, lambda e, k=k: e.transpose(out[:, k, :], l3[:, k, :, :].rearrange("q a p -> q (a p)"),
                                                        IDENTB[:, :]), free if k == 0 else (), k == TPB - 1)

            def stored():
                link(ACTE, lambda e: e.activation(
                    LSE[:, bass.ds(b * SEQ, SEQ)].rearrange("r (k n) -> r k n", n=TILE), out, ACT.Copy))
                assert count[0] == JOIN_STEPS
            return [shifts, factors, sums, logarithm, parts, turned, stored]

        with ExitStack() as ph:
            EG, RE = 8, 4
            ew = [sb(ph, f"expert_w{k}", [P, EG, P]) for k in range(RE)]
            eb = sb(ph, "expert_b", [P, CH, P])
            xc = sb(ph, "xc", [P, SLOTS])
            sq = sb(ph, "sq", [P, SLOTS])
            lam2 = sb(ph, "lam_work", [P, 8])
            m0 = sb(ph, "m0", [P, HALVES, TPB, NP])
            z0 = sb(ph, "z0", [P, HALVES, TPB, NP])
            mj0 = sb(ph, "m_joined0", [P, TPB, NP])
            l30 = sb(ph, "lse_parts0", [P, TPB, 3, NP], BF16)
            yf = sq[:, :].rearrange("q (c h) -> q c h", h=P)
            pm = [psum(ph, f"pm{k}", [P, BANK]) for k in range(4)]
            py = [psum(ph, f"py{k}", [P, BANK]) for k in range(2)]
            pt0 = psum(ph, "pt0", [3 * NP, TPB, TILE], BF16)
            s_ew = stage("pb_expert_b", SP, 16)
            s_ewg = [stage(f"pb_expert_w{k}", SP, 16) for k in range(RE)]
            s_v = stage("pb_vector", DVE)
            s_a = stage("pb_scalar", ACTE)
            s_p = stage("pb_tensor", PE)

            def phase1b(op, eng):
                nv, na, npe = [0], [0], [0]

                def vec(make, waits=()):
                    op(DVE, make, waits, s_v)
                    nv[0] += 1
                    return (s_v, nv[0] - 1)

                def act(make, waits=()):
                    op(ACTE, make, waits, s_a)
                    na[0] += 1
                    return (s_a, na[0] - 1)

                def pe(make, waits=()):
                    op(PE, make, waits, s_p)
                    npe[0] += 1
                    return (s_p, npe[0] - 1)

                def load_experts(g):
                    op(SP, lambda e: e.dma_start(ew[g % RE][:, :, :], t["expert_w"][:, g * EG:(g + 1) * EG, :]),
                       [ys[(g - RE + 1) * EG // EPC - 1]] if g >= RE else (), s_ewg[g % RE])
                for g in range(RE):
                    load_experts(g)
                for j in range(EPC):
                    op(SP, lambda e, j=j: e.dma_start(
                        eb[j * NP:(j + 1) * NP, :, :],
                        t["expert_b"].rearrange("(c j) h -> j c h", j=EPC)[j:j + 1, :, :].broadcast_to([NP, CH, P])),
                       done=s_ew)
                op(ACTE, lambda e: e.dma_start(STATS[:, 0, 1, :, :], SM[:, 1, :, :]), done=s_store)
                op(ACTE, lambda e: e.dma_start(STATS[:, 1, 1, :, :], SS[:, 1, :, :]), done=s_store)
                quarter = [slice(q * BANK, (q + 1) * BANK) for q in range(4)]
                ys = {}
                clip, mean, cen, squ, var, ln, rs, hat, th = ({} for _ in range(9))
                for q, cols in enumerate(quarter):
                    clip[q] = vec(lambda e, cols=cols: e.tensor_scalar(XTT[:, cols], XTT[:, cols], -33000.0, 65000.0,
                                                                       ALU.max, ALU.min))
                tiles0 = slice(0, TPB)
                vec(lambda e: e.tensor_copy(m0[:, :, :, :], SM[:, :, tiles0, :]))
                cz = vec(lambda e: e.tensor_copy(z0[:, :, :, :], SS[:, :, tiles0, :]))
                shifts_, factors_, sums_, logarithm_, parts_, turned_, stored_ = join_steps(
                    op, 0, m0[:, :, :, :], z0[:, :, :, :], mj0[:, :, :], l30[:, :, :, :], pt0[:, :, :], [cz])
                shifts_()
                factors_()
                for q, cols in enumerate(quarter):
                    mean[q] = pe(lambda e, cols=cols, q=q: e.matmul(pm[q][:, :], MEAN[:, :], XTT[:, cols],
                                                                    start=True, stop=True), [clip[q]])
                for q, cols in enumerate(quarter):
                    cen[q] = vec(lambda e, cols=cols, q=q: e.tensor_tensor(xc[:, cols], XTT[:, cols], pm[q][:, :],
                                                                           ALU.subtract), [mean[q]])
                    squ[q] = act(lambda e, cols=cols: e.activation(sq[:, cols], xc[:, cols], ACT.Square), [cen[q]])
                sums_()
                logarithm_()
                l1 = act(lambda e: e.activation(lam2[:, 0:1], VEC[:, V_LAM:V_LAM + 1], ACT.Exp, scale=-1.0))
                l2 = vec(lambda e: e.tensor_scalar(lam2[:, 1:2], lam2[:, 0:1], 1.0, None, ALU.add), [l1])
                l3 = vec(lambda e: e.reciprocal(lam2[:, 2:3], lam2[:, 1:2]), [l2])
                l4 = vec(lambda e: e.tensor_scalar(lam2[:, 4:5], lam2[:, 2:3], 1e-8, None, ALU.add), [l3])
                l5 = act(lambda e: e.activation(lam2[:, 3:4], lam2[:, 4:5], ACT.Ln), [l4])
                vec(lambda e: e.tensor_scalar(VX[:, 2:3], lam2[:, 3:4], 4.0, None, ALU.mult), [l5])
                for q, cols in enumerate(quarter):
                    var[q] = pe(lambda e, cols=cols, q=q: e.matmul(pm[q][:, :], MEAN[:, :], sq[:, cols],
                                                                   start=True, stop=True), [squ[q]])
                for q, cols in enumerate(quarter):
                    ln[q] = act(lambda e, cols=cols, q=q: e.activation(sq[:, cols], pm[q][:, :], ACT.Ln,
                                                                       bias=EPS[:, 0:1]), [var[q]])
                    rs[q] = act(lambda e, cols=cols: e.activation(sq[:, cols], sq[:, cols], ACT.Exp, scale=-0.5),
                                [ln[q]])
                    hat[q] = vec(lambda e, cols=cols: e.tensor_tensor(xc[:, cols], xc[:, cols], sq[:, cols], ALU.mult),
                                 [rs[q]])
                parts_()
                for q, cols in enumerate(quarter):
                    th[q] = act(lambda e, cols=cols: e.activation(XTT[:, cols], xc[:, cols], ACT.Tanh), [hat[q]])
                for c in range(CH):
                    for j in range(EPC):
                        n = c * EPC + j
                        op(PE, lambda e, c=c, j=j, n=n: e.matmul(
                            py[c % 2][j * NP:(j + 1) * NP, 0:P], XTT[:, n * NP:(n + 1) * NP],
                            ew[n // EG % RE][:, n % EG, :],
                            start=True, stop=True),
                           [(s_ewg[n // EG % RE], n // EG // RE), th[c * P // BANK]] + ([ys[c - 2]] if c >= 2 else [])
                           if j == 0 else (), s_p if j == EPC - 1 else None)
                    npe[0] += 1
                    yp = (s_p, npe[0] - 1)
                    ys[c] = vec(lambda e, c=c: e.tensor_tensor(yf[:, c, :], py[c % 2][:, 0:P], eb[:, c, :], ALU.add),
                                [yp, (s_ew, EPC - 1)])
                    if c % 4 == 3:
                        cc = slice(c - 3, c + 1)
                        yh = act(lambda e, cc=cc: e.activation(YHI[:, cc, :], yf[:, cc, :], ACT.Copy), [ys[c]])
                        op(POOL, lambda e, cc=cc: e.tensor_tensor(YLO[:, cc, :], yf[:, cc, :], hi_f32(YHI[:, cc, :]),
                                                                  ALU.subtract), [yh])
                    g = (c + 1) // (EG // EPC) - 1 + RE
                    if (c + 1) % (EG // EPC) == 0 and g < NEXP // EG:
                        load_experts(g)
                turned_()
                stored_()
                op(SP, lambda e: e.nop(), [(s_store, 3)])
            phase(phase1b)
        both.close()

        with ExitStack() as ph:
            LAG = 3
            RC = 4
            cf = [sb(ph, f"cf{k}", [P, SEQ]) for k in range(2)]
            chi = [sb(ph, f"chi{k}", [P, SEQ], F32R) for k in range(RC)]
            clo = [sb(ph, f"clo{k}", [P, SEQ], F32R) for k in range(RC)]
            yt = sb(ph, "yt", [P, SEQ])
            names = ("qf", "e0", "e1", "e2", "e3", "st", "xraw", "ty", "x1", "xc", "x1k",
                     "ti", "tg", "aa", "a2", "hh", "xr", "xk", "kr", "f1")
            B = {n: sb(ph, "b_" + n, [P, SEQ]) for n in names}
            XP = sb(ph, "xn1", [P, SEQ + 1])
            R = {n: sb(ph, "r_" + n, [P, SEQ], F32R) for n in ("qh", "ql", "vh", "vl", "xh", "xl")}
            pth = [sb(ph, f"pth{k}", [P, SEQ], F32R) for k in range(2)]
            ptl = [sb(ph, f"ptl{k}", [P, SEQ], F32R) for k in range(2)]
            nmx = sb(ph, "nmx", [P, 4 * TPB])
            zs = sb(ph, "slot_sums", [P, HALVES, TPB, NP])
            ms = B["tg"][:, 0:HALVES * TPB * NP].rearrange("q (h t p) -> q h t p", h=HALVES, t=TPB)
            mjs = B["tg"][:, HALVES * TPB * NP:(HALVES + 1) * TPB * NP].rearrange("q (t p) -> q t p", t=TPB)
            l3s = B["tg"][:, 0:HALVES * TPB * NP].bitcast(BF16)[:, 0:3 * TPB * NP].rearrange(
                "q (t a p) -> q t a p", t=TPB, a=3)

            lgp = [psum(ph, f"lgp{k}", [P, SEQ]) for k in range(2)]
            yac = psum(ph, "yac", [P, SEQ])
            at = [psum(ph, f"at{k}", [P, SEQ]) for k in range(2)]
            lp = [psum(ph, f"lp{k}", [P, SEQ]) for k in range(3)]
            turned_lse = lp[2][:, :].bitcast(BF16)[0:3 * NP, 0:TPB * TILE].rearrange("r (k n) -> r k n", k=TPB)

            c_l = stage("c_logits", PE)
            c_e = stage("c_exp", ACTE)
            c_h = stage("c_high", DVE)
            c_s = stage("c_low", POOL)
            c_y = stage("c_y", PE)
            side = []

            def once(name, producer, inc=1, credit=1):
                s = stage(name, producer, inc, credit)
                side.append(s)
                return s
            y_c = once("y_copied", ACTE)
            s_st = stage("statistics_loaded", SP, 16)
            ALL = dict(
                q_p=PE, q_f=ACTE, q_h=DVE, q_l=DVE, v_p=PE, v_h=ACTE, v_l=DVE,
                o_c=ACTE,
                xr_dma=SP, out_dma=SP,
                t_y=ACTE, u_y=DVE, us=POOL, res=DVE, x1k=ACTE, mn=PE, xc=DVE, sq=ACTE, vr=PE, ln=ACTE, rs=ACTE, xn=DVE,
                xh=DVE, xl=DVE, p_r=PE, p_i=PE, p_x=PE, t_r=ACTE, t_i=ACTE, a=ACTE, ix=DVE, a2=ACTE, om=DVE,
                sl=ACTE, sr=ACTE, gt=DVE, hh=DVE, hq=ACTE, hm=PE, hl=ACTE, hr=ACTE, po=PE, o1=DVE,
                wr=POOL, wk=POOL, xr=DVE, xk=DVE, pr=PE, pk=PE, tr2=ACTE, kr=ACTE, ka=ACTE, pv=PE, f1=DVE,
                tf=ACTE, f2=DVE, f3=DVE, f4=DVE)
            FOUR = dict(s=PE, m=DVE, n=DVE, x=ACTE, z=DVE, p=DVE, w=PE, k=PE, kh=ACTE, kl=DVE)
            S4 = {n: stage("a_" + n, who) for n, who in FOUR.items()}
            S = {n: once("b_" + n, who, credit=16 if who == SP else 1, inc=16 if who == SP else 1)
                 for n, who in ALL.items()}

            def tiles_of(i, part):
                return XT[:, bass.ds(i * TPB, TPB), part, :]

            def chunk_logits(op, i, c):
                g = i * CH + c
                cols = slice(c * P, (c + 1) * P)
                out = lgp[c % 2][:, :]
                lse_ready = [(s_join, i * JOIN_STEPS + JOIN_STEPS - 1)] if c == 0 else []
                op(PE, lambda e: e.matmul(out, MINUS_P[:, :], LSE[:, bass.ds(i * SEQ, SEQ)], start=True, stop=False),
                   [(c_e, g - 2)] + lse_ready)
                op(PE, lambda e: e.matmul(out, PHI[:, 0, cols], tiles_of(i, 0), start=False, stop=False))
                op(PE, lambda e: e.matmul(out, PHI[:, 0, cols], tiles_of(i, 1), start=False, stop=False))
                op(PE, lambda e: e.matmul(out, PHI[:, 1, cols], tiles_of(i, 0), start=False, stop=True), done=c_l)
                op(ACTE, lambda e: e.activation(cf[c % 2][:, :], out, ACT.Exp),
                   [(c_l, g), (c_s, g - 2)], c_e)
                op(DVE, lambda e: e.tensor_copy(chi[c % RC][:, :], cf[c % 2][:, :]),
                   [(c_e, g), (c_y, g - RC)], c_h)
                op(POOL, lambda e: e.tensor_tensor(clo[c % RC][:, :], cf[c % 2][:, :], hi_f32(chi[c % RC][:, :]),
                                                  ALU.subtract), [(c_h, g)], c_s)

            def chunk_y(op, i, c):
                g = i * CH + c
                op(PE, lambda e: e.matmul(yac[:, :], YHI[:, c, :], chi[c % RC][:, :], start=c == 0, stop=False),
                   [(c_h, g)] + ([(y_c, i - 1)] if c == 0 else []))
                op(PE, lambda e: e.matmul(yac[:, :], YLO[:, c, :], chi[c % RC][:, :], start=False, stop=False))
                op(PE, lambda e: e.matmul(yac[:, :], YHI[:, c, :], clo[c % RC][:, :], start=False, stop=c == CH - 1),
                   [(c_s, g)], c_y)

            def three(op, out, w, hi, lo, waits, done):
                op(PE, lambda e: e.matmul(out, WHI[:, w, :], hi(), start=True, stop=False), waits)
                op(PE, lambda e: e.matmul(out, WHI[:, w, :], lo(), start=False, stop=False))
                op(PE, lambda e: e.matmul(out, WLO[:, w, :], hi(), start=False, stop=True), done=done)

            def attention(op, i):
                j = lambda n, back=0: (S[n], i - back)
                q = lambda n, k, back=0: (S4[n], (i - back) * TPB + k)
                scale = float(P) ** -0.5
                steps = {}

                def project():
                    three(op, at[0][:, :], W_Q, lambda: tiles_of(i, 0), lambda: tiles_of(i, 1), [j("o_c", 1)], S["q_p"])
                    op(ACTE, lambda e: e.activation(B["qf"][:, :], at[0][:, :], ACT.Identity,
                                                    bias=VEC[:, V_BQ:V_BQ + 1]), [j("q_p"), j("v_p", 1)], S["q_f"])

                def project_split():
                    op(DVE, lambda e: e.tensor_copy(R["qh"][:, :], B["qf"][:, :]), [j("q_f"), q("s", TPB - 1, 1)],
                       S["q_h"])
                    op(DVE, lambda e: e.tensor_tensor(R["ql"][:, :], B["qf"][:, :], hi_f32(R["qh"][:, :]),
                                                      ALU.subtract), [j("q_h")], S["q_l"])

                def values():
                    for k in range(TPB):
                        cols = slice(k * TILE, (k + 1) * TILE)
                        op(PE, lambda e, cols=cols: e.transpose(at[1][:, cols], B["qf"][:, cols], IDENT[:, :]),
                           [j("q_f"), q("kl", TPB - 1, 1)] if k == 0 else (), S["v_p"] if k == TPB - 1 else None)

                def values_split():
                    op(ACTE, lambda e: e.activation(R["vh"][:, :], at[1][:, :], ACT.Copy),
                       [j("v_p"), q("w", TPB - 1, 1)], S["v_h"])
                    op(DVE, lambda e: e.tensor_tensor(R["vl"][:, :], at[1][:, :], hi_f32(R["vh"][:, :]), ALU.subtract),
                       [j("v_h")], S["v_l"])
                steps.update(project=project, project_split=project_split, values=values, values_split=values_split)

                def block(r):
                    rows = slice(r * TILE, (r + 1) * TILE)
                    bank = at[r % 2][:, :]
                    free = [j("q_f"), j("v_l"), q("x", 0), q("x", 1)]
                    m, nm, z, rz_ = (nmx[:, 4 * r + k:4 * r + k + 1] for k in range(4))
                    E = B[f"e{r}"][:, :]

                    def scores():
                        op(PE, lambda e: e.matmul(bank, R["qh"][:, rows], R["qh"][:, :], start=True, stop=False),
                           [j("q_h"), free[r]])
                        op(PE, lambda e: e.matmul(bank, R["qh"][:, rows], R["ql"][:, :], start=False, stop=False),
                           [j("q_l")])
                        op(PE, lambda e: e.matmul(bank, R["ql"][:, rows], R["qh"][:, :], start=False, stop=True),
                           done=S4["s"])
                        op(DVE, lambda e: e.tensor_reduce(m, bank, AX_X, ALU.max), [q("s", r)], S4["m"])
                        op(DVE, lambda e: e.tensor_scalar(nm, m, -scale, None, ALU.mult), [q("m", r), q("x", r, 1)],
                           S4["n"])

                    def exponential():
                        op(ACTE, lambda e: e.activation(E, bank, ACT.Exp, bias=nm, scale=scale, accum_out=z),
                           [q("n", r), q("k", TPB - 1, 1), q("z", r, 1)], S4["x"])

                    def weights():
                        op(DVE, lambda e: e.reciprocal(rz_, z), [q("x", r), q("p", r, 1)], S4["z"])
                        op(DVE, lambda e: e.tensor_scalar(E, E, rz_, None, ALU.mult), [q("z", r)], S4["p"])

                    k = r
                    keys = rows

                    def turn():
                        for r in range(TPB):
                            op(PE, lambda e, r=r: e.transpose(at[1][:, r * TILE:(r + 1) * TILE], B[f"e{r}"][:, keys],
                                                              IDENT[:, :]),
                               [q("p", r)] + ([q("x", 3) if k == 0 else q("kl", k - 1)] if r == 0 else []),
                               S4["k"] if r == TPB - 1 else None)

                    def turn_split():
                        op(ACTE, lambda e: e.activation(pth[k % 2][:, :], at[1][:, :], ACT.Copy),
                           [q("k", k), q("w", k - 2) if k >= 2 else q("w", k + 2, 1)], S4["kh"])
                        op(DVE, lambda e: e.tensor_tensor(ptl[k % 2][:, :], at[1][:, :], hi_f32(pth[k % 2][:, :]),
                                                          ALU.subtract), [q("kh", k)], S4["kl"])

                    def weigh():
                        for n, (v, pt_, after) in enumerate(((R["vh"], pth, "kh"), (R["vl"], pth, "kh"),
                                                             (R["vh"], ptl, "kl"))):
                            op(PE, lambda e, v=v, pt_=pt_, n=n: e.matmul(
                                at[0][:, :], v[:, keys], pt_[k % 2][:, :], start=k == 0 and n == 0,
                                stop=k == TPB - 1 and n == 2),
                               [q(after, k)] + ([j("v_l"), q("x", 2)] if k == 0 and n == 0 else []),
                               S4["w"] if n == 2 else None)
                    steps.update({f"{f.__name__}{r}": f for f in (scores, exponential, weights, turn, turn_split,
                                                                  weigh)})
                for r in range(TPB):
                    block(r)

                def attended():
                    op(ACTE, lambda e: e.activation(B["st"][:, :], at[0][:, :], ACT.Copy),
                       [q("w", TPB - 1), (S["us"], i - 1)], S["o_c"])
                steps.update(attended=attended)
                return steps

            def joined(b):
                b = min(b, NB - 1) if isinstance(b, int) else b
                return (s_join, b * JOIN_STEPS + JOIN_STEPS - 1)

            def next_lse(op, b):
                def load_statistics():
                    for k, dst in ((0, ms), (1, zs)):
                        for h in range(HALVES):
                            op(SP, lambda e, k=k, h=h, dst=dst: e.dma_start(
                                dst[:, h, :, :], STATS[:, k, h, bass.ds(b * TPB, TPB), :]),
                               [(S["a"], b - 3), (s_join, (b - 1) * JOIN_STEPS + JOIN_STEPS - 1)], s_st)
                steps = join_steps(op, b, ms, zs[:, :, :, :], mjs, l3s, turned_lse,
                                   [(s_st, b * 2 * HALVES - 1)], [(S["kr"], b - 3), (S["o1"], b - 3)])
                return {"load_statistics": load_statistics, **{"lse_" + f.__name__: f for f in steps}}

            def layer1(op, i):
                j = lambda n, back=0: (S[n], i - back)
                one = lambda v, k: v[:, k:k + 1]
                x_in = XP[:, 1:SEQ + 1]
                x_prev = XP[:, 0:SEQ]

                def tt(who, out, a, b, f, waits, done):
                    op(who, lambda e: e.tensor_tensor(out[:, :], a[:, :], b[:, :], f), waits, S[done])

                def af(out, in_, func, waits, done, **kw):
                    op(ACTE, lambda e: e.activation(out[:, :], in_[:, :], func, **kw), waits, S[done])

                def y_copy():
                    op(ACTE, lambda e: e.activation(yt[:, :], yac[:, :], ACT.Copy),
                       [(c_y, i * CH + CH - 1), j("u_y", 1)], y_c)
                    af(B["ty"], yt, ACT.Tanh, [(y_c, i), j("xn", 1)], "t_y", scale=0.5)

                def silu_y():
                    op(DVE, lambda e: e.scalar_tensor_tensor(B["ty"][:, :], B["ty"][:, :], 1.0, yt[:, :],
                                                             ALU.add, ALU.mult), [j("t_y")], S["u_y"])
                    tt(POOL, B["ty"], B["ty"], B["st"], ALU.mult, [j("u_y"), (S["o_c"], i)], "us")

                def residual():
                    op(SP, lambda e: e.dma_start(B["xraw"][:, :], t["xT"][:, bass.ds(i * SEQ, SEQ)]),
                       [j("res", 1)], S["xr_dma"])
                    op(DVE, lambda e: e.scalar_tensor_tensor(B["x1"][:, :], B["ty"][:, :], 0.5, B["xraw"][:, :],
                                                             ALU.mult, ALU.add),
                       [j("us"), j("xr_dma"), j("x1k", 1)], S["res"])

                def keep():
                    af(B["x1k"], B["x1"], ACT.Copy, [j("res"), j("f4", 1)], "x1k")

                def mean():
                    op(PE, lambda e: e.matmul(lp[0][:, :], MEAN[:, :], B["x1"][:, :], start=True, stop=True),
                       [j("res"), j("f1", 1)], S["mn"])
                    tt(DVE, B["xc"], B["x1"], lp[0], ALU.subtract, [j("mn"), j("xn", 1)], "xc")

                def squares():
                    af(B["ty"], B["xc"], ACT.Square, [j("xc")], "sq")

                def variance():
                    op(PE, lambda e: e.matmul(lp[1][:, :], MEAN[:, :], B["ty"][:, :], start=True, stop=True),
                       [j("sq"), j("ix", 1), j("hl", 1)], S["vr"])

                def deviation():
                    af(B["ty"], lp[1], ACT.Ln, [j("vr")], "ln", bias=one(EPS, 0))
                    af(B["ty"], B["ty"], ACT.Exp, [j("ln")], "rs", scale=-0.5)

                def normalise():
                    op(DVE, lambda e: e.tensor_tensor(x_in, B["xc"][:, :], B["ty"][:, :], ALU.mult),
                       [j("rs"), j("wk", 1)], S["xn"])

                def normalised_split():
                    op(DVE, lambda e: e.tensor_copy(R["xh"][:, :], x_in), [j("xn"), j("p_x", 1)], S["xh"])
                    op(DVE, lambda e: e.tensor_tensor(R["xl"][:, :], x_in, hi_f32(R["xh"][:, :]), ALU.subtract),
                       [j("xh")], S["xl"])

                hi, lo = (lambda: R["xh"][:, :]), (lambda: R["xl"][:, :])

                def decay_gate():
                    three(op, lp[2][:, :], W_RG, hi, lo, [j("xl"), j("o1", 1), joined(i + 2)], S["p_r"])

                def decay_tanh():
                    af(B["tg"], lp[2], ACT.Tanh, [j("p_r"), j("a", 1), joined(i + 2)], "t_r", scale=0.5,
                       bias=one(VX, 1))

                def decay():
                    af(B["aa"], B["tg"], ACT.Exp, [j("t_r"), j("f4", 1)], "a", scale=one(VX, 2), bias=one(VX, 2))
                    af(B["a2"], B["aa"], ACT.Square, [j("a"), j("hm", 1)], "a2")

                def input_gate():
                    three(op, lp[0][:, :], W_IG, hi, lo, [j("xc")], S["p_i"])

                def input_tanh():
                    af(B["ti"], lp[0], ACT.Tanh, [j("p_i"), j("out_dma", 1)], "t_i", scale=0.5, bias=one(VX, 0))

                def input_product():
                    three(op, lp[1][:, :], W_IN, hi, lo, [j("ln")], S["p_x"])

                def gated():
                    op(DVE, lambda e: e.scalar_tensor_tensor(B["ti"][:, :], B["ti"][:, :], 1.0, lp[1][:, :],
                                                             ALU.add, ALU.mult), [j("t_i"), j("p_x")], S["ix"])
                    op(DVE, lambda e: e.tensor_scalar(B["a2"][:, :], B["a2"][:, :], -1.0, 1.0, ALU.mult, ALU.add),
                       [j("a2")], S["om"])

                def mix_previous():
                    for n, dst in ((0, "wr"), (1, "wk")):
                        op(POOL, lambda e, n=n: e.tensor_tensor(
                            B["xr" if n == 0 else "xk"][:, :], x_prev, one(VX, 3 + n).broadcast_to([P, SEQ]),
                            ALU.mult),
                           [j("xn"), j("tf" if n == 0 else "pk", 1), j("f2", 1)], S[dst])

                def mix():
                    for n, k, src, dst in ((0, V_MUR, "xr", "xr"), (1, V_MUK, "xk", "xk")):
                        op(DVE, lambda e, k=k, src=src, dst=dst: e.scalar_tensor_tensor(
                            B[dst][:, :], x_in, one(VEC, k), B[src][:, :], ALU.mult, ALU.add),
                           [j("wr" if n == 0 else "wk")], S[dst])

                def ffn_r():
                    op(PE, lambda e: e.matmul(lp[0][:, :], WRAW[:, W_R, :], B["xr"][:, :], start=True, stop=True),
                       [j("xr"), j("t_i")], S["pr"])

                def ffn_r_tanh():
                    af(B["f1"], lp[0], ACT.Tanh, [j("pr"), j("f4", 1)], "tr2", scale=0.5)

                def ffn_k():
                    op(PE, lambda e: e.matmul(lp[2][:, :], WRAW[:, W_K, :], B["xk"][:, :], start=True, stop=True),
                       [j("xk"), j("t_r")], S["pk"])

                def ffn_k_squared():
                    af(B["kr"], lp[2], ACT.Relu, [j("pk"), j("f2", 1)], "kr")
                    af(B["kr"], B["kr"], ACT.Square, [j("kr")], "ka")

                def ffn_v():
                    op(PE, lambda e: e.matmul(lp[0][:, :], WRAW[:, W_V, :], B["kr"][:, :], start=True, stop=True),
                       [j("ka"), j("tr2")], S["pv"])

                def ffn():
                    op(DVE, lambda e: e.scalar_tensor_tensor(B["kr"][:, :], B["f1"][:, :], 1.0, lp[0][:, :],
                                                             ALU.add, ALU.mult), [j("pv"), j("ka")], S["f1"])

                def ffn_tanh():
                    af(B["xr"], B["kr"], ACT.Tanh, [j("f1"), j("pr")], "tf", scale=0.25)

                def ffn_silu():
                    op(DVE, lambda e: e.scalar_tensor_tensor(B["f1"][:, :], B["xr"][:, :], 1.0, B["kr"][:, :],
                                                             ALU.add, ALU.mult), [j("tf")], S["f2"])

                def input_scale():
                    af(B["a2"], B["a2"], ACT.Ln, [j("om")], "sl", bias=one(EPS, 1))
                    af(B["a2"], B["a2"], ACT.Exp, [j("sl")], "sr", scale=0.5)

                def scan():
                    op(DVE, lambda e: e.scalar_tensor_tensor(B["ti"][:, :], B["ti"][:, :], 0.5, B["a2"][:, :],
                                                             ALU.mult, ALU.mult), [j("sr"), j("ix")], S["gt"])
                    op(DVE, lambda e: e.tensor_tensor_scan(B["hh"][:, :], B["aa"][:, :], B["ti"][:, :],
                                                           one(VEC, V_H0), ALU.mult, ALU.add),
                       [j("gt"), j("a"), j("po", 1)], S["hh"])

                def state_squares():
                    af(B["a2"], B["hh"], ACT.Square, [j("hh")], "hq")

                def state_out():
                    op(PE, lambda e: e.matmul(lp[2][:, :], WRAW[:, W_OUT, :], B["hh"][:, :], start=True, stop=True),
                       [j("hh"), j("kr")], S["po"])

                def state_mean():
                    op(PE, lambda e: e.matmul(lp[1][:, :], MEAN[:, :], B["a2"][:, :], start=True, stop=True),
                       [j("hq"), j("ix")], S["hm"])

                def state_norm():
                    af(B["aa"], lp[1], ACT.Ln, [j("hm")], "hl", bias=one(EPS, 1))
                    af(B["aa"], B["aa"], ACT.Exp, [j("hl")], "hr", scale=-0.5)

                def output():
                    op(DVE, lambda e: e.tensor_tensor(B["aa"][:, :], lp[2][:, :], B["aa"][:, :], ALU.mult),
                       [j("po"), j("hr")], S["o1"])
                    op(DVE, lambda e: e.scalar_tensor_tensor(B["aa"][:, :], B["f1"][:, :], 0.25, B["aa"][:, :],
                                                             ALU.mult, ALU.mult), [j("o1"), j("f2")], S["f3"])
                    op(DVE, lambda e: e.tensor_tensor(B["ti"][:, :], B["aa"][:, :], B["x1k"][:, :], ALU.add),
                       [j("f3"), j("x1k")], S["f4"])
                    op(SP, lambda e: e.dma_start(t["out"][:, bass.ds(i * SEQ, SEQ)], B["ti"][:, :]),
                       [j("f4")], S["out_dma"])

                def table_tanh():
                    op(ACTE, lambda e: e.preload_act_table_set("exp_and_others"))

                def table_ln():
                    op(ACTE, lambda e: e.preload_act_table_set("natural_log_exp_and_others"))

                return {f.__name__: f for f in (
                    y_copy, silu_y, residual, keep, mean, squares, variance, deviation, normalise, normalised_split,
                    decay_gate, decay_tanh, decay, input_gate, input_tanh, input_product, gated, mix_previous, mix,
                    ffn_r, ffn_r_tanh, ffn_k, ffn_k_squared, ffn_v, ffn, ffn_tanh, ffn_silu, input_scale, scan,
                    state_squares, state_out, state_mean, state_norm, output, table_tanh, table_ln)}

            BEFORE, AFTER = False, True
            SCHEDULE = [
                (0, 0, AFTER, "project"),
                (0, 1, BEFORE, "project_split"),
                (0, 1, AFTER, "values"),
                (0, 2, BEFORE, "values_split"),
                (0, 2, AFTER, "scores0"),
                (0, 3, AFTER, "exponential0"),
                (0, 4, BEFORE, "weights0"),
                (0, 3, AFTER, "scores1"),
                (0, 4, AFTER, "exponential1"),
                (0, 6, BEFORE, "weights1"),
                (0, 4, AFTER, "scores2"),
                (0, 5, AFTER, "exponential2"),
                (0, 6, BEFORE, "weights2"),
                (0, 5, AFTER, "scores3"),
                (0, 6, AFTER, "exponential3"),
                (0, 7, BEFORE, "weights3"),
                (0, 8, AFTER, "turn0"),
                (0, 9, BEFORE, "turn_split0"),
                (0, 10, BEFORE, "weigh0"),
                (0, 10, AFTER, "turn1"),
                (0, 11, BEFORE, "turn_split1"),
                (0, 12, BEFORE, "weigh1"),
                (0, 12, AFTER, "turn2"),
                (0, 13, BEFORE, "turn_split2"),
                (0, 14, BEFORE, "weigh2"),
                (0, 14, AFTER, "turn3"),
                (0, 15, BEFORE, "turn_split3"),
                (0, 15, AFTER, "weigh3"),
                (1, 0, BEFORE, "attended"),
                (1, 2, AFTER, "y_copy"),
                (1, 2, AFTER, "table_ln"),
                (1, 3, BEFORE, "silu_y"),
                (1, 4, AFTER, "residual"),
                (1, 6, AFTER, "mean"),
                (1, 7, BEFORE, "squares"),
                (1, 8, AFTER, "variance"),
                (1, 9, BEFORE, "deviation"),
                (1, 9, AFTER, "normalise"),
                (1, 9, AFTER, "table_tanh"),
                (1, 10, BEFORE, "mix_previous"),
                (1, 10, BEFORE, "normalised_split"),
                (1, 12, BEFORE, "decay_gate"),
                (1, 12, AFTER, "decay_tanh"),
                (1, 11, BEFORE, "mix"),
                (1, 11, BEFORE, "keep"),
                (1, 12, AFTER, "decay"),
                (1, 12, AFTER, "input_gate"),
                (1, 13, BEFORE, "input_tanh"),
                (1, 13, AFTER, "input_product"),
                (1, 14, BEFORE, "gated"),
                (1, 12, AFTER, "ffn_k"),
                (1, 13, BEFORE, "ffn_k_squared"),
                (1, 13, AFTER, "ffn_r"),
                (1, 14, BEFORE, "ffn_r_tanh"),
                (1, 14, AFTER, "ffn_v"),
                (1, 15, BEFORE, "ffn"),
                (1, 15, AFTER, "ffn_tanh"),
                (2, 0, BEFORE, "ffn_silu"),
                (2, 4, BEFORE, "input_scale"),
                (2, 4, AFTER, "scan"),
                (2, 5, AFTER, "state_squares"),
                (2, 6, AFTER, "state_mean"),
                (2, 7, AFTER, "state_out"),
                (2, 8, BEFORE, "state_norm"),
                (2, 9, BEFORE, "output"),
                (-1, 0, BEFORE, "load_statistics"),
                (-1, 1, AFTER, "lse_shifts"),
                (-1, 2, AFTER, "lse_factors"),
                (-1, 3, BEFORE, "lse_sums"),
                (-1, 4, AFTER, "lse_logarithm"),
                (-1, 7, AFTER, "lse_parts"),
                (-1, 11, BEFORE, "lse_turned"),
                (-1, 11, AFTER, "lse_stored"),
            ]

            def iteration(op, i, lags=(-1, 0, 1, 2)):
                steps = {lag: {**attention(op, i - lag), **layer1(op, i - lag), **next_lse(op, i - lag)}
                         for lag in lags}

                def place(c, where):
                    for lag, chunk, side_, name in SCHEDULE:
                        if lag in lags and chunk == c and side_ == where:
                            steps[lag][name]()
                for c in range(CH):
                    place(c, BEFORE)
                    if 0 in lags:
                        chunk_logits(op, i, c)
                    if c >= LAG and 0 in lags:
                        chunk_y(op, i, c - LAG)
                    elif c < LAG and 1 in lags:
                        chunk_y(op, i - 1, CH - LAG + c)
                    place(c, AFTER)

            def phase2(op, eng):
                op(DVE, lambda e: e.memset(XP[:, 0:1], 0.0), done=s_zero)
                op(POOL, lambda e: e.nop(), [(s_zero, 0)])
                iteration(op, 0, (-1, 0))
                iteration(op, 1, (-1, 0, 1))
                with eng.Fori(2, NB - 1) as i:
                    iteration(op, i)
                iteration(op, NB - 1, (0, 1, 2))
                iteration(op, NB, (1, 2))
                layer1(op, NB - 1)["table_ln"]()
                iteration(op, NB + 1, (2,))
                op(SP, lambda e: e.nop(), [(S["out_dma"], NB - 1)])
            s_zero = stage("zero_column", DVE)
            phase(phase2, side)


def kernel(**inputs):
    import concourse.bacc as bacc
    from concourse.bass_utils import run_bass_kernel_spmd

    a = {k: np.asarray(v) for k, v in inputs.items()}
    x = a["L0_attn_inputs"]
    tokens, d = x.shape[0] * x.shape[1], x.shape[2]
    x = x.reshape(tokens, d)
    vectors = [a["L0_attn_bq"], a["L1_attn_b_ig"], a["L1_attn_b_rg"], a["L1_attn_lam"],
               a["L1_attn_h0"].reshape(-1), a["L1_attn_norm_w"], a["L1_ffn_mu_r"], a["L1_ffn_mu_k"]]
    weights = [a["L0_attn_Wq"], a["L1_attn_W_in"].T, a["L1_attn_W_ig"].T, a["L1_attn_W_rg"].T,
               a["L1_attn_W_out"].T, a["L1_ffn_W_r"].T, a["L1_ffn_W_k"].T, a["L1_ffn_W_v"].T]
    arrays = {
        "x": x,
        "xT": x.T,
        "phiT": a["L0_ffn_phi_w"].T,
        "phi_b": a["L0_ffn_phi_b"].reshape(1, -1),
        "expert_w": a["L0_ffn_expert_w"].transpose(1, 0, 2),
        "expert_b": a["L0_ffn_expert_b"],
        "weights": np.stack(weights, axis=1),
        "vectors": np.stack(vectors, axis=1),
    }
    nc = bacc.Bacc("TRN2", target_bir_lowering=False, num_devices=1)
    feed, t = {}, {}
    for name, value in arrays.items():
        value = np.ascontiguousarray(value)
        feed[f"in_{name}"] = value
        t[name] = nc.dram_tensor(f"in_{name}", value.shape, mybir.dt.from_np(value.dtype), kind="ExternalInput").ap()
    t["out"] = nc.dram_tensor("out_t", (d, tokens), F32, kind="ExternalOutput").ap()
    build(nc, t)
    r = run_bass_kernel_spmd(nc, [feed], core_ids=[0])
    out = r.results[0]["out_t"]
    return np.ascontiguousarray(out.T).reshape(inputs["L0_attn_inputs"].shape)
```
